# Optimizing a Trainium2 kernel written in Bass

```python
import numpy as np
import jax
import jax.numpy as jnp

def _softmax(x, axis=-1):
    return jax.nn.softmax(x, axis=axis)

def _gelu(x):
    return jax.nn.gelu(x, approximate=True)

def _silu(x):
    return jax.nn.silu(x)

def _sigmoid(x):
    return jax.nn.sigmoid(x)

def _layernorm(x, axis=-1, eps=1e-05):
    m = jnp.mean(x, axis=axis, keepdims=True)
    v = jnp.var(x, axis=axis, keepdims=True)
    return (x - m) / jnp.sqrt(v + eps)

def _scatter_add(tgt, idx, src, axis=0):
    return tgt.at[idx].add(src)

def _segment_sum(src, seg, n):
    return jax.ops.segment_sum(src, seg, n)
kernel_name = 'mk_adaln_d1_jaxref_r8_f686fd'

def setup_inputs(seed: int=0):
    np.random.seed(seed)
    _w = jnp.asarray

    def _L0_attn_setup():
        import jax, jax.numpy as jnp
        import numpy as np
        D_MODEL = 128
        D_STATE = 128
        HEAD_DIM = 64
        EXPAND = 2
        K = 4
        N_GROUPS = 1
        D_INNER = EXPAND * D_MODEL
        N_HEADS = D_INNER // HEAD_DIM
        D_PROJ = 2 * D_INNER + 2 * N_GROUPS * D_STATE + N_HEADS
        EPS = 1e-06

        def _rmsnorm(x, w):
            return x * jax.lax.rsqrt(jnp.mean(x * x, axis=-1, keepdims=True) + EPS) * w
        key = jax.random.key(seed)
        ks = jax.random.split(key, 8)
        B, L = (2, 256)
        x = jax.random.normal(ks[0], (B, L, D_MODEL), jnp.float32)
        norm_w = jnp.ones((D_MODEL,), jnp.float32)
        in_proj_w = jax.random.normal(ks[1], (D_PROJ, D_MODEL), jnp.float32) / np.sqrt(D_MODEL).astype(np.float32)
        conv_w = jax.random.normal(ks[2], (D_INNER, K), jnp.float32) / np.sqrt(K).astype(np.float32)
        conv_b = jnp.zeros((D_INNER,), jnp.float32)
        A_log = jnp.log(jax.random.uniform(ks[3], (N_HEADS,), jnp.float32) * 15.0 + 1.0)
        D = jnp.ones((N_HEADS,), jnp.float32)
        dt_bias = jnp.log(jax.random.uniform(ks[4], (N_HEADS,), jnp.float32) * 0.099 + 0.001)
        out_proj_w = jax.random.normal(ks[5], (D_MODEL, D_INNER), jnp.float32) / np.sqrt(D_INNER).astype(np.float32)
        return dict(x=x, norm_w=norm_w, in_proj_w=in_proj_w, conv_w=conv_w, conv_b=conv_b, A_log=A_log, D=D, dt_bias=dt_bias, out_proj_w=out_proj_w)
    _L0_attn_in = _L0_attn_setup()

    def _L0_ffn_setup():
        import jax, jax.numpy as jnp
        import numpy as np
        B, SEQ, DIM = (2, 512, 128)
        E, S = (8, 64)
        HID = 4 * DIM
        SCALE = DIM ** 0.5

        def rmsnorm(x, gamma):
            n = jnp.linalg.norm(x, axis=-1, keepdims=True)
            return x / jnp.maximum(n, 1e-12) * SCALE * gamma
        key = jax.random.key(seed)
        ks = jax.random.split(key, 4)
        w_init = lambda k, shape: jax.random.normal(k, shape, dtype=jnp.float32) * 0.02
        return {'x': jax.random.normal(ks[0], (B, SEQ, DIM), dtype=jnp.float32), 'norm_gamma': jnp.ones((DIM,), jnp.float32), 'slot_norm_gamma': jnp.ones((DIM,), jnp.float32), 'slot_embeds': jax.random.normal(ks[1], (E, S, DIM), dtype=jnp.float32), 'w1': w_init(ks[2], (E, DIM, HID)), 'b1': jnp.zeros((E, HID), jnp.float32), 'w2': w_init(ks[3], (E, HID, DIM)), 'b2': jnp.zeros((E, DIM), jnp.float32)}
    _L0_ffn_in = _L0_ffn_setup()
    _L0_c = _w((lambda *s: np.random.randn(*s).astype(np.float32) * 0.05)(8, 128))
    _L0_wmod = _w((lambda *s: np.random.randn(*s).astype(np.float32) * 0.05)(128, 6 * 128) * 128 ** (-0.5))
    _d = {'L0_attn_x': _L0_attn_in['x'], 'L0_attn_norm_w': _L0_attn_in['norm_w'], 'L0_attn_in_proj_w': _L0_attn_in['in_proj_w'], 'L0_attn_conv_w': _L0_attn_in['conv_w'], 'L0_attn_conv_b': _L0_attn_in['conv_b'], 'L0_attn_A_log': _L0_attn_in['A_log'], 'L0_attn_D': _L0_attn_in['D'], 'L0_attn_dt_bias': _L0_attn_in['dt_bias'], 'L0_attn_out_proj_w': _L0_attn_in['out_proj_w'], 'L0_ffn_norm_gamma': _L0_ffn_in['norm_gamma'], 'L0_ffn_slot_norm_gamma': _L0_ffn_in['slot_norm_gamma'], 'L0_ffn_slot_embeds': _L0_ffn_in['slot_embeds'], 'L0_ffn_w1': _L0_ffn_in['w1'], 'L0_ffn_b1': _L0_ffn_in['b1'], 'L0_ffn_w2': _L0_ffn_in['w2'], 'L0_ffn_b2': _L0_ffn_in['b2'], 'L0_c': _L0_c, 'L0_wmod': _L0_wmod}
    _x0 = _d['L0_attn_x']
    _d['L0_attn_x'] = jax.random.normal(jax.random.fold_in(jax.random.key(seed), 1), (8, 256, 128), dtype=_x0.dtype)
    del _x0
    return _d

def reference(L0_attn_x, L0_attn_norm_w, L0_attn_in_proj_w, L0_attn_conv_w, L0_attn_conv_b, L0_attn_A_log, L0_attn_D, L0_attn_dt_bias, L0_attn_out_proj_w, L0_ffn_norm_gamma, L0_ffn_slot_norm_gamma, L0_ffn_slot_embeds, L0_ffn_w1, L0_ffn_b1, L0_ffn_w2, L0_ffn_b2, L0_c, L0_wmod):

    def _L0_attn_ref(x, norm_w, in_proj_w, conv_w, conv_b, A_log, D, dt_bias, out_proj_w):
        import jax, jax.numpy as jnp
        import numpy as np
        D_MODEL = 128
        D_STATE = 128
        HEAD_DIM = 64
        EXPAND = 2
        K = 4
        N_GROUPS = 1
        D_INNER = EXPAND * D_MODEL
        N_HEADS = D_INNER // HEAD_DIM
        D_PROJ = 2 * D_INNER + 2 * N_GROUPS * D_STATE + N_HEADS
        EPS = 1e-06

        def _rmsnorm(x, w):
            return x * jax.lax.rsqrt(jnp.mean(x * x, axis=-1, keepdims=True) + EPS) * w
        batch, L, _ = x.shape
        residual = x
        xn = _rmsnorm(x, norm_w)
        proj = jnp.einsum('bld,pd->blp', xn, in_proj_w)
        i = 0
        z = proj[:, :, i:i + D_INNER]
        i += D_INNER
        x_ssm = proj[:, :, i:i + D_INNER]
        i += D_INNER
        bc = N_GROUPS * D_STATE
        Bm = proj[:, :, i:i + bc].reshape(batch, L, N_GROUPS, D_STATE)
        i += bc
        Cm = proj[:, :, i:i + bc].reshape(batch, L, N_GROUPS, D_STATE)
        i += bc
        dt_raw = proj[:, :, i:i + N_HEADS]
        xp = jnp.pad(x_ssm, ((0, 0), (K - 1, 0), (0, 0)))
        x_conv = conv_b
        for k in range(K):
            x_conv = x_conv + xp[:, k:k + L, :] * conv_w[:, k]
        x_conv = jax.nn.silu(x_conv)
        xh = x_conv.reshape(batch, L, N_HEADS, HEAD_DIM)
        dt = jax.nn.softplus(dt_raw + dt_bias)
        dA = jnp.exp(-jnp.exp(A_log) * dt)
        dtx = dt[..., None] * xh
        gidx = jnp.arange(N_HEADS) // (N_HEADS // N_GROUPS)
        Bg = Bm[:, :, gidx, :]
        Cg = Cm[:, :, gidx, :]

        def step(h, inp):
            dA_t, dtx_t, B_t, C_t = inp
            h = h * dA_t[:, :, None, None] + dtx_t[..., None] * B_t[:, :, None, :]
            y_t = jnp.einsum('bhpn,bhn->bhp', h, C_t)
            return (h, y_t)
        h0 = jnp.zeros((batch, N_HEADS, HEAD_DIM, D_STATE), jnp.float32)
        xs = (jnp.swapaxes(dA, 0, 1), jnp.swapaxes(dtx, 0, 1), jnp.swapaxes(Bg, 0, 1), jnp.swapaxes(Cg, 0, 1))
        _, ys = jax.lax.scan(step, h0, xs)
        y = jnp.swapaxes(ys, 0, 1) + D[None, None, :, None] * xh
        y = y.reshape(batch, L, D_INNER) * jax.nn.silu(z)
        return residual + jnp.einsum('bli,di->bld', y, out_proj_w)

    def _L0_ffn_ref(x, norm_gamma, slot_norm_gamma, slot_embeds, w1, b1, w2, b2):
        import jax, jax.numpy as jnp
        import numpy as np
        B, SEQ, DIM = (2, 512, 128)
        E, S = (8, 64)
        HID = 4 * DIM
        SCALE = DIM ** 0.5

        def rmsnorm(x, gamma):
            n = jnp.linalg.norm(x, axis=-1, keepdims=True)
            return x / jnp.maximum(n, 1e-12) * SCALE * gamma
        xn = rmsnorm(x, norm_gamma)
        sn = rmsnorm(slot_embeds, slot_norm_gamma)
        logits = jnp.einsum('bnd,esd->bnes', xn, sn)
        dispatch = jax.nn.softmax(logits, axis=1)
        b, n, e, s = logits.shape
        combine = jax.nn.softmax(logits.reshape(b, n, e * s), axis=-1)
        slots = jnp.einsum('bnd,bnes->besd', xn, dispatch)
        h = jnp.einsum('besd,edh->besh', slots, w1) + b1[None, :, None, :]
        h = jax.nn.gelu(h, approximate=False)
        eo = jnp.einsum('besh,ehd->besd', h, w2) + b2[None, :, None, :]
        eo = eo.reshape(b, e * s, DIM)
        out = jnp.einsum('bmd,bnm->bnd', eo, combine)
        return out
    x = L0_attn_x
    mod = (_silu(L0_c) @ L0_wmod).reshape(L0_c.shape[0], 6, 1, -1)
    sa, ca, ga, sb, cb, gb = (mod[:, 0], mod[:, 1], mod[:, 2], mod[:, 3], mod[:, 4], mod[:, 5])
    ga = (2 * (ga >= 0) - 1) * jnp.maximum(jnp.abs(ga), 0.25)
    gb = (2 * (gb >= 0) - 1) * jnp.maximum(jnp.abs(gb), 0.25)
    h = _layernorm(x, axis=-1) * (1 + ca) + sa
    x = x + ga * _L0_attn_ref(h, L0_attn_norm_w, L0_attn_in_proj_w, L0_attn_conv_w, L0_attn_conv_b, L0_attn_A_log, L0_attn_D, L0_attn_dt_bias, L0_attn_out_proj_w)
    h = _layernorm(x, axis=-1) * (1 + cb) + sb
    x = x + gb * _L0_ffn_ref(h, L0_ffn_norm_gamma, L0_ffn_slot_norm_gamma, L0_ffn_slot_embeds, L0_ffn_w1, L0_ffn_b1, L0_ffn_w2, L0_ffn_b2)
    return x

_drawn_inputs = setup_inputs


def setup_inputs(seed=0):
    import zlib

    import numpy as np

    out = dict(_drawn_inputs(seed))
    spreads = {'L0_attn_norm_w': (1.0, 0.2),
     'L0_attn_conv_b': (0.0, 0.282),
     'L0_attn_D': (1.0, 0.6),
     'L0_ffn_norm_gamma': (1.0, 0.6),
     'L0_ffn_slot_norm_gamma': (1.0, 0.6),
     'L0_ffn_b1': (0.0, 0.8),
     'L0_ffn_b2': (0.0, 0.381)}
    factors = {'L0_ffn_w1': 4.969, 'L0_ffn_w2': 4.505}
    for name, (base, spread) in spreads.items():
        noise = np.random.default_rng([zlib.crc32(name.encode()), seed]).standard_normal(out[name].shape)
        drawn = base * np.exp(spread * noise) if base else spread * noise
        out[name] = jnp.asarray(drawn.astype(out[name].dtype))
    for name, factor in factors.items():
        out[name] = (out[name] * factor).astype(out[name].dtype)
    return out
```

```python
import concourse.bass as bass
from concourse import mybir
from contextlib import ExitStack


def bass_adaln_mamba_softmoe_kernel(
    nc: bass.Bass,
    x: bass.AP,
    norm_w: bass.AP,
    in_proj_w: bass.AP,
    conv_w: bass.AP,
    conv_b: bass.AP,
    A_log: bass.AP,
    D: bass.AP,
    dt_bias: bass.AP,
    out_proj_w: bass.AP,
    norm_gamma: bass.AP,
    slot_norm_gamma: bass.AP,
    slot_embeds: bass.AP,
    w1: bass.AP,
    b1: bass.AP,
    w2: bass.AP,
    b2: bass.AP,
    c: bass.AP,
    wmod: bass.AP,
    out: bass.AP,
):
    fp32, bf16, fp16 = mybir.dt.float32, mybir.dt.bfloat16, mybir.dt.float16
    ALU = mybir.AluOpType
    ACT = mybir.ActivationFunctionType
    AX = mybir.AxisListType

    B, L, DM = x.shape
    H = A_log.shape[0]
    DI = out_proj_w.shape[1]
    HD = DI // H
    TAPS = conv_w.shape[1]
    E, S, _ = slot_embeds.shape
    HID = w1.shape[2]
    P = 128
    CT = DI // P
    NT = L // P
    SL = E * S
    MT = SL // P
    HC = HID // P
    BP = 2
    TP = BP * NT
    W = BP * L
    LN_EPS, RMS_EPS, NORM_FLOOR = 1e-5, 1e-6, 1e-12
    ROWS = in_proj_w.shape[0]
    ROW_BLOCKS = ROWS // P
    Z0, X0, B0, C0 = 0, DI, 2 * DI, 2 * DI + P
    DT0 = 2 * DI + 2 * P
    SHIFT = 64.0
    ATANH_TERMS = [1.0 / k for k in range(15, 1, -2)]
    PART_ROW = 32

    ctx = ExitStack()
    with ctx:
        def sb(name, shape, dt=fp32):
            return ctx.enter_context(nc.sbuf_tensor(name, shape, dt))

        per_pass = {}
        base_value = {}

        def sem(name, count=1, base=0):
            per_pass[name] = count
            base_value[name] = base
            return name, [ctx.enter_context(nc.semaphore(f"{name}_{j}")) for j in range(2)]

        def wait(eng, s, j, it, k=None):
            name, sems = s
            n = per_pass[name]
            eng.wait_ge(sems[j], it * n + ((n if k is None else k) + base_value[name]))

        def hold(eng):
            eng.sem_inc(s_held, 1)

        def wait_before(eng, s, j, it):
            name, sems = s
            eng.wait_ge(sems[j], it * per_pass[name] + base_value[name])

        def start_from_base(eng, *names):
            for name, sems in names:
                for j in range(2):
                    eng.sem_inc(sems[j], base_value[name])

        s_held = ctx.enter_context(nc.semaphore("s_held"))

        ident = sb("ident", [P, P])
        ident_b = sb("ident_b", [P, P], bf16)
        ident_shift = sb("ident_shift", [P, P], fp16)
        neg_shift = sb("neg_shift", [P, P], fp16)
        ones_sq = sb("ones_sq", [P, P])
        neg_half = sb("neg_half", [P, TP])
        causal = sb("causal", [P, P])
        future = sb("future", [P, P], bf16)
        eo = sb("eo", [P, B, MT, P + 1])
        as_loaded = eo[:, :, :, :].rearrange("p b m d -> p (b m d)")
        w_nat = as_loaded[:, 0:ROW_BLOCKS * P].rearrange("p (n d) -> p n d", n=ROW_BLOCKS)
        wmod_sb = as_loaded[:, ROW_BLOCKS * P:(ROW_BLOCKS + 6) * P]
        se_nat = as_loaded[:, (ROW_BLOCKS + 6) * P:(ROW_BLOCKS + 6 + MT) * P].rearrange("p (n d) -> p n d", n=MT)
        wo_nat = as_loaded[:, (ROW_BLOCKS + 6 + MT) * P:(ROW_BLOCKS + 6 + MT + CT) * P]
        se_sq = as_loaded[:, (ROW_BLOCKS + 6 + MT + CT) * P:(ROW_BLOCKS + 7 + MT + CT) * P]
        dt_nat = sb("dt_nat", [H, P])
        winT = sb("winT", [P, ROWS])
        woT = sb("woT", [P, CT, P])
        se_ss = sb("se_ss", [P, MT])
        se_r = sb("se_r", [P, MT])
        snT = sb("snT", [P, SL])
        convw = sb("convw", [P, CT, TAPS])
        d_col = sb("d_col", [P, CT])
        d_half = sb("d_half", [P, CT])
        blk = sb("blk", [P, 2, H])
        dtb_row = sb("dtb_row", [P, H])
        expA_row = sb("expA_row", [P, H])
        expA_t = sb("expA_t", [P, H])
        RB1, RB2 = 0, E * HC
        RC = RB2 + E
        RCB = RC + B
        RNW = RCB + CT
        RG, RSG = RNW + 1, RNW + 2
        VR = RSG + 1
        vec_nat = sb("vec_nat", [VR, P])
        vecT = sb("vecT", [P, VR])
        cs = sb("cs", [P, B])
        cs_t = sb("cs_t", [P, B])
        g_all = sb("g_all", [P, 1])
        gbT = sb("gbT", [P, B])
        mod_rows = sb("mod_rows", [B, 6, P])
        sgn_T = sb("sgn_T", [P, B])
        sgn_r = sb("sgn_r", [B, P])
        slotsT = sb("slotsT", [P, E, B, S])
        x1tok = sb("x1tok", [P, B * NT, P])
        combT = sb("combT", [P, B, MT, L])

        def two(name, shape, dt=fp32):
            return [sb(f"{name}{j}", shape, dt) for j in range(2)]

        xin = two("xin", [P, TP, P])
        bst = two("bst", [P, TP, 6])
        mv = two("mv", [P, TP, 2])
        root = two("root", [P, TP])
        ms = two("ms", [P, TP])
        hh = two("hh", [P, TP, P])
        basis = two("basis", [P, TP, P])
        mods_bc = two("mods_bc", [P, BP, 5, P])
        xnT = two("xnT", [P, W])
        zsT = two("zsT", [P, CT, W])
        xcT = two("xcT", [P, CT, W])
        xhT = two("xhT", [P, CT, W])
        BT = two("BT", [P, W])
        CTr = two("CTr", [P, W])
        dv = two("dv", [P, 8, TP * H])
        Q = two("Q", [P, TP, P], bf16)
        ksm = two("ksm", [P, W], bf16)
        rsm = two("rsm", [P, H, W], bf16)
        gm = two("gm", [P, BP, 3, P])
        seg_e = two("seg_e", [P, 3, 512])
        seg_m = two("seg_m", [P, 3, 512])
        xn2tok = two("xn2tok", [P, TP, P + 1])
        rmax = two("rmax", [P, NT])
        cmax = two("cmax", [P, MT])
        diag_r = two("diag_r", [P, NT, P], fp16)
        diag_c = two("diag_c", [P, MT, P], fp16)
        rcs = two("rcs", [P, MT])

        lt_sb = [t[:, 0:NT, :] for t in seg_e]
        e_disp = [t[:, 0:NT, :] for t in seg_m]
        dtx = [t[:, :, :].rearrange("p k t -> p (k t)").rearrange("p (t c) -> p t c", t=TP) for t in xcT]
        slots = [t[:, :].rearrange("p (m d) -> p m d", m=MT) for t in BT]

        bank = [ctx.enter_context(nc.psum_tensor(f"bank{i}", [P, 512], fp32)) for i in range(8)]

        s_in = ctx.enter_context(nc.semaphore("s_in"))
        s_in2 = ctx.enter_context(nc.semaphore("s_in2"))
        s_pool = ctx.enter_context(nc.semaphore("s_pool"))
        s_pe0 = ctx.enter_context(nc.semaphore("s_pe0"))
        s_dve0 = ctx.enter_context(nc.semaphore("s_dve0"))
        s_act0 = ctx.enter_context(nc.semaphore("s_act0"))
        s_ready = ctx.enter_context(nc.semaphore("s_ready"))

        s_mod = ctx.enter_context(nc.semaphore("s_mod"))
        s_eo_ones = ctx.enter_context(nc.semaphore("s_eo_ones"))

        x_in = sem("x_in", 16)
        mods_in = sem("mods_in", 16 * BP)
        var_done = sem("var_done", 2)
        root_done = sem("root_done", 4)
        h_done = sem("h_done", 2)
        ms_done = sem("ms_done", 2)
        basis_done = sem("basis_done")
        xn_done = sem("xn_done", 2)
        xnT_ps = sem("xnT_ps", 2)
        xnT_done = sem("xnT_done", 2)
        pool_own = sem("pool_own", 5)
        dt_ps = sem("dt_ps")
        x_ps = sem("x_ps", 2)
        bc_ps = sem("bc_ps", 2)
        bc_done = sem("bc_done", 2)
        z_ps = sem("z_ps", 2)
        v_done = sem("v_done")
        nabs_done = sem("nabs_done")
        edt_done = sem("edt_done")
        tap0_done = sem("tap0_done", 2)
        conv_done = sem("conv_done", 2)
        xt_done = sem("xt_done", 2)
        zt_done = sem("zt_done", 2)
        zs_done = sem("zs_done", 2)
        xh_done = sem("xh_done", 2)
        w_done = sem("w_done")
        cum_ps = sem("cum_ps")
        parts_done = sem("parts_done")
        parts_ps = sem("parts_ps")
        ksm_done = sem("ksm_done")
        rsm_in = sem("rsm_in", 48)
        g_ps = sem("g_ps", 2)
        g_done = sem("g_done", 2)
        xht_ps = sem("xht_ps", 2)
        dtx_done = sem("dtx_done", 2)
        seg_ps = sem("seg_ps", 6)
        seg_done = sem("seg_done", 6)
        m_done = sem("m_done", 6)
        y_ps = sem("y_ps", 2, base=1)
        yg_done = sem("yg_done")
        o_ps = sem("o_ps")
        x1_done = sem("x1_done")
        lt_ps = sem("lt_ps", 4)
        lt_done = sem("lt_done", 4)
        diag_r_done = sem("diag_r_done", 2)
        ls_ps = sem("ls_ps", 4)
        diag_c_done = sem("diag_c_done", 2)
        disp_ps = sem("disp_ps", 4)
        comb_ps = sem("comb_ps", 4)
        disp_done = sem("disp_done", 4)
        comb_done = sem("comb_done", 4)
        slots_ps = sem("slots_ps", 4)
        slots_done = sem("slots_done", 2, base=1)
        slotsT_ps = sem("slotsT_ps", 2)
        slotsT_done = sem("slotsT_done", 2, base=1)
        DVE_STEPS = 36
        dve_own = sem("dve_own", DVE_STEPS)

        w1_sb = two("w1_sb", [P, HID])
        w2_sb = two("w2_sb", [P, HC, P])
        act_h = [zsT[0], zsT[1]], [xcT[0], xcT[1]]
        eoT = seg_e[0][:, 0:2, :].rearrange("p a (b e s) -> p (a b) e s", e=2, s=S)
        w1_in = sem("w1_in", 16)
        w2_in = sem("w2_in", 16)
        hid_ps = sem("hid_ps", HC)
        gelu_done = sem("gelu_done", HC, base=1)
        eoT_ps = sem("eoT_ps", base=1)
        eoT_done = sem("eoT_done", base=1)
        eo_ps = ctx.enter_context(nc.semaphore("eo_ps"))
        eo_done = ctx.enter_context(nc.semaphore("eo_done"))
        cb_done = sem("cb_done")
        comb_out_ps = sem("comb_out_ps", NT, base=1)
        y_out = sem("y_out", base=1)
        y_sent = sem("y_sent", 16, base=1)
        rden_done = sem("rden_done")
        rden = two("rden", [P, NT])
        cbuf = xhT
        yout = xin

        mod_dram = nc.dram_tensor("mod_dram", (B, 6 * P), fp32, kind="Internal").ap()
        PASSES = B // (2 * BP)
        SKEW = 6
        VV, NABS, EDT, U, U2, PP, DTH, WD = range(8)
        N_IN, N_IN2 = 16 * 11, 16 * (4 + H)
        POOL_ALL = 17 + 2
        SETUP_VEC = 1
        SETUP_SE = SETUP_VEC + MT
        SETUP_CS = SETUP_SE + 2

        def run(visits, it):
            for pos, j, f in sorted(((p + SKEW * j, j, n) for j in range(2) for n, (p, _) in enumerate(visits)),
                                    key=lambda v: (v[0], v[1], v[2])):
                visits[f][1](j, it)

        def tile_cols(t, n=P):
            return slice(t * n, t * n + n)

        block = ctx.enter_context(nc.Block())

        @block.sync
        def _(sp):
            x_v = x.rearrange("b (n p) d -> p (b n) d", p=P)
            start_from_base(sp, y_sent)
            out_v = out.rearrange("b (n p) d -> p (b n) d", p=P)

            def load_x(j, it):
                sp.dma_start(xin[j][:, :, :], x_v[:, bass.ds(it * 2 * TP + j * TP, TP), :]).then_inc(x_in[1][j], 16)

            for j in range(2):
                load_x(j, 0)
            vecs = [
                (RB1, E * HC, b1.rearrange("e (c p) -> (e c) p", p=P)),
                (RB2, E, b2),
                (RC, B, c),
                (RCB, CT, conv_b.rearrange("(c p) -> c p", p=P)),
                (RNW, 1, norm_w.rearrange("(o p) -> o p", o=1)),
                (RG, 1, norm_gamma.rearrange("(o p) -> o p", o=1)),
                (RSG, 1, slot_norm_gamma.rearrange("(o p) -> o p", o=1)),
            ]
            for r0, n, src in vecs:
                sp.dma_start(vec_nat[r0:r0 + n, :], src).then_inc(s_in, 16)
            sp.dma_start(w_nat[:, :, :],
                         in_proj_w[0:ROW_BLOCKS * P, :].rearrange("(n p) d -> p n d", p=P)).then_inc(s_in, 16)
            sp.dma_start(dt_nat[:, :], in_proj_w[DT0:ROWS, :]).then_inc(s_in, 16)
            sp.dma_start(wo_nat[:, :], out_proj_w).then_inc(s_in, 16)
            sp.dma_start(se_nat[:, :, :],
                         slot_embeds.rearrange("(n a) s d -> (a s) n d", a=P // S)).then_inc(s_in, 16)

            def send_parts(j, it):
                wait(sp, ksm_done, j, it)
                hold(sp)
                wait_before(sp, y_ps, j, it)
                hold(sp)
                for r in range(3):
                    sp.dma_start(
                        rsm[j][r:r + 1, :, :],
                        ksm[j][PART_ROW + H * r:PART_ROW + H * (r + 1), :],
                    ).then_inc(rsm_in[1][j], 16)

            def load_mods(j, it):
                for bi in range(BP):
                    sp.dma_start(mods_bc[j][:, bi, :, :].rearrange("p m d -> p (m d)"),
                                 mod_dram[bass.ds(it * 2 * BP + (j * BP + bi), 1), 0:5 * P].broadcast_to((P, 5 * P))
                                 ).then_inc(mods_in[1][j], 16)

            sp.wait_ge(s_ready, 1)
            sp.dma_start(mod_dram, mod_rows[:, :, :].rearrange("b m d -> b (m d)")).then_inc(s_mod, 16)
            sp.wait_ge(s_mod, 16)
            for j in range(2):
                load_mods(j, 0)

            def next_x(j, it):
                wait(sp, basis_done, j, it)
                hold(sp)
                load_x(j, it + 1)

            def next_mods(j, it):
                wait(sp, h_done, j, it, 2)
                hold(sp)
                load_mods(j, it + 1)

            SP_VISITS = [(12.56, send_parts)]
            with sp.Fori(0, PASSES - 1) as it:
                run([(5, next_x)] + SP_VISITS + [(33, next_mods)], it)
            run(SP_VISITS, PASSES - 1)

            def load_w(j, it):
                sp.dma_start(w1_sb[j][:, :], w1[bass.ds(it * 2 + j, 1), :, :].rearrange("o d h -> d (o h)")
                             ).then_inc(w1_in[1][j], 16)
                sp.dma_start(w2_sb[j][:, :, :],
                             w2[bass.ds(it * 2 + j, 1), :, :].rearrange("o (c p) d -> p (o c) d", p=P)
                             ).then_inc(w2_in[1][j], 16)

            for j in range(2):
                load_w(j, 0)
            with sp.Fori(0, E // 2 - 1) as it:
                for j in range(2):
                    wait(sp, hid_ps, j, it)
                    hold(sp)
                    wait(sp, eoT_ps, j, it)
                    hold(sp)
                    load_w(j, it + 1)
            with sp.Fori(0, B // 2) as it:
                for j in range(2):
                    wait(sp, y_out, j, it)
                    hold(sp)
                    sp.dma_start(out_v[:, bass.ds((it * 2 + j) * NT, NT), :],
                                 yout[j][:, 0:NT, :]).then_inc(y_sent[1][j], 16)
            for j in range(2):
                wait(sp, y_sent, j, B // 2 - 1)
                hold(sp)

        @block.gpsimd
        def _(pool):
            pool.dma_start(wmod_sb[:, :], wmod).then_inc(s_in2, 16)
            pool.dma_start(convw[:, :, :], conv_w.rearrange("(c p) k -> p c k", p=P)).then_inc(s_in2, 16)
            pool.dma_start(dtb_row[:, :],
                           dt_bias.rearrange("(o h) -> o h", o=1).broadcast_to((P, H))).then_inc(s_in2, 16)
            pool.dma_start(expA_row[:, :],
                           A_log.rearrange("(o h) -> o h", o=1).broadcast_to((P, H))).then_inc(s_in2, 16)
            for h in range(H):
                pool.dma_start(d_col[(h % 2) * HD:(h % 2 + 1) * HD, h // 2:h // 2 + 1],
                               D[h:h + 1].rearrange("(o h) -> o h", o=1).broadcast_to((HD, 1))).then_inc(s_in2, 16)
            nc.gpsimd.memset(ones_sq[:, :], 1.0).then_inc(s_pool, 1)
            pool.wait_ge(s_pool, 1)
            nc.gpsimd.affine_select(out=ident[:, :], in_=ones_sq[:, :], compare_op=ALU.is_equal, fill=0.0, base=0,
                                    pattern=[[1, P]], channel_multiplier=-1).then_inc(s_pool, 1)
            nc.gpsimd.affine_select(out=causal[:, :], in_=ones_sq[:, :], compare_op=ALU.is_ge, fill=0.0, base=0,
                                    pattern=[[1, P]], channel_multiplier=-1).then_inc(s_pool, 1)
            nc.gpsimd.memset(neg_half[:, :], -0.5).then_inc(s_pool, 1)
            nc.gpsimd.memset(neg_shift[:, :], -SHIFT).then_inc(s_pool, 1)
            nc.gpsimd.memset(future[:, :], 0.0).then_inc(s_pool, 1)
            for j in range(2):
                nc.gpsimd.memset(Q[j][:, :, 0:3], -1.0).then_inc(s_pool, 1)
                nc.gpsimd.memset(Q[j][:, :, 3:P], 0.0).then_inc(s_pool, 1)
                nc.gpsimd.memset(xn2tok[j][:, :, P:P + 1], 1.0).then_inc(s_pool, 1)
            pool.wait_ge(s_pool, 12)
            nc.gpsimd.tensor_copy(ident_b[:, :], ident[:, :]).then_inc(s_pool, 1)
            nc.gpsimd.tensor_single_scalar(ident_shift[:, :], ident[:, :], 1.0 / SHIFT, ALU.mult).then_inc(s_pool, 1)
            nc.gpsimd.affine_select(out=future[:, :], in_=future[:, :], compare_op=ALU.is_ge, fill=-1e30, base=0,
                                    pattern=[[1, P]], channel_multiplier=-1).then_inc(s_pool, 1)
            nc.gpsimd.tensor_tensor(blk[:, 0, :], ident[:, PART_ROW:PART_ROW + H],
                                    ident[:, PART_ROW + H:PART_ROW + 2 * H], ALU.add).then_inc(s_pool, 1)
            pool.wait_ge(s_pool, 16)
            nc.gpsimd.tensor_tensor(blk[:, 1, :], blk[:, 0, :],
                                    ident[:, PART_ROW + 2 * H:PART_ROW + 3 * H], ALU.add).then_inc(s_pool, 1)
            pool.wait_ge(s_pool, 17)
            for j in range(2):
                nc.gpsimd.tensor_copy(rsm[j][:, :, :],
                                      blk[:, 1, :].unsqueeze(2).broadcast_to((P, H, W))).then_inc(s_pool, 1)
            pool.wait_ge(s_act0, MT)
            nc.gpsimd.tensor_scalar(se_r[:, :], se_ss[:, :], NORM_FLOOR ** 2 / DM, None, ALU.max).then_inc(s_pool, 1)
            pool.wait_ge(s_pool, POOL_ALL + 1)
            nc.gpsimd.tensor_tensor(se_r[:, :], se_r[:, :], neg_half[:, 0:MT], ALU.pow).then_inc(s_pool, 1)
            pool.wait_ge(s_ready, 2)
            nc.gpsimd.memset(eo[:, :, :, P:P + 1], 1.0).then_inc(s_eo_ones, 1)

            def inverse_root(kind, n, src):
                def visit(j, it):
                    if kind == 0:
                        wait(pool, var_done, j, it, n // 2 + 1)
                    else:
                        wait(pool, ms_done, j, it, n // 2 + 1)
                    hold(pool)
                    nc.gpsimd.tensor_scalar(root[j][:, :], src(j), (LN_EPS, RMS_EPS, NORM_FLOOR ** 2 / DM)[kind], None,
                                            ALU.max if kind == 2 else ALU.add).then_inc(pool_own[1][j], 1)
                    wait(pool, pool_own, j, it, n + 1 + (n >= 2))
                    nc.gpsimd.tensor_tensor(root[j][:, :], root[j][:, :], neg_half[:, :], ALU.pow
                                            ).then_inc(root_done[1][j], 1)
                return visit

            def add_basis(j, it):
                wait(pool, h_done, j, it, 1)
                for bi in range(BP):
                    t = slice(bi * NT, (bi + 1) * NT)
                    q = nc.gpsimd.tensor_tensor(basis[j][:, t, :], hh[j][:, t, :],
                                                mods_bc[j][:, bi, 2, :].unsqueeze(1).broadcast_to((P, NT, P)), ALU.mult)
                q.then_inc(pool_own[1][j], 1)
                wait(pool, pool_own, j, it, 3)
                nc.gpsimd.tensor_tensor(basis[j][:, :, :], basis[j][:, :, :], xin[j][:, :, :], ALU.add
                                        ).then_inc(basis_done[1][j], 1)

            variances = lambda j: mv[j][:, :, 1]
            mean_squares = lambda j: ms[j][:, :]
            with pool.Fori(0, PASSES) as it:
                run([(0.5, inverse_root(0, 0, variances)), (2.5, inverse_root(1, 1, mean_squares)),
                     (3.5, add_basis), (28.5, inverse_root(0, 2, variances)),
                     (32.5, inverse_root(2, 3, mean_squares))], it)

        @block.tensor
        def _(pe):
            def mm(o, lhsT, rhs, start=True, stop=True):
                return nc.tensor.matmul(o, lhsT, rhs, start=start, stop=stop)

            start_from_base(pe, y_ps, eoT_ps, comb_out_ps)
            pe.sem_inc(eo_ps, 1)
            pe.wait_ge(s_pool, POOL_ALL)
            pe.wait_ge(s_in, N_IN)
            nc.tensor.transpose(bank[0][:, 0:VR], vec_nat[:, :], ident[0:VR, 0:VR]).then_inc(s_pe0, 1)
            for n in range(ROW_BLOCKS):
                q = nc.tensor.transpose(bank[1 + n // 4][:, tile_cols(n % 4)], w_nat[:, n, :], ident[:, :])
            q = nc.tensor.transpose(bank[3][:, 0:H], dt_nat[:, :], ident[0:H, 0:H])
            for k in range(CT):
                q = nc.tensor.transpose(bank[3][:, tile_cols(1 + k)], wo_nat[:, tile_cols(k)], ident[:, :])
            q.then_inc(s_pe0, 1)
            pe.wait_ge(s_dve0, SETUP_SE)
            for m in range(MT):
                q = nc.tensor.transpose(bank[4][:, tile_cols(m)], se_nat[:, m, :], ident[:, :])
            q.then_inc(s_pe0, 1)
            pe.wait_ge(s_in2, N_IN2)
            pe.wait_ge(s_dve0, SETUP_CS)
            mm(bank[5][0:B, 0:3 * P], cs[:, :], wmod_sb[:, 0:3 * P])
            mm(bank[6][0:B, 0:3 * P], cs[:, :], wmod_sb[:, 3 * P:6 * P])
            mm(bank[7][:, 0:B], wmod_sb[:, tile_cols(5)], cs[:, :]).then_inc(s_pe0, 1)
            pe.wait_ge(s_ready, 2)

            def t_xn(layer):
                def visit(j, it):
                    wait(pe, xn_done, j, it, layer + 1)
                    if layer == 0:
                        wait_before(pe, slots_done, j, it)
                        wait_before(pe, slotsT_done, j, it)
                    for t in range(TP):
                        q = nc.tensor.transpose(bank[4 * j][:, tile_cols(t)], xn2tok[j][:, t, 0:P], ident[:, :])
                    q.then_inc(xnT_ps[1][j], 1)
                return visit

            def project1(j, it):
                b0, b1, b2, b3 = bank[4 * j:4 * j + 4]
                wait(pe, xnT_done, j, it, 1)
                for t in range(TP):
                    q = mm(b3[:, t * H:(t + 1) * H], xnT[j][:, tile_cols(t)], winT[:, DT0:ROWS])
                q.then_inc(dt_ps[1][j], 1)
                mm(b0[:, :], winT[:, X0:X0 + P], xnT[j][:, :]).then_inc(x_ps[1][j], 1)
                mm(b1[:, :], winT[:, X0 + P:X0 + 2 * P], xnT[j][:, :]).then_inc(x_ps[1][j], 1)
                mm(b2[:, :], winT[:, B0:B0 + P], xnT[j][:, :]).then_inc(bc_ps[1][j], 1)

            def project2(j, it):
                wait(pe, v_done, j, it)
                mm(bank[4 * j + 3][:, :], winT[:, C0:C0 + P], xnT[j][:, :]).then_inc(bc_ps[1][j], 1)
                wait(pe, bc_done, j, it, 1)
                mm(bank[4 * j + 2][:, :], winT[:, Z0:Z0 + P], xnT[j][:, :]).then_inc(z_ps[1][j], 1)

            def project3(j, it):
                wait(pe, bc_done, j, it, 2)
                mm(bank[4 * j + 3][:, :], winT[:, Z0 + P:Z0 + 2 * P], xnT[j][:, :]).then_inc(z_ps[1][j], 1)

            def scores(j, it):
                for bi in range(BP):
                    wait(pe, conv_done, j, it, bi + 1)
                    o = bank[4 * j + bi]
                    t0 = bi * L
                    mm(o[:, 0:L], BT[j][:, t0:t0 + P], CTr[j][:, t0:t0 + L])
                    mm(o[:, L:L + P], BT[j][:, t0 + P:t0 + L], CTr[j][:, t0 + P:t0 + L]).then_inc(g_ps[1][j], 1)

            def running_sums(j, it):
                wait(pe, w_done, j, it)
                wait(pe, zs_done, j, it, 1)
                o = bank[4 * j + 2]
                mm(o[:, 0:TP * H], causal[:, :], dv[j][:, WD, :], stop=False)
                w4 = dv[j][:, WD, :].rearrange("p (b n h) -> p b n h", b=BP, n=NT)
                o4 = o[:, 0:TP * H].rearrange("p (b n h) -> p b n h", b=BP, n=NT)
                mm(o4[:, :, 1, :], ones_sq[:, :], w4[:, :, 0, :], start=False).then_inc(cum_ps[1][j], 1)

            def part_rows(j, it):
                wait(pe, parts_done, j, it)
                o = bank[4 * j + 2][:, :].bitcast(bf16)
                for t in range(TP):
                    q = nc.tensor.transpose(o[:, tile_cols(t)], Q[j][:, t, :], ident_b[:, :])
                q.then_inc(parts_ps[1][j], 1)

            def t_xh(j, it):
                for bi in range(BP):
                    wait(pe, g_done, j, it, bi + 1)
                    wait(pe, xh_done, j, it, 2)
                    for n in range(NT):
                        for k in range(CT):
                            t = bi * NT + n
                            q = nc.tensor.transpose(bank[4 * j + bi][:, tile_cols(n * CT + k)],
                                                    xhT[j][:, k, tile_cols(t)], ident[:, :])
                    q.then_inc(xht_ps[1][j], 1)

            def segment(f):
                def visit(j, it):
                    bi, g = divmod(f, 3)
                    o = bank[4 * j + 2 + f % 2]
                    if f == 0:
                        wait(pe, ksm_done, j, it)
                        wait(pe, rsm_in, j, it)
                    if f == 1:
                        wait(pe, zs_done, j, it, 2)
                    if f >= 2:
                        wait(pe, seg_done, j, it, f - 1)
                    if g < 2:
                        mm(o[:, :], ksm[j][:, bi * L:bi * L + P],
                           rsm[j][:, 2 * g:2 * g + 2, bi * L:(bi + 1) * L], stop=False)
                        mm(o[:, :].rearrange("p (h t) -> p h t", h=2)[:, :, 0:P], ident_b[:, :],
                           future[:, :].unsqueeze(1).broadcast_to((P, 2, P)), start=False).then_inc(seg_ps[1][j], 1)
                    else:
                        mm(o[:, :], ksm[j][:, bi * L + P:bi * L + L],
                           rsm[j][:, :, bi * L + P:(bi + 1) * L], stop=False)
                        mm(o[:, :].rearrange("p (h t) -> p h t", h=H), ident_b[:, :],
                           future[:, :].unsqueeze(1).broadcast_to((P, H, P)), start=False).then_inc(seg_ps[1][j], 1)
                return visit

            def y_of(bi):
                def visit(j, it):
                    wait(pe, dtx_done, j, it, 2)
                    wait(pe, m_done, j, it, 3 * bi + 3)
                    for h in range(H):
                        o = bank[4 * j + h // 2][(h % 2) * HD:(h % 2 + 1) * HD, bi * L:(bi + 1) * L]
                        mm(o, dtx[j][:, bi * NT, h * HD:(h + 1) * HD],
                           seg_m[j][:, h // 2, (h % 2) * L:(h % 2 + 1) * L], stop=False)
                        q = mm(o[:, P:L], dtx[j][:, bi * NT + 1, h * HD:(h + 1) * HD],
                               seg_m[j][:, 2, tile_cols(h)], start=False)
                    q.then_inc(y_ps[1][j], 1)
                return visit

            def project_out(j, it):
                wait(pe, yg_done, j, it)
                wait(pe, seg_done, j, it, 6)
                for t in range(TP):
                    for k in range(CT):
                        q = mm(bank[4 * j + 2][:, tile_cols(t)], xhT[j][:, k, tile_cols(t)], woT[:, k, :],
                               start=k == 0, stop=k == CT - 1)
                q.then_inc(o_ps[1][j], 1)

            def logits(bi):
                def visit(j, it):
                    wait(pe, xnT_done, j, it, 2)
                    if bi:
                        wait(pe, slots_done, j, it, bi)
                    for n in range(NT):
                        mm(bank[4 * j + n][:, :], xnT[j][:, tile_cols(bi * NT + n)],
                           snT[:, :]).then_inc(lt_ps[1][j], 1)
                return visit

            def t_logits(bi):
                def visit(j, it):
                    if bi:
                        wait(pe, slotsT_done, j, it, bi)
                    wait(pe, lt_done, j, it, 2 * bi + 2)
                    for m in range(MT):
                        o = bank[4 * j + 2 + m // 2]
                        for n in range(NT):
                            at = (m % 2) * L + n * P
                            q = nc.tensor.matmul(o[:, at:at + P], lt_sb[j][:, n, tile_cols(m)], ident[:, :],
                                                 is_transpose=True, start=at == 0, stop=at == 512 - P,
                                                 skip_group_check=True)
                        if m % 2:
                            q.then_inc(ls_ps[1][j], 1)
                return visit

            def shifts(bi):
                def visit(j, it):
                    wait(pe, diag_r_done, j, it, bi + 1)
                    wait(pe, diag_c_done, j, it, bi + 1)
                    for n in range(NT):
                        nc.tensor.matmul(bank[4 * j + n][:, :], neg_shift[:, :], diag_c[j][:, :, :],
                                         start=False, stop=True, skip_group_check=True
                                         ).then_inc(disp_ps[1][j], 1)
                    for m2 in range(2):
                        nc.tensor.matmul(bank[4 * j + 2 + m2][:, :], neg_shift[:, :],
                                         diag_r[j][:, :, :].rearrange("p n t -> p (n t)").unsqueeze(1).broadcast_to((P, 2, L)),
                                         start=False, stop=True, skip_group_check=True
                                         ).then_inc(comb_ps[1][j], 1)
                return visit

            def fill_slots(bi):
                def visit(j, it):
                    wait(pe, disp_done, j, it, 2 * bi + 2)
                    for m in range(MT):
                        o = bank[4 * j + m // 2][:, (m % 2) * (P + 1):(m % 2 + 1) * (P + 1)]
                        for n in range(NT):
                            q = mm(o, e_disp[j][:, n, tile_cols(m)], xn2tok[j][:, bi * NT + n, :],
                                   start=n == 0, stop=n == NT - 1)
                        if m % 2:
                            q.then_inc(slots_ps[1][j], 1)
                return visit

            def t_slots(bi):
                def visit(j, it):
                    wait(pe, slots_done, j, it, bi + 1)
                    wait(pe, comb_done, j, it, 2 * bi + 2)
                    for m in range(MT):
                        q = nc.tensor.transpose(bank[4 * j + 2][:, tile_cols(m)], slots[j][:, m, :], ident[:, :])
                    q.then_inc(slotsT_ps[1][j], 1)
                return visit

            visits = [(3.5, t_xn(0)), (5, project1), (7, project2), (9, project3), (10, scores),
                      (11, running_sums), (12.5, part_rows), (12.6, t_xh),
                      (14, segment(0)), (14.1, segment(1)), (16, segment(2)), (16.1, segment(3)),
                      (19, y_of(0)), (19.1, segment(4)), (21, segment(5)), (23, y_of(1)),
                      (26, project_out), (33.5, t_xn(1))]
            for bi in range(BP):
                o = 9 * bi
                visits += [(35.1 + o, logits(bi)), (37 + o, t_logits(bi)), (39 + o, shifts(bi)),
                           (41 + o, fill_slots(bi)), (43 + o, t_slots(bi))]
            with pe.Fori(0, PASSES) as it:
                run(visits, it)

            for j in range(2):
                wait(pe, slotsT_done, j, PASSES - 1)
            with pe.Fori(0, E // 2) as it:
                for j in range(2):
                    wait(pe, w1_in, j, it)
                    for k in range(HC):
                        if j == 0:
                            wait_before(pe, gelu_done, 1, it)
                        else:
                            wait(pe, gelu_done, 0, it, k + 1)
                        mm(bank[k][:, :], w1_sb[j][:, tile_cols(k)],
                           slotsT[:, bass.ds(it * 2 + j, 1), :, :].rearrange("p e b s -> p (e b s)")
                           ).then_inc(hid_ps[1][j], 1)
                for j in range(2):
                    wait(pe, w2_in, j, it)
                    wait(pe, gelu_done, j, it)
                    wait_before(pe, eoT_done, j, it)
                    for k in range(HC):
                        q = mm(bank[4 + j][:, :], w2_sb[j][:, k, :], act_h[j][k // 2][:, k % 2, :],
                               start=k == 0, stop=k == HC - 1)
                    q.then_inc(eoT_ps[1][j], 1)
                for j in range(2):
                    wait(pe, eoT_done, j, it)
                pe.wait_ge(eo_done, it * 2 + 1)
                for b in range(B):
                    q = nc.tensor.transpose(bank[6 + b // 4][:, tile_cols(b % 4)],
                                            eoT[:, b, :, :].rearrange("p e s -> p (e s)"), ident[:, :])
                    if b % 4 == 3:
                        q.then_inc(eo_ps, 1)
            pe.wait_ge(eo_done, E + 1)
            pe.wait_ge(s_eo_ones, 1)
            with pe.Fori(0, B // 2) as it:
                for j in range(2):
                    wait(pe, cb_done, j, it)
                    wait_before(pe, y_out, j, it)
                    for n in range(NT):
                        for m in range(MT):
                            q = mm(bank[2 * j + n][:, 0:P + 1], cbuf[j][:, m // 2, (m % 2) * L + n * P:(m % 2) * L + n * P + P],
                                   eo[:, bass.ds(it * 2 + j, 1), m, :].rearrange("p b d -> p (b d)"),
                                   start=m == 0, stop=m == MT - 1)
                        q.then_inc(comb_out_ps[1][j], 1)

        @block.scalar
        def _(act):
            A = nc.scalar.activation
            start_from_base(act, slotsT_done, gelu_done)
            act.sem_inc(eo_done, 1)
            nc.scalar.preload_act_table(ACT.Exp)
            act.wait_ge(s_in, N_IN)
            for m in range(MT):
                A(se_sq[:, :], se_nat[:, m, :], ACT.Square, scale=float(DM) ** -0.5, accum_out=se_ss[:, m:m + 1]).then_inc(s_act0, 1)
                act.wait_ge(s_act0, m + 1)
            act.wait_ge(s_in2, N_IN2)
            A(expA_t[:, :], expA_row[:, :], ACT.Exp).then_inc(s_act0, 1)
            act.wait_ge(s_dve0, SETUP_VEC)
            A(cs_t[:, :], vecT[:, RC:RC + B], ACT.Tanh, scale=0.5).then_inc(s_act0, 1)
            act.wait_ge(s_ready, 1)

            def mods(j, it, bi):
                return bass.ds(it * 2 * BP + j * BP + bi, 1)

            def mean_squares(layer):
                def visit(j, it):
                    wait(act, h_done, j, it, layer + 1)
                    for t in range(TP):
                        q = A(xn2tok[j][:, t, 0:P], hh[j][:, t, :], ACT.Square, scale=float(DM) ** -0.5,
                              accum_out=ms[j][:, t:t + 1])
                    q.then_inc(ms_done[1][j], 1)
                return visit

            def copy_xnT(layer):
                def visit(j, it):
                    wait(act, xnT_ps, j, it, layer + 1)
                    A(xnT[j][:, :], bank[4 * j][:, :], ACT.Copy).then_inc(xnT_done[1][j], 1)
                return visit

            def first_tap(j, it):
                for k in range(CT):
                    wait(act, x_ps, j, it, k + 1)
                    A(xcT[j][:, k, :], bank[4 * j + k][:, :], ACT.Identity, bias=vecT[:, RCB + k:RCB + k + 1],
                      scale=convw[:, k, TAPS - 1:TAPS]).then_inc(tap0_done[1][j], 1)
                wait(act, bc_ps, j, it, 1)
                A(BT[j][:, :], bank[4 * j + 2][:, :], ACT.Copy).then_inc(bc_done[1][j], 1)

            def exp_dt(j, it):
                wait(act, nabs_done, j, it)
                A(dv[j][:, EDT, :], dv[j][:, NABS, :], ACT.Exp).then_inc(edt_done[1][j], 1)

            def copy_c(j, it):
                wait(act, bc_ps, j, it, 2)
                A(CTr[j][:, :], bank[4 * j + 3][:, :], ACT.Copy).then_inc(bc_done[1][j], 1)

            def tanh_xz(k):
                def visit(j, it):
                    wait(act, z_ps, j, it, k + 1)
                    A(zsT[j][:, k, :], bank[4 * j + 2 + k][:, :], ACT.Tanh, scale=0.5).then_inc(zt_done[1][j], 1)
                    wait(act, conv_done, j, it, k + 1)
                    A(xhT[j][:, k, :], xcT[j][:, k, :], ACT.Tanh, scale=0.5).then_inc(xt_done[1][j], 1)
                return visit

            def copy_scores(j, it):
                for bi in range(BP):
                    wait(act, g_ps, j, it, bi + 1)
                    A(gm[j][:, bi, :, :].rearrange("p n t -> p (n t)"), bank[4 * j + bi][:, 0:3 * P], ACT.Copy
                      ).then_inc(g_done[1][j], 1)

            def copy_parts(j, it):
                wait(act, parts_ps, j, it)
                A(ksm[j][:, :], bank[4 * j + 2][:, :].bitcast(bf16)[:, 0:W], ACT.Copy).then_inc(ksm_done[1][j], 1)

            def decay(f):
                def visit(j, it):
                    wait(act, seg_ps, j, it, f + 1)
                    if f >= 3:
                        wait(act, m_done, j, it, f - 2)
                    A(seg_e[j][:, f % 3, :], bank[4 * j + 2 + f % 2][:, :], ACT.Exp).then_inc(seg_done[1][j], 1)
                return visit

            def copy_logits(bi):
                def visit(j, it):
                    for n in range(NT):
                        wait(act, lt_ps, j, it, 2 * bi + n + 1)
                        A(lt_sb[j][:, n, :], bank[4 * j + n][:, :], ACT.Copy).then_inc(lt_done[1][j], 1)
                return visit

            def exps(bi):
                def visit(j, it):
                    for n in range(NT):
                        wait(act, disp_ps, j, it, 2 * bi + n + 1)
                        A(e_disp[j][:, n, :], bank[4 * j + n][:, :], ACT.Exp).then_inc(disp_done[1][j], 1)
                    for m2 in range(2):
                        wait(act, comb_ps, j, it, 2 * bi + m2 + 1)
                        A(combT[:, mods(j, it, bi), 2 * m2:2 * m2 + 2, :].rearrange("p b m t -> p (b m t)"),
                          bank[4 * j + 2 + m2][:, :], ACT.Exp).then_inc(comb_done[1][j], 1)
                return visit

            def copy_slotsT(bi):
                def visit(j, it):
                    wait(act, slotsT_ps, j, it, bi + 1)
                    A(slotsT[:, :, mods(j, it, bi), :].rearrange("p e b s -> p e (b s)"),
                      bank[4 * j + 2][:, :].rearrange("p (e s) -> p e s", e=E),
                      ACT.Identity, scale=vecT[:, RG:RG + 1]).then_inc(slotsT_done[1][j], 1)
                return visit

            visits = [(2, mean_squares(0)), (4, copy_xnT(0)), (6, first_tap), (7, exp_dt), (8, copy_c),
                      (9.5, tanh_xz(0)), (10.5, tanh_xz(1)), (10.9, copy_scores), (12.55, copy_parts),
                      (15, decay(0)), (15.1, decay(1)), (17, decay(2)), (17.1, decay(3)), (20.5, decay(4)),
                      (22, decay(5)), (32, mean_squares(1)), (34, copy_xnT(1))]
            for bi in range(BP):
                o = 9 * bi
                visits += [(36.1 + o, copy_logits(bi)), (40 + o, exps(bi)), (43.5 + o, copy_slotsT(bi))]
            with act.Fori(0, PASSES) as it:
                run(visits, it)

            with act.Fori(0, E // 2) as it:
                for j in range(2):
                    for k in range(HC):
                        wait(act, hid_ps, j, it, k + 1)
                        wait_before(act, eoT_ps, j, it)
                        A(act_h[j][k // 2][:, k % 2, :], bank[k][:, :], ACT.Gelu,
                          bias=vecT[:, bass.ds(it * 2 * HC + (RB1 + j * HC + k), 1)]).then_inc(gelu_done[1][j], 1)
                for g in range(2):
                    act.wait_ge(eo_ps, it * 2 + (g + 2))
                    A(eo[:, 4 * g:4 * g + 4, bass.ds(it, 1), 0:P].rearrange("p b m d -> p b (m d)"),
                      bank[6 + g][:, :].rearrange("p (b d) -> p b d", b=4), ACT.Copy).then_inc(eo_done, 1)

        @block.vector
        def _(dve):
            V = nc.vector
            start_from_base(dve, slots_done, eoT_done, y_out)
            n0 = [0]

            def step0(q):
                n0[0] += 1
                q.then_inc(s_dve0, 1)
                dve.wait_ge(s_dve0, n0[0])

            dve.wait_ge(s_pe0, 1)
            step0(V.tensor_copy(vecT[:, :], bank[0][:, 0:VR]))
            assert n0[0] == SETUP_VEC
            dve.wait_ge(s_pool, POOL_ALL + 2)
            for m in range(MT):
                step0(V.tensor_scalar(se_nat[:, m, :], se_nat[:, m, :], se_r[:, m:m + 1], None, ALU.mult))
            assert n0[0] == SETUP_SE
            dve.wait_ge(s_act0, MT + 2)
            step0(V.scalar_tensor_tensor(cs[:, :], cs_t[:, :], 1.0, vecT[:, RC:RC + B], ALU.add, ALU.mult))
            step0(V.tensor_scalar(cs[:, :], cs[:, :], 0.5, None, ALU.mult))
            assert n0[0] == SETUP_CS
            dve.wait_ge(s_pe0, 2)
            step0(V.tensor_scalar(winT[:, 0:512], bank[1][:, :], vecT[:, RNW:RNW + 1], None, ALU.mult))
            step0(V.tensor_scalar(winT[:, 512:DT0], bank[2][:, 0:DT0 - 512], vecT[:, RNW:RNW + 1], None, ALU.mult))
            step0(V.tensor_scalar(winT[:, DT0:ROWS], bank[3][:, 0:H], vecT[:, RNW:RNW + 1], None, ALU.mult))
            step0(V.tensor_scalar(woT[:, :, :], bank[3][:, P:P + CT * P].rearrange("p (k d) -> p k d", k=CT),
                                  0.5, None, ALU.mult))
            step0(V.tensor_scalar(d_half[:, :], d_col[:, :], 0.5, None, ALU.mult))
            dve.wait_ge(s_pe0, 3)
            step0(V.tensor_tensor(g_all[:, :], vecT[:, RG:RG + 1], vecT[:, RSG:RSG + 1], ALU.mult))
            step0(V.tensor_scalar(snT[:, :], bank[4][:, :], g_all[:, :], None, ALU.mult))
            dve.wait_ge(s_pe0, 4)
            for g in range(2):
                step0(V.tensor_copy(mod_rows[:, 3 * g:3 * g + 3, :],
                                    bank[5 + g][0:B, 0:3 * P].rearrange("b (m d) -> b m d", m=3)))
            for m in (1, 4):
                step0(V.tensor_scalar(mod_rows[:, m, :], mod_rows[:, m, :], 1.0, None, ALU.add))
            step0(V.tensor_copy(gbT[:, :], bank[7][:, 0:B]))
            for g, sg in ((mod_rows[:, 2, :], sgn_r[:, :]), (gbT[:, :], sgn_T[:, :])):
                step0(V.tensor_scalar(sg, g, 0.0, 2.0, ALU.is_ge, ALU.mult))
                step0(V.tensor_scalar(sg, sg, 1.0, None, ALU.subtract))
                step0(V.scalar_tensor_tensor(g, g, -1.0, g, ALU.mult, ALU.max))
                step0(V.tensor_scalar(g, g, 0.25, None, ALU.max))
                step0(V.tensor_tensor(g, g, sg, ALU.mult))
            dve.sem_inc(s_ready, 2)

            count = [0, 0]

            def step(j, it, q):
                count[j] += 1
                q.then_inc(dve_own[1][j], 1)
                wait(dve, dve_own, j, it, count[j])

            def x1_tile(j, it, t, n=1):
                return x1tok[:, bass.ds(it * 2 * TP + (j * TP + t), n), :]

            def layer_input(layer, j, it, t):
                if layer == 0:
                    return xin[j][:, t, :]
                return x1_tile(j, it, t).rearrange("p t d -> p (t d)")

            def statistics(layer):
                def visit(j, it):
                    if layer == 0:
                        count[j] = 0
                        wait(dve, x_in, j, it)
                    hold(dve)
                    for t in range(TP):
                        q = V.bn_stats(bst[j][:, t, :], layer_input(layer, j, it, t))
                    step(j, it, q)
                    hold(dve)
                    for t in range(TP):
                        q = V.bn_aggr(mv[j][:, t, :], bst[j][:, t, :])
                    q.then_inc(var_done[1][j], 1)
                return visit

            def modulate(layer):
                def visit(j, it):
                    wait(dve, root_done, j, it, 2 * layer + 1)
                    for t in range(TP):
                        q = V.tensor_scalar(hh[j][:, t, :], layer_input(layer, j, it, t), mv[j][:, t, 0:1],
                                            root[j][:, t:t + 1], ALU.subtract, ALU.mult)
                    step(j, it, q)
                    wait(dve, mods_in, j, it)
                    for m, op in ((3 * layer + 1, ALU.mult), (3 * layer, ALU.add)):
                        for bi in range(BP):
                            v = hh[j][:, bi * NT:(bi + 1) * NT, :]
                            q = V.tensor_tensor(v, v, mods_bc[j][:, bi, m, :].unsqueeze(1).broadcast_to((P, NT, P)), op)
                        if op == ALU.mult:
                            step(j, it, q)
                    q.then_inc(h_done[1][j], 1)
                return visit

            def unit(layer):
                def visit(j, it):
                    wait(dve, root_done, j, it, 2 * layer + 2)
                    for t in range(TP):
                        q = V.tensor_scalar(xn2tok[j][:, t, 0:P], hh[j][:, t, :], root[j][:, t:t + 1], None, ALU.mult)
                    q.then_inc(xn_done[1][j], 1)
                return visit

            def dt_in(j, it):
                wait(dve, dt_ps, j, it)
                d = dv[j]
                V.tensor_tensor(d[:, VV, :].rearrange("p (t h) -> p t h", h=H),
                                bank[4 * j + 3][:, 0:TP * H].rearrange("p (t h) -> p t h", h=H),
                                dtb_row[:, :].unsqueeze(1).broadcast_to((P, TP, H)), ALU.add
                                ).then_inc(v_done[1][j], 1)
                wait(dve, v_done, j, it)
                V.scalar_tensor_tensor(d[:, NABS, :], d[:, VV, :], -1.0, d[:, VV, :], ALU.mult, ALU.min
                                       ).then_inc(nabs_done[1][j], 1)

            def softplus(j, it):
                wait(dve, edt_done, j, it)
                d = dv[j]
                step(j, it, V.tensor_scalar(d[:, U, :], d[:, EDT, :], 2.0, None, ALU.add))
                step(j, it, V.reciprocal(d[:, U, :], d[:, U, :]))
                step(j, it, V.tensor_tensor(d[:, U, :], d[:, U, :], d[:, EDT, :], ALU.mult))
                step(j, it, V.tensor_tensor(d[:, U2, :], d[:, U, :], d[:, U, :], ALU.mult))
                step(j, it, V.tensor_scalar(d[:, PP, :], d[:, U2, :], ATANH_TERMS[0], None, ALU.mult))
                for term in ATANH_TERMS[1:]:
                    step(j, it, V.scalar_tensor_tensor(d[:, PP, :], d[:, PP, :], term, d[:, U2, :], ALU.add, ALU.mult))
                step(j, it, V.scalar_tensor_tensor(d[:, PP, :], d[:, PP, :], 1.0, d[:, U, :], ALU.add, ALU.mult))
                step(j, it, V.tensor_scalar(d[:, VV, :], d[:, VV, :], 0.0, 0.5, ALU.max, ALU.mult))
                step(j, it, V.tensor_tensor(d[:, DTH, :], d[:, PP, :], d[:, VV, :], ALU.add))
                V.scalar_tensor_tensor(d[:, WD, :].rearrange("p (t h) -> p t h", h=H),
                                       d[:, DTH, :].rearrange("p (t h) -> p t h", h=H), 2.0,
                                       expA_t[:, :].unsqueeze(1).broadcast_to((P, TP, H)), ALU.mult, ALU.mult
                                       ).then_inc(w_done[1][j], 1)

            def conv(k):
                def visit(j, it):
                    wait(dve, tap0_done, j, it, k + 1)
                    acc = xcT[j][:, k, :].rearrange("p (b t) -> p b t", b=BP)
                    src = bank[4 * j + k][:, :].rearrange("p (b t) -> p b t", b=BP)
                    for back in range(1, TAPS):
                        q = V.scalar_tensor_tensor(acc[:, :, back:L], src[:, :, 0:L - back],
                                                   convw[:, k, TAPS - 1 - back:TAPS - back],
                                                   acc[:, :, back:L], ALU.mult, ALU.add)
                        if back < TAPS - 1:
                            step(j, it, q)
                    q.then_inc(conv_done[1][j], 1)
                return visit

            def silus(k):
                def visit(j, it):
                    wait(dve, zt_done, j, it, k + 1)
                    V.scalar_tensor_tensor(zsT[j][:, k, :], zsT[j][:, k, :], 1.0, bank[4 * j + 2 + k][:, :],
                                           ALU.add, ALU.mult).then_inc(zs_done[1][j], 1)
                    wait(dve, xt_done, j, it, k + 1)
                    V.scalar_tensor_tensor(xhT[j][:, k, :], xhT[j][:, k, :], 1.0, xcT[j][:, k, :],
                                           ALU.add, ALU.mult).then_inc(xh_done[1][j], 1)
                return visit

            def parts(j, it):
                wait(dve, cum_ps, j, it)
                cum = bank[4 * j + 2][:, 0:TP * H].rearrange("p (t h) -> p t h", h=H)
                r = dv[j][:, PP, :].rearrange("p (t h) -> p t h", h=H)

                def part(i):
                    return Q[j][:, :, PART_ROW + i * H:PART_ROW + (i + 1) * H]
                step(j, it, V.tensor_copy(part(0), cum))
                step(j, it, V.tensor_tensor(r, cum, part(0), ALU.subtract))
                step(j, it, V.tensor_copy(part(1), r))
                step(j, it, V.tensor_tensor(r, r, part(1), ALU.subtract))
                V.tensor_copy(part(2), r).then_inc(parts_done[1][j], 1)

            def dt_times_x(j, it):
                for bi in range(BP):
                    wait(dve, xht_ps, j, it, bi + 1)
                    V.tensor_tensor(
                        dtx[j][:, bi * NT:(bi + 1) * NT, :].rearrange("p t (h d) -> p (t h) d", h=H),
                        bank[4 * j + bi][:, :].rearrange("p (g d) -> p g d", d=HD),
                        dv[j][:, DTH, bi * NT * H:(bi + 1) * NT * H].unsqueeze(2).broadcast_to((P, NT * H, HD)),
                        ALU.mult).then_inc(dtx_done[1][j], 1)

            def weigh(f):
                def visit(j, it):
                    bi, g = divmod(f, 3)
                    wait(dve, seg_done, j, it, f + 1)
                    if f >= 3:
                        wait(dve, y_ps, j, it, 1)
                    if g < 2:
                        n, s = 2, gm[j][:, bi, 0:2, :].rearrange("p n t -> p (n t)")
                    else:
                        n, s = H, gm[j][:, bi, 2, :]
                    w = 512 // n
                    V.tensor_tensor(seg_m[j][:, g, :].rearrange("p (h t) -> p h t", h=n),
                                    seg_e[j][:, g, :].rearrange("p (h t) -> p h t", h=n),
                                    s.unsqueeze(1).broadcast_to((P, n, w)), ALU.mult).then_inc(m_done[1][j], 1)
                return visit

            def gate(j, it):
                wait(dve, y_ps, j, it)
                for k in range(CT):
                    q = V.scalar_tensor_tensor(xhT[j][:, k, :], xhT[j][:, k, :], d_half[:, k:k + 1],
                                               bank[4 * j + k][:, :], ALU.mult, ALU.add)
                step(j, it, q)
                V.tensor_tensor(xhT[j][:, :, :], xhT[j][:, :, :], zsT[j][:, :, :], ALU.mult
                                ).then_inc(yg_done[1][j], 1)

            def x1(j, it):
                wait(dve, o_ps, j, it)
                for bi in range(BP):
                    q = V.tensor_tensor(hh[j][:, bi * NT:(bi + 1) * NT, :],
                                        bank[4 * j + 2][:, bi * L:(bi + 1) * L].rearrange("p (t d) -> p t d", t=NT),
                                        mods_bc[j][:, bi, 2, :].unsqueeze(1).broadcast_to((P, NT, P)), ALU.mult)
                step(j, it, q)
                wait(dve, basis_done, j, it)
                V.tensor_tensor(x1_tile(j, it, 0, TP), hh[j][:, :, :], basis[j][:, :, :], ALU.add
                                ).then_inc(x1_done[1][j], 1)
                wait(dve, x1_done, j, it)

            def token_max(bi):
                def visit(j, it):
                    wait(dve, lt_done, j, it, 2 * bi + 2)
                    step(j, it, V.reduce_max(rmax[j][:, :], lt_sb[j][:, :, :], AX.X))
                    V.tensor_tensor(diag_r[j][:, :, :], ident_shift[:, :].unsqueeze(1).broadcast_to((P, NT, P)),
                                    rmax[j][:, :].unsqueeze(2).broadcast_to((P, NT, P)), ALU.mult
                                    ).then_inc(diag_r_done[1][j], 1)
                return visit

            def slot_max(bi):
                def visit(j, it):
                    for m2 in range(2):
                        wait(dve, ls_ps, j, it, 2 * bi + m2 + 1)
                        q = V.reduce_max(cmax[j][:, 2 * m2:2 * m2 + 2],
                                         bank[4 * j + 2 + m2][:, :].rearrange("p (m t) -> p m t", m=2), AX.X)
                    step(j, it, q)
                    V.tensor_tensor(diag_c[j][:, :, :], ident_shift[:, :].unsqueeze(1).broadcast_to((P, MT, P)),
                                    cmax[j][:, :].unsqueeze(2).broadcast_to((P, MT, P)), ALU.mult
                                    ).then_inc(diag_c_done[1][j], 1)
                return visit

            def norm_slots(bi):
                def visit(j, it):
                    ps = [bank[4 * j + m2][:, 0:2 * (P + 1)].rearrange("p (m d) -> p m d", m=2) for m2 in range(2)]
                    for m2 in range(2):
                        wait(dve, slots_ps, j, it, 2 * bi + m2 + 1)
                        q = V.reciprocal(rcs[j][:, 2 * m2:2 * m2 + 2], ps[m2][:, :, P])
                    step(j, it, q)
                    for m2 in range(2):
                        q = V.tensor_tensor(slots[j][:, 2 * m2:2 * m2 + 2, :], ps[m2][:, :, 0:P],
                                            rcs[j][:, 2 * m2:2 * m2 + 2].unsqueeze(2).broadcast_to((P, 2, P)), ALU.mult)
                    q.then_inc(slots_done[1][j], 1)
                return visit

            visits = [(0, statistics(0)), (1, modulate(0)), (3, unit(0)), (6, dt_in), (7, conv(0)),
                      (8, softplus), (9, conv(1)), (10, silus(0)), (10.8, silus(1)), 
                      (12, parts), (13, dt_times_x),
                      (16, weigh(0)), (16.1, weigh(1)), (18, weigh(2)), (20, weigh(3)), (21, weigh(4)), (22.5, weigh(5)),
                      (25, gate), (27, x1), (28, statistics(1)),
                      (31, modulate(1)), (33, unit(1))]
            for bi in range(BP):
                o = 9 * bi
                visits += [(37 + o, token_max(bi)), (38 + o, slot_max(bi)), (42 + o, norm_slots(bi))]
            with dve.Fori(0, PASSES) as it:
                run(visits, it)
            assert count == [DVE_STEPS] * 2, count

            with dve.Fori(0, E // 2) as it:
                for j in range(2):
                    wait(dve, eoT_ps, j, it)
                    dve.wait_ge(eo_ps, it * 2 + 1)
                    V.scalar_tensor_tensor(eoT[:, :, j, :], bank[4 + j][:, :].rearrange("p (b s) -> p b s", b=B),
                                           vecT[:, bass.ds(it * 2 + (RB2 + j), 1)],
                                           gbT[:, :].unsqueeze(2).broadcast_to((P, B, S)), ALU.add, ALU.mult
                                           ).then_inc(eoT_done[1][j], 1)
            with dve.Fori(0, B // 2) as it:
                for j in range(2):
                    wait_before(dve, comb_out_ps, j, it)
                    V.tensor_copy(cbuf[j][:, :, :].rearrange("p a b -> p (a b)"),
                                  combT[:, bass.ds(it * 2 + j, 1), :, :].rearrange("p b m t -> p (b m t)")
                                  ).then_inc(cb_done[1][j], 1)
                for j in range(2):
                    wait_before(dve, y_sent, j, it)
                    for n in range(NT):
                        wait(dve, comb_out_ps, j, it, n + 1)
                        ps = bank[2 * j + n]
                        q = V.reciprocal(rden[j][:, n:n + 1], ps[:, P:P + 1])
                    q.then_inc(rden_done[1][j], 1)
                    wait(dve, rden_done, j, it)
                    for n in range(NT):
                        q = V.scalar_tensor_tensor(yout[j][:, n, :], bank[2 * j + n][:, 0:P], rden[j][:, n:n + 1],
                                                   x1tok[:, bass.ds(it * 2 * NT + (j * NT + n), 1), :]
                                                   .rearrange("p t d -> p (t d)"), ALU.mult, ALU.add)
                    q.then_inc(y_out[1][j], 1)


_INS = ["L0_attn_x", "L0_attn_norm_w", "L0_attn_in_proj_w", "L0_attn_conv_w", "L0_attn_conv_b", "L0_attn_A_log",
        "L0_attn_D", "L0_attn_dt_bias", "L0_attn_out_proj_w", "L0_ffn_norm_gamma", "L0_ffn_slot_norm_gamma",
        "L0_ffn_slot_embeds", "L0_ffn_w1", "L0_ffn_b1", "L0_ffn_w2", "L0_ffn_b2", "L0_c", "L0_wmod"]


def kernel(**inputs):
    import numpy as _np
    import concourse.bacc as _bacc
    from concourse import mybir as _mybir
    from concourse.bass_utils import run_bass_kernel_spmd as _run

    nc = _bacc.Bacc("TRN2", target_bir_lowering=False, num_devices=1)
    arrays, args = {}, []
    for name in _INS:
        a = _np.ascontiguousarray(inputs[name])
        arrays[f"in_{name}_dram"] = a
        args.append(nc.dram_tensor(f"in_{name}_dram", a.shape, _mybir.dt.from_np(a.dtype), kind="ExternalInput").ap())
    shape = inputs["L0_attn_x"].shape
    args.append(nc.dram_tensor("out_0_dram", shape, _mybir.dt.float32, kind="ExternalOutput").ap())
    bass_adaln_mamba_softmoe_kernel(nc, *args)
    r = _run(nc, [arrays], core_ids=[0])
    return r.results[0]["out_0_dram"]
```

```python
import concourse.bass as bass
from concourse import mybir
from contextlib import ExitStack


def bass_adaln_mamba_softmoe_kernel(
    nc: bass.Bass,
    x: bass.AP,
    norm_w: bass.AP,
    in_proj_w: bass.AP,
    conv_w: bass.AP,
    conv_b: bass.AP,
    A_log: bass.AP,
    D: bass.AP,
    dt_bias: bass.AP,
    out_proj_w: bass.AP,
    norm_gamma: bass.AP,
    slot_norm_gamma: bass.AP,
    slot_embeds: bass.AP,
    w1: bass.AP,
    b1: bass.AP,
    w2: bass.AP,
    b2: bass.AP,
    c: bass.AP,
    wmod: bass.AP,
    out: bass.AP,
):
    fp32, bf16, fp16 = mybir.dt.float32, mybir.dt.bfloat16, mybir.dt.float16
    ALU = mybir.AluOpType
    ACT = mybir.ActivationFunctionType
    AX = mybir.AxisListType

    B, L, DM = x.shape
    H = A_log.shape[0]
    DI = out_proj_w.shape[1]
    HD = DI // H
    TAPS = conv_w.shape[1]
    E, S, _ = slot_embeds.shape
    HID = w1.shape[2]
    P = 128
    CT = DI // P
    NT = L // P
    SL = E * S
    MT = SL // P
    HC = HID // P
    BP = 2
    TP = BP * NT
    W = BP * L
    LN_EPS, RMS_EPS, NORM_FLOOR = 1e-5, 1e-6, 1e-12
    ROWS = in_proj_w.shape[0]
    ROW_BLOCKS = ROWS // P
    Z0, X0, B0, C0 = 0, DI, 2 * DI, 2 * DI + P
    DT0 = 2 * DI + 2 * P
    SHIFT = 64.0
    ATANH_TERMS = [1.0 / k for k in range(15, 1, -2)]
    PART_ROW = 32

    ctx = ExitStack()
    with ctx:
        def sb(name, shape, dt=fp32):
            return ctx.enter_context(nc.sbuf_tensor(name, shape, dt))

        per_pass = {}
        base_value = {}

        def sem(name, count=1, base=0):
            per_pass[name] = count
            base_value[name] = base
            return name, [ctx.enter_context(nc.semaphore(f"{name}_{j}")) for j in range(2)]

        def wait(eng, s, j, it, k=None):
            name, sems = s
            n = per_pass[name]
            eng.wait_ge(sems[j], it * n + ((n if k is None else k) + base_value[name]))

        def hold(eng):
            eng.sem_inc(s_held, 1)

        def wait_before(eng, s, j, it):
            name, sems = s
            eng.wait_ge(sems[j], it * per_pass[name] + base_value[name])

        def start_from_base(eng, *names):
            for name, sems in names:
                for j in range(2):
                    eng.sem_inc(sems[j], base_value[name])

        s_held = ctx.enter_context(nc.semaphore("s_held"))

        ident = sb("ident", [P, P])
        ident_b = sb("ident_b", [P, P], bf16)
        ident_shift = sb("ident_shift", [P, P], fp16)
        neg_shift = sb("neg_shift", [P, P], fp16)
        ones_sq = sb("ones_sq", [P, P])
        neg_half = sb("neg_half", [P, TP])
        causal = sb("causal", [P, P])
        future = sb("future", [P, P], bf16)
        eo = sb("eo", [P, B, MT, P + 1])
        as_loaded = eo[:, :, :, :].rearrange("p b m d -> p (b m d)")
        w_nat = as_loaded[:, 0:ROW_BLOCKS * P].rearrange("p (n d) -> p n d", n=ROW_BLOCKS)
        wmod_sb = as_loaded[:, ROW_BLOCKS * P:(ROW_BLOCKS + 6) * P]
        se_nat = as_loaded[:, (ROW_BLOCKS + 6) * P:(ROW_BLOCKS + 6 + MT) * P].rearrange("p (n d) -> p n d", n=MT)
        wo_nat = as_loaded[:, (ROW_BLOCKS + 6 + MT) * P:(ROW_BLOCKS + 6 + MT + CT) * P]
        se_sq = as_loaded[:, (ROW_BLOCKS + 6 + MT + CT) * P:(ROW_BLOCKS + 7 + MT + CT) * P]
        dt_nat = sb("dt_nat", [H, P])
        winT = sb("winT", [P, ROWS])
        woT = sb("woT", [P, CT, P])
        se_ss = sb("se_ss", [P, MT])
        se_r = sb("se_r", [P, MT])
        snT = sb("snT", [P, SL])
        convw = sb("convw", [P, CT, TAPS])
        d_col = sb("d_col", [P, CT])
        d_half = sb("d_half", [P, CT])
        blk = sb("blk", [P, 2, H])
        dtb_row = sb("dtb_row", [P, H])
        expA_row = sb("expA_row", [P, H])
        expA_t = sb("expA_t", [P, H])
        RB1, RB2 = 0, E * HC
        RC = RB2 + E
        RCB = RC + B
        RNW = RCB + CT
        RG, RSG = RNW + 1, RNW + 2
        VR = RSG + 1
        vec_nat = sb("vec_nat", [VR, P])
        vecT = sb("vecT", [P, VR])
        cs = sb("cs", [P, B])
        cs_t = sb("cs_t", [P, B])
        g_all = sb("g_all", [P, 1])
        gbT = sb("gbT", [P, B])
        mod_rows = sb("mod_rows", [B, 6, P])
        sgn_T = sb("sgn_T", [P, B])
        sgn_r = sb("sgn_r", [B, P])
        slotsT = sb("slotsT", [P, E, B, S])
        x1tok = sb("x1tok", [P, B * NT, P])
        combT = sb("combT", [P, B, MT, L])

        def two(name, shape, dt=fp32):
            return [sb(f"{name}{j}", shape, dt) for j in range(2)]

        xin = two("xin", [P, TP, P])
        bst = two("bst", [P, TP, 6])
        mv = two("mv", [P, TP, 2])
        root = two("root", [P, TP])
        ms = two("ms", [P, TP])
        hh = two("hh", [P, TP, P])
        basis = two("basis", [P, TP, P])
        mods_bc = two("mods_bc", [P, BP, 5, P])
        xntok = two("xntok", [P, TP, P])
        xnT = two("xnT", [P, W])
        zsT = two("zsT", [P, CT, W])
        xcT = two("xcT", [P, CT, W])
        xhT = two("xhT", [P, CT, W])
        BT = two("BT", [P, W])
        CTr = two("CTr", [P, W])
        dv = two("dv", [P, 8, TP * H])
        Q = two("Q", [P, TP, P], bf16)
        ksm = two("ksm", [P, W], bf16)
        rsm = two("rsm", [P, H, W], bf16)
        gm = two("gm", [P, BP, 3, P])
        seg_e = two("seg_e", [P, 3, 512])
        seg_m = two("seg_m", [P, 3, 512])
        xn2tok = two("xn2tok", [P, TP, P + 1])
        rmax = two("rmax", [P, NT])
        cmax = two("cmax", [P, MT])
        diag_r = two("diag_r", [P, NT, P], fp16)
        diag_c = two("diag_c", [P, MT, P], fp16)
        rcs = two("rcs", [P, MT])

        lt_sb = [t[:, 0:NT, :] for t in seg_e]
        e_disp = [t[:, 0:NT, :] for t in seg_m]
        dtx = [t[:, :, :].rearrange("p k t -> p (k t)").rearrange("p (t c) -> p t c", t=TP) for t in xcT]
        xn2T = CTr
        slots = [t[:, :].rearrange("p (m d) -> p m d", m=MT) for t in BT]

        bank = [ctx.enter_context(nc.psum_tensor(f"bank{i}", [P, 512], fp32)) for i in range(8)]

        s_vec, s_wmod, s_w, s_se, s_small = [ctx.enter_context(nc.semaphore(n)) for n in
                                             ("s_vec", "s_wmod", "s_w", "s_se", "s_small")]
        s_pool = ctx.enter_context(nc.semaphore("s_pool"))
        s_pe0 = ctx.enter_context(nc.semaphore("s_pe0"))
        s_dve0 = ctx.enter_context(nc.semaphore("s_dve0"))
        s_act0 = ctx.enter_context(nc.semaphore("s_act0"))
        s_ready = ctx.enter_context(nc.semaphore("s_ready"))

        s_mod = ctx.enter_context(nc.semaphore("s_mod"))
        s_eo_ones = ctx.enter_context(nc.semaphore("s_eo_ones"))

        x_in = sem("x_in", 16)
        mods_in = sem("mods_in", 16 * BP)
        var_done = sem("var_done", 2)
        root_done = sem("root_done", 4)
        h_done = sem("h_done", 2, base=1)
        ms_done = sem("ms_done", 2)
        basis_done = sem("basis_done", base=1)
        xn_done = sem("xn_done", 2)
        xnT_ps = sem("xnT_ps", 2)
        xnT_done = sem("xnT_done", 2)
        pool_own = sem("pool_own", 5)
        dt_ps = sem("dt_ps")
        x_ps = sem("x_ps", 2)
        bc_ps = sem("bc_ps", 2)
        bc_done = sem("bc_done", 2)
        z_ps = sem("z_ps", 2)
        v_done = sem("v_done")
        nabs_done = sem("nabs_done")
        edt_done = sem("edt_done")
        tap0_done = sem("tap0_done", 2)
        conv_done = sem("conv_done", 2)
        xt_done = sem("xt_done", 2)
        zt_done = sem("zt_done", 2)
        zs_done = sem("zs_done", 2)
        xh_done = sem("xh_done", 2)
        w_done = sem("w_done")
        cum_ps = sem("cum_ps")
        parts_done = sem("parts_done")
        parts_ps = sem("parts_ps")
        ksm_done = sem("ksm_done")
        rsm_in = sem("rsm_in", 48)
        g_ps = sem("g_ps", 2)
        g_done = sem("g_done", 2)
        xht_ps = sem("xht_ps", 2)
        dtx_done = sem("dtx_done", 2)
        seg_ps = sem("seg_ps", 6)
        seg_done = sem("seg_done", 6)
        m_done = sem("m_done", 6)
        y_ps = sem("y_ps", 2, base=1)
        yg_done = sem("yg_done")
        o_ps = sem("o_ps")
        x1_done = sem("x1_done")
        lt_ps = sem("lt_ps", 4)
        lt_done = sem("lt_done", 4)
        diag_r_done = sem("diag_r_done", 2)
        ls_ps = sem("ls_ps", 4)
        diag_c_done = sem("diag_c_done", 2)
        disp_ps = sem("disp_ps", 4)
        comb_ps = sem("comb_ps", 4)
        disp_done = sem("disp_done", 4)
        comb_done = sem("comb_done", 4, base=1)
        slots_ps = sem("slots_ps", 4)
        slots_done = sem("slots_done", 2, base=1)
        slotsT_ps = sem("slotsT_ps", 2)
        slotsT_done = sem("slotsT_done", 2, base=1)
        STEPS = {"norm1": 3, "rest": 33}
        own_norm1 = sem("own_norm1", STEPS["norm1"])
        own_rest = sem("own_rest", STEPS["rest"])

        w1_sb = two("w1_sb", [P, HID])
        w2_sb = two("w2_sb", [P, HC, P])
        act_h = [zsT[0], zsT[1]], [xcT[0], xcT[1]]
        eoT = seg_e[0][:, 0:2, :].rearrange("p a (b e s) -> p (a b) e s", e=2, s=S)
        w1_in = sem("w1_in", 16)
        w2_in = sem("w2_in", 16)
        hid_ps = sem("hid_ps", HC)
        gelu_done = sem("gelu_done", HC, base=1)
        eoT_ps = sem("eoT_ps", base=1)
        eoT_done = sem("eoT_done", base=1)
        eo_ps = ctx.enter_context(nc.semaphore("eo_ps"))
        eo_done = ctx.enter_context(nc.semaphore("eo_done"))
        cb_done = sem("cb_done")
        comb_out_ps = sem("comb_out_ps", NT, base=1)
        y_out = sem("y_out", base=1)
        y_sent = sem("y_sent", 16, base=1)
        rden_done = sem("rden_done")
        rden = two("rden", [P, NT])
        cbuf = xhT
        yout = xin

        mod_dram = nc.dram_tensor("mod_dram", (B, 6 * P), fp32, kind="Internal").ap()
        PASSES = B // (2 * BP)
        SKEW, PERIOD, START = 4.37, 225.44, -14

        VV, NABS, EDT, U, U2, PP, DTH, WD = range(8)
        N_VEC, N_W, N_SMALL = 16 * 7, 16 * 3, 16 * (3 + H)
        POOL_IDENT, POOL_ALL = 2, 17
        POOL_SE = POOL_ALL + 2
        ACT_TANH = 1
        ACT_SE = ACT_TANH + MT
        DVE_VEC = 1
        DVE_CS = DVE_VEC + 2
        PE_VEC, PE_MOD, PE_W, PE_SE = 1, 2, 3, 4

        def pipeline(eng, visits):
            todo = []
            for j in range(2):
                for n, (p, _) in enumerate(visits):
                    late, at = divmod(p - START + SKEW * j, PERIOD)
                    assert late in (0, 1)
                    todo.append((at, j, n, int(late)))
            todo.sort()

            def turn(new, old):
                for _, j, n, late in todo:
                    it = old if late else new
                    if it is not None:
                        visits[n][1](j, it)

            turn(0, None)
            with eng.Fori(0, PASSES - 1) as i:
                turn(i + 1, i)
            turn(None, PASSES - 1)

        def tile_cols(t, n=P):
            return slice(t * n, t * n + n)

        block = ctx.enter_context(nc.Block())

        @block.sync
        def _(sp):
            x_v = x.rearrange("b (n p) d -> p (b n) d", p=P)
            start_from_base(sp, y_sent)
            out_v = out.rearrange("b (n p) d -> p (b n) d", p=P)

            def load_x(j, it):
                sp.dma_start(xin[j][:, :, :], x_v[:, bass.ds(it * 2 * TP + j * TP, TP), :]).then_inc(x_in[1][j], 16)

            vecs = [
                (RC, B, c),
                (RB1, E * HC, b1.rearrange("e (c p) -> (e c) p", p=P)),
                (RB2, E, b2),
                (RCB, CT, conv_b.rearrange("(c p) -> c p", p=P)),
                (RNW, 1, norm_w.rearrange("(o p) -> o p", o=1)),
                (RG, 1, norm_gamma.rearrange("(o p) -> o p", o=1)),
                (RSG, 1, slot_norm_gamma.rearrange("(o p) -> o p", o=1)),
            ]
            for r0, n, src in vecs:
                sp.dma_start(vec_nat[r0:r0 + n, :], src).then_inc(s_vec, 16)
            for j in range(2):
                load_x(j, 0)

            def load_mods(j, it):
                for bi in range(BP):
                    sp.dma_start(mods_bc[j][:, bi, :, :].rearrange("p m d -> p (m d)"),
                                 mod_dram[bass.ds(it * 2 * BP + (j * BP + bi), 1), 0:5 * P].broadcast_to((P, 5 * P))
                                 ).then_inc(mods_in[1][j], 16)

            sp.wait_ge(s_ready, 1)
            sp.dma_start(mod_dram, mod_rows[:, :, :].rearrange("b m d -> b (m d)")).then_inc(s_mod, 16)
            sp.wait_ge(s_mod, 16)
            for j in range(2):
                load_mods(j, 0)

            def next_x(j, it):
                if isinstance(it, int) and it == 0:
                    return
                wait_before(sp, basis_done, j, it)
                hold(sp)
                load_x(j, it)

            def next_mods(j, it):
                if isinstance(it, int) and it == 0:
                    return
                wait_before(sp, h_done, j, it)
                hold(sp)
                load_mods(j, it)

            def send_parts(j, it):
                wait(sp, ksm_done, j, it)
                hold(sp)
                wait_before(sp, y_ps, j, it)
                hold(sp)
                for r in range(3):
                    sp.dma_start(
                        rsm[j][r:r + 1, :, :],
                        ksm[j][PART_ROW + H * r:PART_ROW + H * (r + 1), :],
                    ).then_inc(rsm_in[1][j], 16)

            pipeline(sp, [(84.34, next_x), (167.26, next_mods), (364.88, send_parts)])

            def load_w(j, it):
                sp.dma_start(w1_sb[j][:, :], w1[bass.ds(it * 2 + j, 1), :, :].rearrange("o d h -> d (o h)")
                             ).then_inc(w1_in[1][j], 16)
                sp.dma_start(w2_sb[j][:, :, :],
                             w2[bass.ds(it * 2 + j, 1), :, :].rearrange("o (c p) d -> p (o c) d", p=P)
                             ).then_inc(w2_in[1][j], 16)

            for j in range(2):
                load_w(j, 0)
            with sp.Fori(0, E // 2 - 1) as it:
                for j in range(2):
                    wait(sp, hid_ps, j, it)
                    hold(sp)
                    wait(sp, eoT_ps, j, it)
                    hold(sp)
                    load_w(j, it + 1)
            with sp.Fori(0, B // 2) as it:
                for j in range(2):
                    wait(sp, y_out, j, it)
                    hold(sp)
                    sp.dma_start(out_v[:, bass.ds((it * 2 + j) * NT, NT), :],
                                 yout[j][:, 0:NT, :]).then_inc(y_sent[1][j], 16)
            for j in range(2):
                wait(sp, y_sent, j, B // 2 - 1)
                hold(sp)

        @block.gpsimd
        def _(pool):
            nc.gpsimd.memset(ones_sq[:, :], 1.0).then_inc(s_pool, 1)
            pool.wait_ge(s_pool, 1)
            nc.gpsimd.affine_select(out=ident[:, :], in_=ones_sq[:, :], compare_op=ALU.is_equal, fill=0.0, base=0,
                                    pattern=[[1, P]], channel_multiplier=-1).then_inc(s_pool, 1)
            nc.gpsimd.affine_select(out=causal[:, :], in_=ones_sq[:, :], compare_op=ALU.is_ge, fill=0.0, base=0,
                                    pattern=[[1, P]], channel_multiplier=-1).then_inc(s_pool, 1)
            nc.gpsimd.memset(neg_half[:, :], -0.5).then_inc(s_pool, 1)
            nc.gpsimd.memset(neg_shift[:, :], -SHIFT).then_inc(s_pool, 1)
            nc.gpsimd.memset(future[:, :], 0.0).then_inc(s_pool, 1)
            for j in range(2):
                nc.gpsimd.memset(Q[j][:, :, 0:3], -1.0).then_inc(s_pool, 1)
                nc.gpsimd.memset(Q[j][:, :, 3:P], 0.0).then_inc(s_pool, 1)
                nc.gpsimd.memset(xn2tok[j][:, :, P:P + 1], 1.0).then_inc(s_pool, 1)
            pool.wait_ge(s_pool, 12)
            nc.gpsimd.tensor_copy(ident_b[:, :], ident[:, :]).then_inc(s_pool, 1)
            nc.gpsimd.tensor_single_scalar(ident_shift[:, :], ident[:, :], 1.0 / SHIFT, ALU.mult).then_inc(s_pool, 1)
            nc.gpsimd.affine_select(out=future[:, :], in_=future[:, :], compare_op=ALU.is_ge, fill=-1e30, base=0,
                                    pattern=[[1, P]], channel_multiplier=-1).then_inc(s_pool, 1)
            nc.gpsimd.tensor_tensor(blk[:, 0, :], ident[:, PART_ROW:PART_ROW + H],
                                    ident[:, PART_ROW + H:PART_ROW + 2 * H], ALU.add).then_inc(s_pool, 1)
            pool.wait_ge(s_pool, 16)
            nc.gpsimd.tensor_tensor(blk[:, 1, :], blk[:, 0, :],
                                    ident[:, PART_ROW + 2 * H:PART_ROW + 3 * H], ALU.add).then_inc(s_pool, 1)
            pool.wait_ge(s_act0, ACT_SE)
            nc.gpsimd.tensor_scalar(se_r[:, :], se_ss[:, :], NORM_FLOOR ** 2 / DM, None, ALU.max).then_inc(s_pool, 1)
            pool.wait_ge(s_pool, POOL_ALL + 1)
            nc.gpsimd.tensor_tensor(se_r[:, :], se_r[:, :], neg_half[:, 0:MT], ALU.pow).then_inc(s_pool, 1)
            pool.wait_ge(s_ready, 3)
            nc.gpsimd.memset(eo[:, :, :, P:P + 1], 1.0).then_inc(s_eo_ones, 1)

            def inverse_root(kind, n, src):
                def visit(j, it):
                    if kind == 0:
                        wait(pool, var_done, j, it, n // 2 + 1)
                    else:
                        wait(pool, ms_done, j, it, n // 2 + 1)
                    hold(pool)
                    nc.gpsimd.tensor_scalar(root[j][:, :], src(j), (LN_EPS, RMS_EPS, NORM_FLOOR ** 2 / DM)[kind], None,
                                            ALU.max if kind == 2 else ALU.add).then_inc(pool_own[1][j], 1)
                    wait(pool, pool_own, j, it, n + 1 + (n >= 2))
                    nc.gpsimd.tensor_tensor(root[j][:, :], root[j][:, :], neg_half[:, :], ALU.pow
                                            ).then_inc(root_done[1][j], 1)
                return visit

            def add_basis(j, it):
                wait(pool, h_done, j, it, 1)
                for bi in range(BP):
                    t = slice(bi * NT, (bi + 1) * NT)
                    q = nc.gpsimd.tensor_tensor(basis[j][:, t, :], hh[j][:, t, :],
                                                mods_bc[j][:, bi, 2, :].unsqueeze(1).broadcast_to((P, NT, P)), ALU.mult)
                q.then_inc(pool_own[1][j], 1)
                wait(pool, pool_own, j, it, 3)
                nc.gpsimd.tensor_tensor(basis[j][:, :, :], basis[j][:, :, :], xin[j][:, :, :], ALU.add
                                        ).then_inc(basis_done[1][j], 1)

            start_from_base(pool, basis_done)
            variances = lambda j: mv[j][:, :, 1]
            mean_squares = lambda j: ms[j][:, :]
            pipeline(pool, [(113.76, inverse_root(0, 0, variances)),
                            (180.03, inverse_root(1, 1, mean_squares)), (228.84, add_basis),
                            (289.07, inverse_root(0, 2, variances)), (318.9, inverse_root(2, 3, mean_squares))])

        @block.tensor
        def _(pe):
            def mm(o, lhsT, rhs, start=True, stop=True):
                return nc.tensor.matmul(o, lhsT, rhs, start=start, stop=stop)

            start_from_base(pe, y_ps, eoT_ps, comb_out_ps)
            pe.sem_inc(eo_ps, 1)
            pe.wait_ge(s_pool, POOL_IDENT)
            pe.wait_ge(s_vec, N_VEC)
            nc.tensor.transpose(bank[0][:, 0:VR], vec_nat[:, :], ident[0:VR, 0:VR]).then_inc(s_pe0, 1)
            pe.wait_ge(s_wmod, 16)
            pe.wait_ge(s_dve0, DVE_CS)
            mm(bank[5][0:B, 0:3 * P], cs[:, :], wmod_sb[:, 0:3 * P])
            mm(bank[6][0:B, 0:3 * P], cs[:, :], wmod_sb[:, 3 * P:6 * P])
            mm(bank[7][:, 0:B], wmod_sb[:, tile_cols(5)], cs[:, :]).then_inc(s_pe0, 1)
            pe.wait_ge(s_w, N_W)
            for n in range(ROW_BLOCKS):
                q = nc.tensor.transpose(bank[1 + n // 4][:, tile_cols(n % 4)], w_nat[:, n, :], ident[:, :])
            q = nc.tensor.transpose(bank[3][:, 0:H], dt_nat[:, :], ident[0:H, 0:H])
            for k in range(CT):
                q = nc.tensor.transpose(bank[3][:, tile_cols(1 + k)], wo_nat[:, tile_cols(k)], ident[:, :])
            q.then_inc(s_pe0, 1)
            pe.wait_ge(s_ready, 2)
            for m in range(MT):
                q = nc.tensor.transpose(bank[4][:, tile_cols(m)], se_nat[:, m, :], ident[:, :])
            q.then_inc(s_pe0, 1)
            pe.wait_ge(s_pool, POOL_ALL)
            pe.wait_ge(s_ready, 3)

            def t_xn(layer):
                def visit(j, it):
                    wait(pe, xn_done, j, it, layer + 1)
                    if layer == 0:
                        wait_before(pe, comb_done, j, it)
                        o, src = bank[4 * j + 3], xntok[j]
                    else:
                        o, src = bank[4 * j], xn2tok[j]
                    for t in range(TP):
                        q = nc.tensor.transpose(o[:, tile_cols(t)], src[:, t, 0:P], ident[:, :])
                    q.then_inc(xnT_ps[1][j], 1)
                return visit

            def project1(j, it):
                b0, b1, b2, b3 = bank[4 * j:4 * j + 4]
                wait(pe, xnT_done, j, it, 1)
                for t in range(TP):
                    q = mm(b3[:, t * H:(t + 1) * H], xnT[j][:, tile_cols(t)], winT[:, DT0:ROWS])
                q.then_inc(dt_ps[1][j], 1)
                wait_before(pe, slots_done, j, it)
                mm(b0[:, :], winT[:, X0:X0 + P], xnT[j][:, :]).then_inc(x_ps[1][j], 1)
                mm(b1[:, :], winT[:, X0 + P:X0 + 2 * P], xnT[j][:, :]).then_inc(x_ps[1][j], 1)
                wait_before(pe, slotsT_done, j, it)
                mm(b2[:, :], winT[:, B0:B0 + P], xnT[j][:, :]).then_inc(bc_ps[1][j], 1)

            def project2(j, it):
                wait(pe, v_done, j, it)
                mm(bank[4 * j + 3][:, :], winT[:, C0:C0 + P], xnT[j][:, :]).then_inc(bc_ps[1][j], 1)
                wait(pe, bc_done, j, it, 1)
                mm(bank[4 * j + 2][:, :], winT[:, Z0:Z0 + P], xnT[j][:, :]).then_inc(z_ps[1][j], 1)

            def project3(j, it):
                wait(pe, bc_done, j, it, 2)
                mm(bank[4 * j + 3][:, :], winT[:, Z0 + P:Z0 + 2 * P], xnT[j][:, :]).then_inc(z_ps[1][j], 1)

            def scores(j, it):
                for bi in range(BP):
                    wait(pe, conv_done, j, it, bi + 1)
                    o = bank[4 * j + bi]
                    t0 = bi * L
                    mm(o[:, 0:L], BT[j][:, t0:t0 + P], CTr[j][:, t0:t0 + L])
                    mm(o[:, L:L + P], BT[j][:, t0 + P:t0 + L], CTr[j][:, t0 + P:t0 + L]).then_inc(g_ps[1][j], 1)

            def running_sums(j, it):
                wait(pe, w_done, j, it)
                wait(pe, zs_done, j, it, 1)
                o = bank[4 * j + 2]
                mm(o[:, 0:TP * H], causal[:, :], dv[j][:, WD, :], stop=False)
                w4 = dv[j][:, WD, :].rearrange("p (b n h) -> p b n h", b=BP, n=NT)
                o4 = o[:, 0:TP * H].rearrange("p (b n h) -> p b n h", b=BP, n=NT)
                mm(o4[:, :, 1, :], ones_sq[:, :], w4[:, :, 0, :], start=False).then_inc(cum_ps[1][j], 1)

            def part_rows(j, it):
                wait(pe, parts_done, j, it)
                o = bank[4 * j + 2][:, :].bitcast(bf16)
                for t in range(TP):
                    q = nc.tensor.transpose(o[:, tile_cols(t)], Q[j][:, t, :], ident_b[:, :])
                q.then_inc(parts_ps[1][j], 1)

            def t_xh(j, it):
                for bi in range(BP):
                    wait(pe, g_done, j, it, bi + 1)
                    wait(pe, xh_done, j, it, 2)
                    for n in range(NT):
                        for k in range(CT):
                            t = bi * NT + n
                            q = nc.tensor.transpose(bank[4 * j + bi][:, tile_cols(n * CT + k)],
                                                    xhT[j][:, k, tile_cols(t)], ident[:, :])
                    q.then_inc(xht_ps[1][j], 1)

            def segment(f):
                def visit(j, it):
                    bi, g = divmod(f, 3)
                    o = bank[4 * j + 2 + f % 2]
                    if f == 0:
                        wait(pe, ksm_done, j, it)
                        wait(pe, rsm_in, j, it)
                    if f == 1:
                        wait(pe, zs_done, j, it, 2)
                    if f >= 2:
                        wait(pe, seg_done, j, it, f - 1)
                    if g < 2:
                        mm(o[:, :], ksm[j][:, bi * L:bi * L + P],
                           rsm[j][:, 2 * g:2 * g + 2, bi * L:(bi + 1) * L], stop=False)
                        mm(o[:, :].rearrange("p (h t) -> p h t", h=2)[:, :, 0:P], ident_b[:, :],
                           future[:, :].unsqueeze(1).broadcast_to((P, 2, P)), start=False).then_inc(seg_ps[1][j], 1)
                    else:
                        mm(o[:, :], ksm[j][:, bi * L + P:bi * L + L],
                           rsm[j][:, :, bi * L + P:(bi + 1) * L], stop=False)
                        mm(o[:, :].rearrange("p (h t) -> p h t", h=H), ident_b[:, :],
                           future[:, :].unsqueeze(1).broadcast_to((P, H, P)), start=False).then_inc(seg_ps[1][j], 1)
                return visit

            def y_of(bi):
                def visit(j, it):
                    wait(pe, dtx_done, j, it, 2)
                    wait(pe, m_done, j, it, 3 * bi + 3)
                    for h in range(H):
                        o = bank[4 * j + h // 2][(h % 2) * HD:(h % 2 + 1) * HD, bi * L:(bi + 1) * L]
                        mm(o, dtx[j][:, bi * NT, h * HD:(h + 1) * HD],
                           seg_m[j][:, h // 2, (h % 2) * L:(h % 2 + 1) * L], stop=False)
                        q = mm(o[:, P:L], dtx[j][:, bi * NT + 1, h * HD:(h + 1) * HD],
                               seg_m[j][:, 2, tile_cols(h)], start=False)
                    q.then_inc(y_ps[1][j], 1)
                return visit

            def project_out(j, it):
                wait(pe, yg_done, j, it)
                wait(pe, seg_done, j, it, 6)
                for t in range(TP):
                    for k in range(CT):
                        q = mm(bank[4 * j + 2][:, tile_cols(t)], xhT[j][:, k, tile_cols(t)], woT[:, k, :],
                               start=k == 0, stop=k == CT - 1)
                q.then_inc(o_ps[1][j], 1)

            def logits(bi):
                def visit(j, it):
                    wait(pe, xnT_done, j, it, 2)
                    if bi:
                        wait(pe, slots_done, j, it, bi)
                    for n in range(NT):
                        mm(bank[4 * j + n][:, :], xn2T[j][:, tile_cols(bi * NT + n)],
                           snT[:, :]).then_inc(lt_ps[1][j], 1)
                return visit

            def t_logits(bi):
                def visit(j, it):
                    if bi:
                        wait(pe, slotsT_done, j, it, bi)
                    wait(pe, lt_done, j, it, 2 * bi + 2)
                    for m in range(MT):
                        o = bank[4 * j + 2 + m // 2]
                        for n in range(NT):
                            at = (m % 2) * L + n * P
                            q = nc.tensor.matmul(o[:, at:at + P], lt_sb[j][:, n, tile_cols(m)], ident[:, :],
                                                 is_transpose=True, start=at == 0, stop=at == 512 - P,
                                                 skip_group_check=True)
                        if m % 2:
                            q.then_inc(ls_ps[1][j], 1)
                return visit

            def shifts(bi):
                def visit(j, it):
                    wait(pe, diag_r_done, j, it, bi + 1)
                    wait(pe, diag_c_done, j, it, bi + 1)
                    for n in range(NT):
                        nc.tensor.matmul(bank[4 * j + n][:, :], neg_shift[:, :], diag_c[j][:, :, :],
                                         start=False, stop=True, skip_group_check=True
                                         ).then_inc(disp_ps[1][j], 1)
                    for m2 in range(2):
                        nc.tensor.matmul(bank[4 * j + 2 + m2][:, :], neg_shift[:, :],
                                         diag_r[j][:, :, :].rearrange("p n t -> p (n t)").unsqueeze(1).broadcast_to((P, 2, L)),
                                         start=False, stop=True, skip_group_check=True
                                         ).then_inc(comb_ps[1][j], 1)
                return visit

            def fill_slots(bi):
                def visit(j, it):
                    wait(pe, disp_done, j, it, 2 * bi + 2)
                    for m in range(MT):
                        o = bank[4 * j + m // 2][:, (m % 2) * (P + 1):(m % 2 + 1) * (P + 1)]
                        for n in range(NT):
                            q = mm(o, e_disp[j][:, n, tile_cols(m)], xn2tok[j][:, bi * NT + n, :],
                                   start=n == 0, stop=n == NT - 1)
                        if m % 2:
                            q.then_inc(slots_ps[1][j], 1)
                return visit

            def t_slots(bi):
                def visit(j, it):
                    wait(pe, slots_done, j, it, bi + 1)
                    wait(pe, comb_done, j, it, 2 * bi + 2)
                    for m in range(MT):
                        q = nc.tensor.transpose(bank[4 * j + 2][:, tile_cols(m)], slots[j][:, m, :], ident[:, :])
                    q.then_inc(slotsT_ps[1][j], 1)
                return visit

            visits = [(-1.71, t_xn(0)), (27.9, project1), (56.4, project2), (60.99, project3), (62.38, scores),
                      (62.4, running_sums), (80.03, part_rows), (80.05, t_xh), (99.54, segment(0)),
                      (99.56, segment(1)), (99.58, segment(2)), (99.95, segment(3)), (104.22, y_of(0)),
                      (106.64, segment(4)), (108.55, segment(5)), (119.38, y_of(1)), (124.32, project_out),
                      (147.76, t_xn(1)), (149.41, logits(0)), (152.31, t_logits(0)), (173.97, shifts(0)),
                      (176.28, fill_slots(0)), (179.5, t_slots(0)), (183.21, logits(1)), (206.77, t_logits(1)),
                      (217.23, shifts(1)), (221.51, fill_slots(1)), (251.71, t_slots(1))]
            pipeline(pe, visits)

            for j in range(2):
                wait(pe, slotsT_done, j, PASSES - 1)
            def hidden(it):
                for j in range(2):
                    wait(pe, w1_in, j, it)
                    for k in range(HC):
                        if j == 0:
                            wait_before(pe, gelu_done, 1, it)
                        else:
                            wait(pe, gelu_done, 0, it, k + 1)
                        mm(bank[k][:, :], w1_sb[j][:, tile_cols(k)],
                           slotsT[:, bass.ds(it * 2 + j, 1), :, :].rearrange("p e b s -> p (e b s)")
                           ).then_inc(hid_ps[1][j], 1)

            def outputs(it):
                for j in range(2):
                    wait(pe, w2_in, j, it)
                    wait(pe, gelu_done, j, it)
                    wait_before(pe, eoT_done, j, it)
                    for k in range(HC):
                        q = mm(bank[4 + j][:, :], w2_sb[j][:, k, :], act_h[j][k // 2][:, k % 2, :],
                               start=k == 0, stop=k == HC - 1)
                    q.then_inc(eoT_ps[1][j], 1)

            def t_outputs(it):
                for j in range(2):
                    wait(pe, eoT_done, j, it)
                pe.wait_ge(eo_done, it * 2 + 1)
                for b in range(B):
                    q = nc.tensor.transpose(bank[6 + b // 4][:, tile_cols(b % 4)],
                                            eoT[:, b, :, :].rearrange("p e s -> p (e s)"), ident[:, :])
                    if b % 4 == 3:
                        q.then_inc(eo_ps, 1)

            hidden(0)
            outputs(0)
            with pe.Fori(0, E // 2 - 1) as it:
                hidden(it + 1)
                t_outputs(it)
                outputs(it + 1)
            t_outputs(E // 2 - 1)
            pe.wait_ge(eo_done, E + 1)
            pe.wait_ge(s_eo_ones, 1)
            with pe.Fori(0, B // 2) as it:
                for j in range(2):
                    wait(pe, cb_done, j, it)
                    wait_before(pe, y_out, j, it)
                    for n in range(NT):
                        for m in range(MT):
                            q = mm(bank[2 * j + n][:, 0:P + 1], cbuf[j][:, m // 2, (m % 2) * L + n * P:(m % 2) * L + n * P + P],
                                   eo[:, bass.ds(it * 2 + j, 1), m, :].rearrange("p b d -> p (b d)"),
                                   start=m == 0, stop=m == MT - 1)
                        q.then_inc(comb_out_ps[1][j], 1)

        @block.scalar
        def _(act):
            A = nc.scalar.activation
            start_from_base(act, slotsT_done, comb_done, gelu_done)
            act.sem_inc(eo_done, 1)
            act.dma_start(wmod_sb[:, :], wmod).then_inc(s_wmod, 16)
            act.dma_start(se_nat[:, :, :],
                          slot_embeds.rearrange("(n a) s d -> (a s) n d", a=P // S)).then_inc(s_se, 16)
            act.dma_start(w_nat[:, :, :],
                          in_proj_w[0:ROW_BLOCKS * P, :].rearrange("(n p) d -> p n d", p=P)).then_inc(s_w, 16)
            act.dma_start(dt_nat[:, :], in_proj_w[DT0:ROWS, :]).then_inc(s_w, 16)
            act.dma_start(wo_nat[:, :], out_proj_w).then_inc(s_w, 16)
            nc.scalar.preload_act_table(ACT.Exp)
            act.wait_ge(s_dve0, DVE_VEC)
            A(cs_t[:, :], vecT[:, RC:RC + B], ACT.Tanh, scale=0.5).then_inc(s_act0, 1)
            act.dma_start(convw[:, :, :], conv_w.rearrange("(c p) k -> p c k", p=P)).then_inc(s_small, 16)
            act.dma_start(dtb_row[:, :],
                          dt_bias.rearrange("(o h) -> o h", o=1).broadcast_to((P, H))).then_inc(s_small, 16)
            act.dma_start(expA_row[:, :],
                          A_log.rearrange("(o h) -> o h", o=1).broadcast_to((P, H))).then_inc(s_small, 16)
            for h in range(H):
                act.dma_start(d_col[(h % 2) * HD:(h % 2 + 1) * HD, h // 2:h // 2 + 1],
                              D[h:h + 1].rearrange("(o h) -> o h", o=1).broadcast_to((HD, 1))).then_inc(s_small, 16)
            act.wait_ge(s_se, 16)
            for m in range(MT):
                A(se_sq[:, :], se_nat[:, m, :], ACT.Square, scale=float(DM) ** -0.5, accum_out=se_ss[:, m:m + 1]).then_inc(s_act0, 1)
                act.wait_ge(s_act0, ACT_TANH + m + 1)
            act.wait_ge(s_small, N_SMALL)
            A(expA_t[:, :], expA_row[:, :], ACT.Exp).then_inc(s_act0, 1)
            act.wait_ge(s_pool, POOL_ALL)
            for j in range(2):
                A(rsm[j][:, :, :], blk[:, 1, :].unsqueeze(2).broadcast_to((P, H, W)), ACT.Copy).then_inc(s_act0, 1)
            act.wait_ge(s_ready, 1)

            def mods(j, it, bi):
                return bass.ds(it * 2 * BP + j * BP + bi, 1)

            def mean_squares(layer):
                def visit(j, it):
                    wait(act, h_done, j, it, layer + 1)
                    unused = xn2tok[j] if layer else xntok[j]
                    for t in range(TP):
                        q = A(unused[:, t, 0:P], hh[j][:, t, :], ACT.Square, scale=float(DM) ** -0.5,
                              accum_out=ms[j][:, t:t + 1])
                    q.then_inc(ms_done[1][j], 1)
                return visit

            def copy_xnT(layer):
                def visit(j, it):
                    wait(act, xnT_ps, j, it, layer + 1)
                    dst, src = (xn2T[j], bank[4 * j]) if layer else (xnT[j], bank[4 * j + 3])
                    A(dst[:, :], src[:, :], ACT.Copy).then_inc(xnT_done[1][j], 1)
                return visit

            def first_tap(j, it):
                for k in range(CT):
                    wait(act, x_ps, j, it, k + 1)
                    A(xcT[j][:, k, :], bank[4 * j + k][:, :], ACT.Identity, bias=vecT[:, RCB + k:RCB + k + 1],
                      scale=convw[:, k, TAPS - 1:TAPS]).then_inc(tap0_done[1][j], 1)
                wait(act, bc_ps, j, it, 1)
                A(BT[j][:, :], bank[4 * j + 2][:, :], ACT.Copy).then_inc(bc_done[1][j], 1)

            def exp_dt(j, it):
                wait(act, nabs_done, j, it)
                A(dv[j][:, EDT, :], dv[j][:, NABS, :], ACT.Exp).then_inc(edt_done[1][j], 1)

            def copy_c(j, it):
                wait(act, bc_ps, j, it, 2)
                A(CTr[j][:, :], bank[4 * j + 3][:, :], ACT.Copy).then_inc(bc_done[1][j], 1)

            def tanh_xz(k):
                def visit(j, it):
                    wait(act, z_ps, j, it, k + 1)
                    A(zsT[j][:, k, :], bank[4 * j + 2 + k][:, :], ACT.Tanh, scale=0.5).then_inc(zt_done[1][j], 1)
                    wait(act, conv_done, j, it, k + 1)
                    A(xhT[j][:, k, :], xcT[j][:, k, :], ACT.Tanh, scale=0.5).then_inc(xt_done[1][j], 1)
                return visit

            def copy_scores(j, it):
                for bi in range(BP):
                    wait(act, g_ps, j, it, bi + 1)
                    A(gm[j][:, bi, :, :].rearrange("p n t -> p (n t)"), bank[4 * j + bi][:, 0:3 * P], ACT.Copy
                      ).then_inc(g_done[1][j], 1)

            def copy_parts(j, it):
                wait(act, parts_ps, j, it)
                A(ksm[j][:, :], bank[4 * j + 2][:, :].bitcast(bf16)[:, 0:W], ACT.Copy).then_inc(ksm_done[1][j], 1)

            def decay(f):
                def visit(j, it):
                    wait(act, seg_ps, j, it, f + 1)
                    if f >= 3:
                        wait(act, m_done, j, it, f - 2)
                    A(seg_e[j][:, f % 3, :], bank[4 * j + 2 + f % 2][:, :], ACT.Exp).then_inc(seg_done[1][j], 1)
                return visit

            def copy_logits(bi):
                def visit(j, it):
                    for n in range(NT):
                        wait(act, lt_ps, j, it, 2 * bi + n + 1)
                        A(lt_sb[j][:, n, :], bank[4 * j + n][:, :], ACT.Copy).then_inc(lt_done[1][j], 1)
                return visit

            def exps(bi):
                def visit(j, it):
                    for n in range(NT):
                        wait(act, disp_ps, j, it, 2 * bi + n + 1)
                        A(e_disp[j][:, n, :], bank[4 * j + n][:, :], ACT.Exp).then_inc(disp_done[1][j], 1)
                    for m2 in range(2):
                        wait(act, comb_ps, j, it, 2 * bi + m2 + 1)
                        A(combT[:, mods(j, it, bi), 2 * m2:2 * m2 + 2, :].rearrange("p b m t -> p (b m t)"),
                          bank[4 * j + 2 + m2][:, :], ACT.Exp).then_inc(comb_done[1][j], 1)
                return visit

            def copy_slotsT(bi):
                def visit(j, it):
                    wait(act, slotsT_ps, j, it, bi + 1)
                    A(slotsT[:, :, mods(j, it, bi), :].rearrange("p e b s -> p e (b s)"),
                      bank[4 * j + 2][:, :].rearrange("p (e s) -> p e s", e=E),
                      ACT.Identity, scale=vecT[:, RG:RG + 1]).then_inc(slotsT_done[1][j], 1)
                return visit

            visits = [(7.98, mean_squares(0)), (39.02, copy_xnT(0)), (63.4, first_tap), (64.74, exp_dt),
                      (72.61, copy_c), (86.5, tanh_xz(0)), (98.84, tanh_xz(1)), (98.86, copy_scores),
                      (119.38, copy_parts), (134, decay(0)), (138.05, decay(1)), (138.07, decay(2)),
                      (143.43, decay(3)), (171.22, decay(4)), (175.45, decay(5)), (182.6, mean_squares(1)),
                      (196.45, copy_xnT(1)), (198.07, copy_logits(0)), (214.95, exps(0)),
                      (230.28, copy_slotsT(0)), (234.33, copy_logits(1)), (249.68, exps(1)),
                      (285.08, copy_slotsT(1))]
            pipeline(act, visits)

            def copy_comb(j, it):
                A(cbuf[j][:, :, :].rearrange("p a b -> p (a b)"),
                  combT[:, bass.ds(it * 2 + j, 1), :, :].rearrange("p b m t -> p (b m t)"), ACT.Copy
                  ).then_inc(cb_done[1][j], 1)

            def gelus(it):
                for j in range(2):
                    for k in range(HC):
                        wait(act, hid_ps, j, it, k + 1)
                        wait_before(act, eoT_ps, j, it)
                        A(act_h[j][k // 2][:, k % 2, :], bank[k][:, :], ACT.Gelu,
                          bias=vecT[:, bass.ds(it * 2 * HC + (RB1 + j * HC + k), 1)]).then_inc(gelu_done[1][j], 1)

            def copy_eo(it):
                for g in range(2):
                    act.wait_ge(eo_ps, it * 2 + (g + 2))
                    A(eo[:, 4 * g:4 * g + 4, bass.ds(it, 1), 0:P].rearrange("p b m d -> p b (m d)"),
                      bank[6 + g][:, :].rearrange("p (b d) -> p b d", b=4), ACT.Copy).then_inc(eo_done, 1)

            gelus(0)
            for j in range(2):
                copy_comb(j, 0)
            with act.Fori(0, E // 2 - 1) as it:
                gelus(it + 1)
                copy_eo(it)
            copy_eo(E // 2 - 1)
            with act.Fori(0, B // 2 - 1) as it:
                for j in range(2):
                    wait(act, comb_out_ps, j, it)
                    copy_comb(j, it + 1)

        @block.vector
        def _(dve):
            V = nc.vector
            start_from_base(dve, slots_done, h_done, eoT_done, y_out)
            n0 = [0]

            def step0(q):
                n0[0] += 1
                q.then_inc(s_dve0, 1)
                dve.wait_ge(s_dve0, n0[0])

            dve.wait_ge(s_pe0, PE_VEC)
            step0(V.tensor_copy(vecT[:, :], bank[0][:, 0:VR]))
            assert n0[0] == DVE_VEC
            dve.wait_ge(s_act0, ACT_TANH)
            step0(V.scalar_tensor_tensor(cs[:, :], cs_t[:, :], 1.0, vecT[:, RC:RC + B], ALU.add, ALU.mult))
            step0(V.tensor_scalar(cs[:, :], cs[:, :], 0.5, None, ALU.mult))
            assert n0[0] == DVE_CS
            done = [{own_norm1[0]: 0, own_rest[0]: 0} for _ in range(2)]

            def step(j, it, q, own=own_rest):
                name, sems = own
                done[j][name] = done[j][name] % per_pass[name] + 1
                q.then_inc(sems[j], 1)
                wait(dve, own, j, it, done[j][name])

            def x1_tile(j, it, t, n=1):
                return x1tok[:, bass.ds(it * 2 * TP + (j * TP + t), n), :]

            def layer_input(layer, j, it, t):
                if layer == 0:
                    return xin[j][:, t, :]
                return x1_tile(j, it, t).rearrange("p t d -> p (t d)")

            def statistics(layer, first=False):
                def visit(j, it):
                    if layer == 0 and not first and isinstance(it, int) and it == 0:
                        return
                    if layer == 0:
                        wait(dve, x_in, j, it)
                    hold(dve)
                    for t in range(TP):
                        q = V.bn_stats(bst[j][:, t, :], layer_input(layer, j, it, t))
                    step(j, it, q, (own_norm1, own_rest)[layer])
                    hold(dve)
                    for t in range(TP):
                        q = V.bn_aggr(mv[j][:, t, :], bst[j][:, t, :])
                    q.then_inc(var_done[1][j], 1)
                return visit

            for j in range(2):
                statistics(0, first=True)(j, 0)
            dve.wait_ge(s_pe0, PE_MOD)
            for g in range(2):
                q = V.tensor_copy(mod_rows[:, 3 * g:3 * g + 3, :],
                                  bank[5 + g][0:B, 0:3 * P].rearrange("b (m d) -> b m d", m=3))
            step0(q)
            for m in (1, 4):
                V.tensor_scalar(mod_rows[:, m, :], mod_rows[:, m, :], 1.0, None, ALU.add)
            step0(V.tensor_copy(gbT[:, :], bank[7][:, 0:B]))

            def gate_of(g, sg):
                step0(V.tensor_scalar(sg, g, 0.0, 2.0, ALU.is_ge, ALU.mult))
                V.tensor_scalar(sg, sg, 1.0, None, ALU.subtract)
                step0(V.scalar_tensor_tensor(g, g, -1.0, g, ALU.mult, ALU.max))
                step0(V.tensor_scalar(g, g, 0.25, None, ALU.max))
                step0(V.tensor_tensor(g, g, sg, ALU.mult))

            gate_of(mod_rows[:, 2, :], sgn_r[:, :])
            dve.sem_inc(s_ready, 1)
            gate_of(gbT[:, :], sgn_T[:, :])
            dve.wait_ge(s_pool, POOL_SE)
            for m in range(MT):
                q = V.tensor_scalar(se_nat[:, m, :], se_nat[:, m, :], se_r[:, m:m + 1], None, ALU.mult)
            step0(q)
            dve.sem_inc(s_ready, 1)
            dve.wait_ge(s_pe0, PE_W)
            V.tensor_scalar(winT[:, 0:512], bank[1][:, :], vecT[:, RNW:RNW + 1], None, ALU.mult)
            V.tensor_scalar(winT[:, 512:DT0], bank[2][:, 0:DT0 - 512], vecT[:, RNW:RNW + 1], None, ALU.mult)
            V.tensor_scalar(winT[:, DT0:ROWS], bank[3][:, 0:H], vecT[:, RNW:RNW + 1], None, ALU.mult)
            V.tensor_scalar(woT[:, :, :], bank[3][:, P:P + CT * P].rearrange("p (k d) -> p k d", k=CT),
                            0.5, None, ALU.mult)
            dve.wait_ge(s_small, N_SMALL)
            V.tensor_scalar(d_half[:, :], d_col[:, :], 0.5, None, ALU.mult)
            step0(V.tensor_tensor(g_all[:, :], vecT[:, RG:RG + 1], vecT[:, RSG:RSG + 1], ALU.mult))
            dve.wait_ge(s_pe0, PE_SE)
            step0(V.tensor_scalar(snT[:, :], bank[4][:, :], g_all[:, :], None, ALU.mult))
            dve.sem_inc(s_ready, 1)

            def modulate(layer):
                def visit(j, it):
                    wait(dve, root_done, j, it, 2 * layer + 1)
                    for t in range(TP):
                        q = V.tensor_scalar(hh[j][:, t, :], layer_input(layer, j, it, t), mv[j][:, t, 0:1],
                                            root[j][:, t:t + 1], ALU.subtract, ALU.mult)
                    step(j, it, q, (own_norm1, own_rest)[layer])
                    wait(dve, mods_in, j, it)
                    for m, op in ((3 * layer + 1, ALU.mult), (3 * layer, ALU.add)):
                        for bi in range(BP):
                            v = hh[j][:, bi * NT:(bi + 1) * NT, :]
                            q = V.tensor_tensor(v, v, mods_bc[j][:, bi, m, :].unsqueeze(1).broadcast_to((P, NT, P)), op)
                        if op == ALU.mult:
                            step(j, it, q, (own_norm1, own_rest)[layer])
                    q.then_inc(h_done[1][j], 1)
                return visit

            def unit(layer):
                def visit(j, it):
                    wait(dve, root_done, j, it, 2 * layer + 2)
                    for t in range(TP):
                        q = V.tensor_scalar((xn2tok[j] if layer else xntok[j])[:, t, 0:P], hh[j][:, t, :], root[j][:, t:t + 1], None, ALU.mult)
                    q.then_inc(xn_done[1][j], 1)
                return visit

            def dt_in(j, it):
                wait(dve, dt_ps, j, it)
                d = dv[j]
                V.tensor_tensor(d[:, VV, :].rearrange("p (t h) -> p t h", h=H),
                                bank[4 * j + 3][:, 0:TP * H].rearrange("p (t h) -> p t h", h=H),
                                dtb_row[:, :].unsqueeze(1).broadcast_to((P, TP, H)), ALU.add
                                ).then_inc(v_done[1][j], 1)
                wait(dve, v_done, j, it)
                V.scalar_tensor_tensor(d[:, NABS, :], d[:, VV, :], -1.0, d[:, VV, :], ALU.mult, ALU.min
                                       ).then_inc(nabs_done[1][j], 1)

            def softplus(j, it):
                wait(dve, edt_done, j, it)
                d = dv[j]
                step(j, it, V.tensor_scalar(d[:, U, :], d[:, EDT, :], 2.0, None, ALU.add))
                step(j, it, V.reciprocal(d[:, U, :], d[:, U, :]))
                step(j, it, V.tensor_tensor(d[:, U, :], d[:, U, :], d[:, EDT, :], ALU.mult))
                step(j, it, V.tensor_tensor(d[:, U2, :], d[:, U, :], d[:, U, :], ALU.mult))
                step(j, it, V.tensor_scalar(d[:, PP, :], d[:, U2, :], ATANH_TERMS[0], None, ALU.mult))
                for term in ATANH_TERMS[1:]:
                    step(j, it, V.scalar_tensor_tensor(d[:, PP, :], d[:, PP, :], term, d[:, U2, :], ALU.add, ALU.mult))
                step(j, it, V.scalar_tensor_tensor(d[:, PP, :], d[:, PP, :], 1.0, d[:, U, :], ALU.add, ALU.mult))
                step(j, it, V.tensor_scalar(d[:, VV, :], d[:, VV, :], 0.0, 0.5, ALU.max, ALU.mult))
                step(j, it, V.tensor_tensor(d[:, DTH, :], d[:, PP, :], d[:, VV, :], ALU.add))
                V.scalar_tensor_tensor(d[:, WD, :].rearrange("p (t h) -> p t h", h=H),
                                       d[:, DTH, :].rearrange("p (t h) -> p t h", h=H), 2.0,
                                       expA_t[:, :].unsqueeze(1).broadcast_to((P, TP, H)), ALU.mult, ALU.mult
                                       ).then_inc(w_done[1][j], 1)

            def conv(k):
                def visit(j, it):
                    wait(dve, tap0_done, j, it, k + 1)
                    acc = xcT[j][:, k, :].rearrange("p (b t) -> p b t", b=BP)
                    src = bank[4 * j + k][:, :].rearrange("p (b t) -> p b t", b=BP)
                    for back in range(1, TAPS):
                        q = V.scalar_tensor_tensor(acc[:, :, back:L], src[:, :, 0:L - back],
                                                   convw[:, k, TAPS - 1 - back:TAPS - back],
                                                   acc[:, :, back:L], ALU.mult, ALU.add)
                        if back < TAPS - 1:
                            step(j, it, q)
                    q.then_inc(conv_done[1][j], 1)
                return visit

            def silus(k):
                def visit(j, it):
                    wait(dve, zt_done, j, it, k + 1)
                    V.scalar_tensor_tensor(zsT[j][:, k, :], zsT[j][:, k, :], 1.0, bank[4 * j + 2 + k][:, :],
                                           ALU.add, ALU.mult).then_inc(zs_done[1][j], 1)
                    wait(dve, xt_done, j, it, k + 1)
                    V.scalar_tensor_tensor(xhT[j][:, k, :], xhT[j][:, k, :], 1.0, xcT[j][:, k, :],
                                           ALU.add, ALU.mult).then_inc(xh_done[1][j], 1)
                return visit

            def parts(j, it):
                wait(dve, cum_ps, j, it)
                cum = bank[4 * j + 2][:, 0:TP * H].rearrange("p (t h) -> p t h", h=H)
                r = dv[j][:, PP, :].rearrange("p (t h) -> p t h", h=H)

                def part(i):
                    return Q[j][:, :, PART_ROW + i * H:PART_ROW + (i + 1) * H]
                step(j, it, V.tensor_copy(part(0), cum))
                step(j, it, V.tensor_tensor(r, cum, part(0), ALU.subtract))
                step(j, it, V.tensor_copy(part(1), r))
                step(j, it, V.tensor_tensor(r, r, part(1), ALU.subtract))
                V.tensor_copy(part(2), r).then_inc(parts_done[1][j], 1)

            def dt_times_x(j, it):
                for bi in range(BP):
                    wait(dve, xht_ps, j, it, bi + 1)
                    V.tensor_tensor(
                        dtx[j][:, bi * NT:(bi + 1) * NT, :].rearrange("p t (h d) -> p (t h) d", h=H),
                        bank[4 * j + bi][:, :].rearrange("p (g d) -> p g d", d=HD),
                        dv[j][:, DTH, bi * NT * H:(bi + 1) * NT * H].unsqueeze(2).broadcast_to((P, NT * H, HD)),
                        ALU.mult).then_inc(dtx_done[1][j], 1)

            def weigh(f):
                def visit(j, it):
                    bi, g = divmod(f, 3)
                    wait(dve, seg_done, j, it, f + 1)
                    if f >= 3:
                        wait(dve, y_ps, j, it, 1)
                    if g < 2:
                        n, s = 2, gm[j][:, bi, 0:2, :].rearrange("p n t -> p (n t)")
                    else:
                        n, s = H, gm[j][:, bi, 2, :]
                    w = 512 // n
                    V.tensor_tensor(seg_m[j][:, g, :].rearrange("p (h t) -> p h t", h=n),
                                    seg_e[j][:, g, :].rearrange("p (h t) -> p h t", h=n),
                                    s.unsqueeze(1).broadcast_to((P, n, w)), ALU.mult).then_inc(m_done[1][j], 1)
                return visit

            def gate(j, it):
                wait(dve, y_ps, j, it)
                for k in range(CT):
                    q = V.scalar_tensor_tensor(xhT[j][:, k, :], xhT[j][:, k, :], d_half[:, k:k + 1],
                                               bank[4 * j + k][:, :], ALU.mult, ALU.add)
                step(j, it, q)
                V.tensor_tensor(xhT[j][:, :, :], xhT[j][:, :, :], zsT[j][:, :, :], ALU.mult
                                ).then_inc(yg_done[1][j], 1)

            def x1(j, it):
                wait(dve, o_ps, j, it)
                wait(dve, basis_done, j, it)
                hold(dve)
                for bi in range(BP):
                    q = V.tensor_tensor(hh[j][:, bi * NT:(bi + 1) * NT, :],
                                        bank[4 * j + 2][:, bi * L:(bi + 1) * L].rearrange("p (t d) -> p t d", t=NT),
                                        mods_bc[j][:, bi, 2, :].unsqueeze(1).broadcast_to((P, NT, P)), ALU.mult)
                step(j, it, q)
                V.tensor_tensor(x1_tile(j, it, 0, TP), hh[j][:, :, :], basis[j][:, :, :], ALU.add
                                ).then_inc(x1_done[1][j], 1)
                wait(dve, x1_done, j, it)

            def token_max(bi):
                def visit(j, it):
                    wait(dve, lt_done, j, it, 2 * bi + 2)
                    step(j, it, V.reduce_max(rmax[j][:, :], lt_sb[j][:, :, :], AX.X))
                    V.tensor_tensor(diag_r[j][:, :, :], ident_shift[:, :].unsqueeze(1).broadcast_to((P, NT, P)),
                                    rmax[j][:, :].unsqueeze(2).broadcast_to((P, NT, P)), ALU.mult
                                    ).then_inc(diag_r_done[1][j], 1)
                return visit

            def slot_max(bi):
                def visit(j, it):
                    for m2 in range(2):
                        wait(dve, ls_ps, j, it, 2 * bi + m2 + 1)
                        q = V.reduce_max(cmax[j][:, 2 * m2:2 * m2 + 2],
                                         bank[4 * j + 2 + m2][:, :].rearrange("p (m t) -> p m t", m=2), AX.X)
                    step(j, it, q)
                    V.tensor_tensor(diag_c[j][:, :, :], ident_shift[:, :].unsqueeze(1).broadcast_to((P, MT, P)),
                                    cmax[j][:, :].unsqueeze(2).broadcast_to((P, MT, P)), ALU.mult
                                    ).then_inc(diag_c_done[1][j], 1)
                return visit

            def norm_slots(bi):
                def visit(j, it):
                    ps = [bank[4 * j + m2][:, 0:2 * (P + 1)].rearrange("p (m d) -> p m d", m=2) for m2 in range(2)]
                    for m2 in range(2):
                        wait(dve, slots_ps, j, it, 2 * bi + m2 + 1)
                        q = V.reciprocal(rcs[j][:, 2 * m2:2 * m2 + 2], ps[m2][:, :, P])
                    step(j, it, q)
                    for m2 in range(2):
                        q = V.tensor_tensor(slots[j][:, 2 * m2:2 * m2 + 2, :], ps[m2][:, :, 0:P],
                                            rcs[j][:, 2 * m2:2 * m2 + 2].unsqueeze(2).broadcast_to((P, 2, P)), ALU.mult)
                    q.then_inc(slots_done[1][j], 1)
                return visit

            visits = [(-1.67, statistics(0)), (27.67, modulate(0)), (67.23, unit(0)), (89.37, dt_in),
                      (91.27, conv(0)), (94.17, softplus), (97.83, conv(1)), (99.55, silus(0)),
                      (99.57, silus(1)), (99.68, parts), (114.63, dt_times_x), (117.57, weigh(0)),
                      (117.59, weigh(1)), (118.91, weigh(2)), (127.88, weigh(3)), (131.05, weigh(4)),
                      (131.35, weigh(5)), (136.25, gate), (194, x1), (194.02, statistics(1)),
                      (210.33, modulate(1)), (221.8, unit(1)), (238.19, token_max(0)), (238.64, slot_max(0)),
                      (254.62, norm_slots(0)), (276.82, token_max(1)), (276.84, slot_max(1)),
                      (297.78, norm_slots(1))]
            pipeline(dve, visits)

            with dve.Fori(0, E // 2) as it:
                for j in range(2):
                    wait(dve, eoT_ps, j, it)
                    dve.wait_ge(eo_ps, it * 2 + 1)
                    V.scalar_tensor_tensor(eoT[:, :, j, :], bank[4 + j][:, :].rearrange("p (b s) -> p b s", b=B),
                                           vecT[:, bass.ds(it * 2 + (RB2 + j), 1)],
                                           gbT[:, :].unsqueeze(2).broadcast_to((P, B, S)), ALU.add, ALU.mult
                                           ).then_inc(eoT_done[1][j], 1)
            with dve.Fori(0, B // 2) as it:
                for j in range(2):
                    wait_before(dve, y_sent, j, it)
                    for n in range(NT):
                        wait(dve, comb_out_ps, j, it, n + 1)
                        ps = bank[2 * j + n]
                        q = V.reciprocal(rden[j][:, n:n + 1], ps[:, P:P + 1])
                    q.then_inc(rden_done[1][j], 1)
                    wait(dve, rden_done, j, it)
                    for n in range(NT):
                        q = V.scalar_tensor_tensor(yout[j][:, n, :], bank[2 * j + n][:, 0:P], rden[j][:, n:n + 1],
                                                   x1tok[:, bass.ds(it * 2 * NT + (j * NT + n), 1), :]
                                                   .rearrange("p t d -> p (t d)"), ALU.mult, ALU.add)
                    q.then_inc(y_out[1][j], 1)


_INS = ["L0_attn_x", "L0_attn_norm_w", "L0_attn_in_proj_w", "L0_attn_conv_w", "L0_attn_conv_b", "L0_attn_A_log",
        "L0_attn_D", "L0_attn_dt_bias", "L0_attn_out_proj_w", "L0_ffn_norm_gamma", "L0_ffn_slot_norm_gamma",
        "L0_ffn_slot_embeds", "L0_ffn_w1", "L0_ffn_b1", "L0_ffn_w2", "L0_ffn_b2", "L0_c", "L0_wmod"]


def kernel(**inputs):
    import numpy as _np
    import concourse.bacc as _bacc
    from concourse import mybir as _mybir
    from concourse.bass_utils import run_bass_kernel_spmd as _run

    nc = _bacc.Bacc("TRN2", target_bir_lowering=False, num_devices=1)
    arrays, args = {}, []
    for name in _INS:
        a = _np.ascontiguousarray(inputs[name])
        arrays[f"in_{name}_dram"] = a
        args.append(nc.dram_tensor(f"in_{name}_dram", a.shape, _mybir.dt.from_np(a.dtype), kind="ExternalInput").ap())
    shape = inputs["L0_attn_x"].shape
    args.append(nc.dram_tensor("out_0_dram", shape, _mybir.dt.float32, kind="ExternalOutput").ap())
    bass_adaln_mamba_softmoe_kernel(nc, *args)
    r = _run(nc, [arrays], core_ids=[0])
    return r.results[0]["out_0_dram"]
```

```python
import concourse.bass as bass
from concourse import mybir
from contextlib import ExitStack


def bass_adaln_mamba_softmoe_kernel(
    nc: bass.Bass,
    x: bass.AP,
    norm_w: bass.AP,
    in_proj_w: bass.AP,
    conv_w: bass.AP,
    conv_b: bass.AP,
    A_log: bass.AP,
    D: bass.AP,
    dt_bias: bass.AP,
    out_proj_w: bass.AP,
    norm_gamma: bass.AP,
    slot_norm_gamma: bass.AP,
    slot_embeds: bass.AP,
    w1: bass.AP,
    b1: bass.AP,
    w2: bass.AP,
    b2: bass.AP,
    c: bass.AP,
    wmod: bass.AP,
    out: bass.AP,
):
    fp32, bf16, fp16 = mybir.dt.float32, mybir.dt.bfloat16, mybir.dt.float16
    ALU = mybir.AluOpType
    ACT = mybir.ActivationFunctionType
    AX = mybir.AxisListType

    B, L, DM = x.shape
    H = A_log.shape[0]
    DI = out_proj_w.shape[1]
    HD = DI // H
    TAPS = conv_w.shape[1]
    E, S, _ = slot_embeds.shape
    HID = w1.shape[2]
    P = 128
    CT = DI // P
    NT = L // P
    SL = E * S
    MT = SL // P
    HC = HID // P
    BP = 2
    TP = BP * NT
    W = BP * L
    LN_EPS, RMS_EPS, NORM_FLOOR = 1e-5, 1e-6, 1e-12
    ROWS = in_proj_w.shape[0]
    ROW_BLOCKS = ROWS // P
    Z0, X0, B0, C0 = 0, DI, 2 * DI, 2 * DI + P
    DT0 = 2 * DI + 2 * P
    SHIFT = 64.0
    ATANH_TERMS = [1.0 / k for k in range(15, 1, -2)]
    PART_ROW = 32

    ctx = ExitStack()
    with ctx:
        def sb(name, shape, dt=fp32):
            return ctx.enter_context(nc.sbuf_tensor(name, shape, dt))

        per_pass = {}
        base_value = {}

        def sem(name, count=1, base=0):
            per_pass[name] = count
            base_value[name] = base
            return name, [ctx.enter_context(nc.semaphore(f"{name}_{j}")) for j in range(2)]

        def wait(eng, s, j, it, k=None):
            name, sems = s
            n = per_pass[name]
            eng.wait_ge(sems[j], it * n + ((n if k is None else k) + base_value[name]))

        def hold(eng):
            eng.sem_inc(s_held, 1)

        def wait_before(eng, s, j, it):
            name, sems = s
            eng.wait_ge(sems[j], it * per_pass[name] + base_value[name])

        def start_from_base(eng, *names):
            for name, sems in names:
                for j in range(2):
                    eng.sem_inc(sems[j], base_value[name])

        s_held = ctx.enter_context(nc.semaphore("s_held"))

        ident = sb("ident", [P, P])
        ident_b = sb("ident_b", [P, P], bf16)
        ident_shift = sb("ident_shift", [P, P], fp16)
        neg_shift = sb("neg_shift", [P, P], fp16)
        ones_sq = sb("ones_sq", [P, P])
        neg_half = sb("neg_half", [P, TP])
        causal = sb("causal", [P, P])
        future = sb("future", [P, P], bf16)
        eo = sb("eo", [P, B, MT, P + 1])
        as_loaded = eo[:, :, :, :].rearrange("p b m d -> p (b m d)")
        w_nat = as_loaded[:, 0:ROW_BLOCKS * P].rearrange("p (n d) -> p n d", n=ROW_BLOCKS)
        wmod_sb = as_loaded[:, ROW_BLOCKS * P:(ROW_BLOCKS + 6) * P]
        se_nat = as_loaded[:, (ROW_BLOCKS + 6) * P:(ROW_BLOCKS + 6 + MT) * P].rearrange("p (n d) -> p n d", n=MT)
        wo_nat = as_loaded[:, (ROW_BLOCKS + 6 + MT) * P:(ROW_BLOCKS + 6 + MT + CT) * P]
        se_sq = as_loaded[:, (ROW_BLOCKS + 6 + MT + CT) * P:(ROW_BLOCKS + 7 + MT + CT) * P]
        spare = as_loaded[:, (ROW_BLOCKS + 7 + MT + CT) * P:(ROW_BLOCKS + 7 + MT + 2 * CT + 2 * BP * CT) * P]
        spare = spare.rearrange("p (n k d) -> p n k d", k=CT, d=P)
        diag_d = spare[:, 0, :, :]
        wo_gated = [spare[:, 1 + BP * j:1 + BP * (j + 1), :, :] for j in range(2)]
        dt_nat = sb("dt_nat", [H, P])
        winT = sb("winT", [P, ROWS])
        woT = sb("woT", [P, CT, P])
        se_ss = sb("se_ss", [P, MT])
        se_r = sb("se_r", [P, MT])
        snT = sb("snT", [P, SL])
        convw = sb("convw", [P, CT, TAPS])
        d_col = sb("d_col", [P, CT])
        d_half = sb("d_half", [P, CT])
        blk = sb("blk", [P, 2, H])
        dtb_row = sb("dtb_row", [P, H])
        expA_row = sb("expA_row", [P, H])
        expA_t = sb("expA_t", [P, H])
        RB1, RB2 = 0, E * HC
        RCB = RB2 + E
        RNW = RCB + CT
        RG, RSG = RNW + 1, RNW + 2
        VR = RSG + 1
        vec_nat = sb("vec_nat", [VR, P])
        vecT = sb("vecT", [P, VR])
        c_nat = sb("c_nat", [B, P])
        cT = sb("cT", [P, B])
        cs = sb("cs", [P, B])
        cs_t = sb("cs_t", [P, B])
        g_all = sb("g_all", [P, 1])
        gbT = sb("gbT", [P, B])
        mod_rows = sb("mod_rows", [B, 6, P])
        sgn_T = sb("sgn_T", [P, B])
        sgn_r = sb("sgn_r", [B, P])
        slotsT = sb("slotsT", [P, E, B, S])
        x1tok = sb("x1tok", [P, B * NT, P])
        combT = sb("combT", [P, B, MT, L])

        def two(name, shape, dt=fp32):
            return [sb(f"{name}{j}", shape, dt) for j in range(2)]

        xin = two("xin", [P, TP, P])
        bst = two("bst", [P, TP, 6])
        mv = two("mv", [P, TP, 2])
        root = two("root", [P, TP])
        ms = two("ms", [P, TP])
        hh = two("hh", [P, TP, P])
        basis = two("basis", [P, TP, P])
        mods_bc = two("mods_bc", [P, BP, 5, P])
        xntok = two("xntok", [P, TP, P])
        xnT = two("xnT", [P, W])
        zsT = two("zsT", [P, CT, W])
        xcT = two("xcT", [P, CT, W])
        xhT = two("xhT", [P, CT, W])
        BT = two("BT", [P, W])
        CTr = two("CTr", [P, W])
        dv = two("dv", [P, 8, TP * H])
        Q = two("Q", [P, TP, P], bf16)
        ksm = two("ksm", [P, W], bf16)
        rsm = two("rsm", [P, H, W], bf16)
        gm = two("gm", [P, BP, 3, P])
        seg_e = two("seg_e", [P, 3, 512])
        seg_m = two("seg_m", [P, 3, 512])
        xn2tok = two("xn2tok", [P, TP, P + 1])
        rmax = two("rmax", [P, NT])
        cmax = two("cmax", [P, MT])
        diag_r = two("diag_r", [P, NT, P], fp16)
        diag_c = two("diag_c", [P, MT, P], fp16)
        rcs = two("rcs", [P, MT])

        lt_sb = [t[:, 0:NT, :] for t in seg_e]
        e_disp = [t[:, 0:NT, :] for t in seg_m]
        dtx = [t[:, :, :].rearrange("p k t -> p (k t)").rearrange("p (t c) -> p t c", t=TP) for t in xcT]
        xn2T = CTr
        slots = [t[:, :].rearrange("p (m d) -> p m d", m=MT) for t in BT]

        bank = [ctx.enter_context(nc.psum_tensor(f"bank{i}", [P, 512], fp32)) for i in range(8)]

        s_c, s_vec, s_wmod, s_w, s_se, s_small = [ctx.enter_context(nc.semaphore(n)) for n in
                                             ("s_c", "s_vec", "s_wmod", "s_w", "s_se", "s_small")]
        s_pool = ctx.enter_context(nc.semaphore("s_pool"))
        s_pe0 = ctx.enter_context(nc.semaphore("s_pe0"))
        s_dve0 = ctx.enter_context(nc.semaphore("s_dve0"))
        s_act0 = ctx.enter_context(nc.semaphore("s_act0"))
        s_ready = ctx.enter_context(nc.semaphore("s_ready"))

        s_mod = ctx.enter_context(nc.semaphore("s_mod"))
        s_eo_ones = ctx.enter_context(nc.semaphore("s_eo_ones"))

        x_in = sem("x_in", 16)
        mods_in = sem("mods_in", 16 * BP)
        var_done = sem("var_done")
        root_done = sem("root_done", 2)
        h_done = sem("h_done")
        ms_done = sem("ms_done")
        basis_done = sem("basis_done", 2, base=1)
        xn_done = sem("xn_done")
        xnT_ps = sem("xnT_ps")
        xnT_done = sem("xnT_done")
        pool_own = sem("pool_own", 3)
        proj_ps = sem("proj_ps", 5)
        z_ps = sem("z_ps", 2)
        nabs_done = sem("nabs_done")
        edt_done = sem("edt_done")
        xbc_done = sem("xbc_done", 4)
        conv_done = sem("conv_done", 2)
        tanh_done = sem("tanh_done", 4)
        silu_done = sem("silu_done", 4)
        w_done = sem("w_done")
        cum_ps = sem("cum_ps")
        parts_done = sem("parts_done")
        parts_ps = sem("parts_ps")
        ksm_done = sem("ksm_done")
        rsm_in = sem("rsm_in", 16)
        g_ps = sem("g_ps", 2)
        g_done = sem("g_done", 2)
        xht_ps = sem("xht_ps", 2)
        dtx_done = sem("dtx_done", 2)
        seg_ps = sem("seg_ps", 6)
        seg_done = sem("seg_done", 6)
        m_done = sem("m_done", 6)
        y_ps = sem("y_ps", 2, base=1)
        yg_done = sem("yg_done", 2)
        o_ps = sem("o_ps", 2, base=1)
        var2_done = sem("var2_done", 2)
        var_root_done = sem("var_root_done", 2)
        h2_done = sem("h2_done", 2, base=1)
        ms2_done = sem("ms2_done", 2)
        ms_root_done = sem("ms_root_done", 2)
        xn2_done = sem("xn2_done", 2)
        xn2T_ps = sem("xn2T_ps", 2)
        xn2T_done = sem("xn2T_done", 2)
        pool_own_var = sem("pool_own_var", 2)
        pool_own_ms = sem("pool_own_ms", 2)
        lt_ps = sem("lt_ps", 4)
        lt_done = sem("lt_done", 4)
        diag_r_done = sem("diag_r_done", 2)
        ls_ps = sem("ls_ps", 4)
        diag_c_done = sem("diag_c_done", 2)
        shift_ps = sem("shift_ps", 8)
        disp_done = sem("disp_done", 4)
        comb_done = sem("comb_done", 4, base=1)
        slots_ps = sem("slots_ps", 4)
        slots_done = sem("slots_done", 2, base=1)
        slotsT_ps = sem("slotsT_ps", 2)
        slotsT_done = sem("slotsT_done", 2, base=1)
        STEPS = {"norm1": 2, "rest": 35}
        own_norm1 = sem("own_norm1", STEPS["norm1"])
        own_rest = sem("own_rest", STEPS["rest"])

        w1_sb = two("w1_sb", [P, HID])
        w2_sb = two("w2_sb", [P, HC, P])
        act_h = [zsT[0], zsT[1]], [xcT[0], xcT[1]]
        eoT = seg_e[0][:, 0:2, :].rearrange("p a (b e s) -> p (a b) e s", e=2, s=S)
        w1_in = sem("w1_in", 16)
        w2_in = sem("w2_in", 16)
        hid_ps = sem("hid_ps", HC)
        gelu_done = sem("gelu_done", HC, base=1)
        eoT_ps = sem("eoT_ps", base=1)
        eoT_done = sem("eoT_done", base=1)
        eo_ps = ctx.enter_context(nc.semaphore("eo_ps"))
        eo_done = ctx.enter_context(nc.semaphore("eo_done"))
        cb_done = sem("cb_done")
        comb_out_ps = sem("comb_out_ps", NT, base=1)
        y_out = sem("y_out", base=1)
        y_sent = sem("y_sent", 16, base=1)
        rden_done = ctx.enter_context(nc.semaphore("rden_done"))
        rden = two("rden", [P, NT])
        cbuf = xhT
        yout = xin

        mod_dram = nc.dram_tensor("mod_dram", (B, 6 * P), fp32, kind="Internal").ap()
        PASSES = B // (2 * BP)
        SKEW, PERIOD, START = 4.04, 91.03, -39.27

        VV, NABS, EDT, U, U2, PP, DTH, WD = range(8)
        N_VEC, N_W, N_SMALL = 16 * 6, 16 * 3, 16 * (3 + H)
        POOL_IDENT, POOL_ALL = 2, 17
        POOL_SE = POOL_ALL + 2
        ACT_TANH = 1
        ACT_SE = ACT_TANH + MT
        DVE_C = 1
        DVE_CS = DVE_C + 2
        PE_C, PE_MOD, PE_W, PE_SE = 1, 2, 3, 4

        def pipeline(eng, visits):
            todo = []
            for j in range(2):
                for n, (p, _) in enumerate(visits):
                    late, at = divmod(p - START + SKEW * j, PERIOD)
                    assert late in (0, 1)
                    todo.append((at, j, n, int(late)))
            todo.sort()

            def turn(new, old):
                for _, j, n, late in todo:
                    it = old if late else new
                    if it is not None:
                        visits[n][1](j, it)

            turn(0, None)
            with eng.Fori(0, PASSES - 1) as i:
                turn(i + 1, i)
            turn(None, PASSES - 1)

        def of_batch(bi):
            return slice(bi * NT, (bi + 1) * NT)

        def tile_cols(t, n=P):
            return slice(t * n, t * n + n)

        block = ctx.enter_context(nc.Block())

        @block.sync
        def _(sp):
            x_v = x.rearrange("b (n p) d -> p (b n) d", p=P)
            start_from_base(sp, y_sent)
            out_v = out.rearrange("b (n p) d -> p (b n) d", p=P)

            def load_x(j, it):
                sp.dma_start(xin[j][:, :, :], x_v[:, bass.ds(it * 2 * TP + j * TP, TP), :]).then_inc(x_in[1][j], 16)

            sp.dma_start(c_nat[:, :], c).then_inc(s_c, 16)
            for j in range(2):
                load_x(j, 0)
            vecs = [
                (RB1, E * HC, b1.rearrange("e (c p) -> (e c) p", p=P)),
                (RB2, E, b2),
                (RCB, CT, conv_b.rearrange("(c p) -> c p", p=P)),
                (RNW, 1, norm_w.rearrange("(o p) -> o p", o=1)),
                (RG, 1, norm_gamma.rearrange("(o p) -> o p", o=1)),
                (RSG, 1, slot_norm_gamma.rearrange("(o p) -> o p", o=1)),
            ]
            for r0, n, src in vecs:
                sp.dma_start(vec_nat[r0:r0 + n, :], src).then_inc(s_vec, 16)

            def load_mods(j, it):
                for bi in range(BP):
                    sp.dma_start(mods_bc[j][:, bi, :, :].rearrange("p m d -> p (m d)"),
                                 mod_dram[bass.ds(it * 2 * BP + (j * BP + bi), 1), 0:5 * P].broadcast_to((P, 5 * P))
                                 ).then_inc(mods_in[1][j], 16)

            sp.wait_ge(s_ready, 1)
            sp.dma_start(mod_dram, mod_rows[:, :, :].rearrange("b m d -> b (m d)")).then_inc(s_mod, 16)
            sp.wait_ge(s_mod, 16)
            for j in range(2):
                load_mods(j, 0)

            def next_x(j, it):
                if isinstance(it, int) and it == 0:
                    return
                wait_before(sp, basis_done, j, it)
                hold(sp)
                load_x(j, it)

            def next_mods(j, it):
                if isinstance(it, int) and it == 0:
                    return
                wait_before(sp, h2_done, j, it)
                hold(sp)
                load_mods(j, it)

            def send_parts(j, it):
                wait(sp, ksm_done, j, it)
                hold(sp)
                wait_before(sp, y_ps, j, it)
                hold(sp)
                sp.dma_start(rsm[j][0:3, :, :], ksm[j][PART_ROW:PART_ROW + 3 * H, :]).then_inc(rsm_in[1][j], 16)

            pipeline(sp, [(17.06, next_x), (27.7, next_mods), (77.23, send_parts)])

            def load_w(j, it):
                sp.dma_start(w1_sb[j][:, :], w1[bass.ds(it * 2 + j, 1), :, :].rearrange("o d h -> d (o h)")
                             ).then_inc(w1_in[1][j], 16)
                sp.dma_start(w2_sb[j][:, :, :],
                             w2[bass.ds(it * 2 + j, 1), :, :].rearrange("o (c p) d -> p (o c) d", p=P)
                             ).then_inc(w2_in[1][j], 16)

            for j in range(2):
                load_w(j, 0)
            with sp.Fori(0, E // 2 - 1) as it:
                for j in range(2):
                    wait(sp, hid_ps, j, it)
                    hold(sp)
                    wait(sp, eoT_ps, j, it)
                    hold(sp)
                    load_w(j, it + 1)
            with sp.Fori(0, B // 2) as it:
                for j in range(2):
                    wait(sp, y_out, j, it)
                    hold(sp)
                    sp.dma_start(out_v[:, bass.ds((it * 2 + j) * NT, NT), :],
                                 yout[j][:, 0:NT, :]).then_inc(y_sent[1][j], 16)
            for j in range(2):
                wait(sp, y_sent, j, B // 2 - 1)
                hold(sp)

        @block.gpsimd
        def _(pool):
            nc.gpsimd.memset(ones_sq[:, :], 1.0).then_inc(s_pool, 1)
            pool.wait_ge(s_pool, 1)
            nc.gpsimd.affine_select(out=ident[:, :], in_=ones_sq[:, :], compare_op=ALU.is_equal, fill=0.0, base=0,
                                    pattern=[[1, P]], channel_multiplier=-1).then_inc(s_pool, 1)
            nc.gpsimd.affine_select(out=causal[:, :], in_=ones_sq[:, :], compare_op=ALU.is_ge, fill=0.0, base=0,
                                    pattern=[[1, P]], channel_multiplier=-1).then_inc(s_pool, 1)
            nc.gpsimd.memset(neg_half[:, :], -0.5).then_inc(s_pool, 1)
            nc.gpsimd.memset(neg_shift[:, :], -SHIFT).then_inc(s_pool, 1)
            nc.gpsimd.memset(future[:, :], 0.0).then_inc(s_pool, 1)
            for j in range(2):
                nc.gpsimd.memset(Q[j][:, :, 0:3], -1.0).then_inc(s_pool, 1)
                nc.gpsimd.memset(Q[j][:, :, 3:P], 0.0).then_inc(s_pool, 1)
                nc.gpsimd.memset(xn2tok[j][:, :, P:P + 1], 1.0).then_inc(s_pool, 1)
            pool.wait_ge(s_pool, 12)
            nc.gpsimd.tensor_copy(ident_b[:, :], ident[:, :]).then_inc(s_pool, 1)
            nc.gpsimd.tensor_single_scalar(ident_shift[:, :], ident[:, :], 1.0 / SHIFT, ALU.mult).then_inc(s_pool, 1)
            nc.gpsimd.affine_select(out=future[:, :], in_=future[:, :], compare_op=ALU.is_ge, fill=-1e30, base=0,
                                    pattern=[[1, P]], channel_multiplier=-1).then_inc(s_pool, 1)
            nc.gpsimd.tensor_tensor(blk[:, 0, :], ident[:, PART_ROW:PART_ROW + H],
                                    ident[:, PART_ROW + H:PART_ROW + 2 * H], ALU.add).then_inc(s_pool, 1)
            pool.wait_ge(s_pool, 16)
            nc.gpsimd.tensor_tensor(blk[:, 1, :], blk[:, 0, :],
                                    ident[:, PART_ROW + 2 * H:PART_ROW + 3 * H], ALU.add).then_inc(s_pool, 1)
            pool.wait_ge(s_act0, ACT_SE)
            nc.gpsimd.tensor_scalar(se_r[:, :], se_ss[:, :], NORM_FLOOR ** 2 / DM, None, ALU.max).then_inc(s_pool, 1)
            pool.wait_ge(s_pool, POOL_ALL + 1)
            nc.gpsimd.tensor_tensor(se_r[:, :], se_r[:, :], neg_half[:, 0:MT], ALU.pow).then_inc(s_pool, 1)
            pool.wait_ge(s_ready, 3)

            def inverse_root(kind, done, own, ready, src, k, tiles):
                def visit(j, it):
                    wait(pool, done, j, it, k)
                    hold(pool)
                    nc.gpsimd.tensor_scalar(root[j][:, tiles], src(j)[:, tiles],
                                            (LN_EPS, RMS_EPS, NORM_FLOOR ** 2 / DM)[kind], None,
                                            ALU.max if kind == 2 else ALU.add).then_inc(own[1][j], 1)
                    at = 2 if ready is root_done and kind == 1 else k
                    wait(pool, own, j, it, at)
                    nc.gpsimd.tensor_tensor(root[j][:, tiles], root[j][:, tiles], neg_half[:, tiles], ALU.pow
                                            ).then_inc(ready[1][j], 1)
                return visit

            def var_root(bi):
                return inverse_root(0, var2_done, pool_own_var, var_root_done, variances, bi + 1, of_batch(bi))

            def ms_root(bi):
                return inverse_root(2, ms2_done, pool_own_ms, ms_root_done, mean_squares, bi + 1, of_batch(bi))

            def add_basis(j, it):
                wait(pool, h_done, j, it)
                for bi in range(BP):
                    t = slice(bi * NT, (bi + 1) * NT)
                    q = nc.gpsimd.tensor_tensor(basis[j][:, t, :], hh[j][:, t, :],
                                                mods_bc[j][:, bi, 2, :].unsqueeze(1).broadcast_to((P, NT, P)), ALU.mult)
                q.then_inc(pool_own[1][j], 1)
                wait(pool, pool_own, j, it, 3)
                nc.gpsimd.tensor_tensor(basis[j][:, :, :], basis[j][:, :, :], xin[j][:, :, :], ALU.add
                                        ).then_inc(basis_done[1][j], 1)

            start_from_base(pool, basis_done)
            variances = lambda j: mv[j][:, :, 1]
            mean_squares = lambda j: ms[j][:, :]
            def gate_weights(j, it):
                wait(pool, mods_in, j, it)
                hold(pool)
                wait_before(pool, o_ps, j, it)
                for bi in range(BP):
                    q = nc.gpsimd.tensor_tensor(wo_gated[j][:, bi, :, :], woT[:, :, :],
                                                mods_bc[j][:, bi, 2, :].unsqueeze(1).broadcast_to((P, CT, P)), ALU.mult)
                q.then_inc(basis_done[1][j], 1)

            var_root1 = inverse_root(0, var_done, pool_own, root_done, variances, 1, slice(0, TP))
            ms_root1 = inverse_root(1, ms_done, pool_own, root_done, mean_squares, 1, slice(0, TP))
            visits = [(-23.59, var_root1), (-14.84, ms_root1), (-0.21, add_basis), (3.06, gate_weights),
                      (15.9, var_root(0)), (55.17, var_root(1)), (56.18, ms_root(0)), (56.2, ms_root(1))]
            pipeline(pool, visits)

            for j in range(2):
                wait(pool, slotsT_done, j, PASSES - 1)
            nc.gpsimd.memset(eo[:, :, :, P:P + 1], 1.0).then_inc(s_eo_ones, 1)

        @block.tensor
        def _(pe):
            def mm(o, lhsT, rhs, start=True, stop=True):
                return nc.tensor.matmul(o, lhsT, rhs, start=start, stop=stop)

            start_from_base(pe, y_ps, o_ps, eoT_ps, comb_out_ps)
            pe.sem_inc(eo_ps, 1)
            pe.wait_ge(s_pool, POOL_IDENT)
            pe.wait_ge(s_c, 16)
            nc.tensor.transpose(bank[0][:, P:P + B], c_nat[:, :], ident[0:B, 0:B]).then_inc(s_pe0, 1)
            pe.wait_ge(s_wmod, 16)
            pe.wait_ge(s_dve0, DVE_CS)
            mm(bank[5][0:B, 0:3 * P], cs[:, :], wmod_sb[:, 0:3 * P])
            mm(bank[6][0:B, 0:3 * P], cs[:, :], wmod_sb[:, 3 * P:6 * P])
            mm(bank[7][:, 0:B], wmod_sb[:, tile_cols(5)], cs[:, :]).then_inc(s_pe0, 1)
            pe.wait_ge(s_vec, N_VEC)
            nc.tensor.transpose(bank[0][:, 0:VR], vec_nat[:, :], ident[0:VR, 0:VR])
            pe.wait_ge(s_w, N_W)
            for n in range(ROW_BLOCKS):
                q = nc.tensor.transpose(bank[1 + n // 4][:, tile_cols(n % 4)], w_nat[:, n, :], ident[:, :])
            q = nc.tensor.transpose(bank[3][:, 0:H], dt_nat[:, :], ident[0:H, 0:H])
            for k in range(CT):
                q = nc.tensor.transpose(bank[3][:, tile_cols(1 + k)], wo_nat[:, tile_cols(k)], ident[:, :])
            q.then_inc(s_pe0, 1)
            pe.wait_ge(s_ready, 2)
            for m in range(MT):
                q = nc.tensor.transpose(bank[4][:, tile_cols(m)], se_nat[:, m, :], ident[:, :])
            q.then_inc(s_pe0, 1)
            pe.wait_ge(s_pool, POOL_ALL)
            pe.wait_ge(s_ready, 3)

            def t_xn(j, it):
                wait(pe, xn_done, j, it)
                wait_before(pe, comb_done, j, it)
                for t in range(TP):
                    q = nc.tensor.transpose(bank[4 * j + 3][:, tile_cols(t)], xntok[j][:, t, 0:P], ident[:, :])
                q.then_inc(xnT_ps[1][j], 1)

            def t_xn2(bi):
                def visit(j, it):
                    wait(pe, xn2_done, j, it, bi + 1)
                    for n in range(NT):
                        q = nc.tensor.transpose(bank[4 * j + bi][:, L + n * P:L + (n + 1) * P],
                                                xn2tok[j][:, bi * NT + n, 0:P], ident[:, :])
                    q.then_inc(xn2T_ps[1][j], 1)
                return visit

            def project1(j, it):
                b0, b1, b2, b3 = bank[4 * j:4 * j + 4]
                wait(pe, xnT_done, j, it)
                for t in range(TP):
                    q = mm(b3[:, t * H:(t + 1) * H], xnT[j][:, tile_cols(t)], winT[:, DT0:ROWS])
                q.then_inc(proj_ps[1][j], 1)
                wait_before(pe, slots_done, j, it)
                mm(b0[:, :], winT[:, X0:X0 + P], xnT[j][:, :]).then_inc(proj_ps[1][j], 1)
                mm(b1[:, :], winT[:, X0 + P:X0 + 2 * P], xnT[j][:, :]).then_inc(proj_ps[1][j], 1)
                wait_before(pe, slotsT_done, j, it)
                mm(b2[:, :], winT[:, B0:B0 + P], xnT[j][:, :]).then_inc(proj_ps[1][j], 1)

            def project2(j, it):
                wait(pe, nabs_done, j, it)
                mm(bank[4 * j + 3][:, :], winT[:, C0:C0 + P], xnT[j][:, :]).then_inc(proj_ps[1][j], 1)
                wait(pe, xbc_done, j, it, 3)
                mm(bank[4 * j + 2][:, :], winT[:, Z0:Z0 + P], xnT[j][:, :]).then_inc(z_ps[1][j], 1)

            def project3(j, it):
                wait(pe, xbc_done, j, it, 4)
                mm(bank[4 * j + 3][:, :], winT[:, Z0 + P:Z0 + 2 * P], xnT[j][:, :]).then_inc(z_ps[1][j], 1)

            def scores(j, it):
                wait(pe, xbc_done, j, it)
                for bi in range(BP):
                    wait(pe, conv_done, j, it, bi + 1)
                    o = bank[4 * j + bi]
                    t0 = bi * L
                    mm(o[:, 0:L], BT[j][:, t0:t0 + P], CTr[j][:, t0:t0 + L])
                    mm(o[:, L:L + P], BT[j][:, t0 + P:t0 + L], CTr[j][:, t0 + P:t0 + L]).then_inc(g_ps[1][j], 1)

            def running_sums(j, it):
                wait(pe, w_done, j, it)
                wait(pe, silu_done, j, it, 1)
                o = bank[4 * j + 2]
                mm(o[:, 0:TP * H], causal[:, :], dv[j][:, WD, :], stop=False)
                w4 = dv[j][:, WD, :].rearrange("p (b n h) -> p b n h", b=BP, n=NT)
                o4 = o[:, 0:TP * H].rearrange("p (b n h) -> p b n h", b=BP, n=NT)
                mm(o4[:, :, 1, :], ones_sq[:, :], w4[:, :, 0, :], start=False).then_inc(cum_ps[1][j], 1)

            def part_rows(j, it):
                wait(pe, parts_done, j, it)
                o = bank[4 * j + 2][:, :].bitcast(bf16)
                for t in range(TP):
                    q = nc.tensor.transpose(o[:, tile_cols(t)], Q[j][:, t, :], ident_b[:, :])
                q.then_inc(parts_ps[1][j], 1)

            def t_xh(j, it):
                for bi in range(BP):
                    wait(pe, g_done, j, it, bi + 1)
                    wait(pe, silu_done, j, it, 4)
                    for n in range(NT):
                        for k in range(CT):
                            t = bi * NT + n
                            q = nc.tensor.transpose(bank[4 * j + bi][:, tile_cols(n * CT + k)],
                                                    xhT[j][:, k, tile_cols(t)], ident[:, :])
                    q.then_inc(xht_ps[1][j], 1)

            def segment(f):
                def visit(j, it):
                    bi, g = divmod(f, 3)
                    o = bank[4 * j + 2 + f % 2]
                    if f == 0:
                        wait(pe, ksm_done, j, it)
                        wait(pe, rsm_in, j, it)
                    if f == 1:
                        wait(pe, silu_done, j, it, 3)
                    if f >= 2:
                        wait(pe, seg_done, j, it, f - 1)
                    if g < 2:
                        mm(o[:, :], ksm[j][:, bi * L:bi * L + P],
                           rsm[j][:, 2 * g:2 * g + 2, bi * L:(bi + 1) * L], stop=False)
                        mm(o[:, :].rearrange("p (h t) -> p h t", h=2)[:, :, 0:P], ident_b[:, :],
                           future[:, :].unsqueeze(1).broadcast_to((P, 2, P)), start=False).then_inc(seg_ps[1][j], 1)
                    else:
                        mm(o[:, :], ksm[j][:, bi * L + P:bi * L + L],
                           rsm[j][:, :, bi * L + P:(bi + 1) * L], stop=False)
                        mm(o[:, :].rearrange("p (h t) -> p h t", h=H), ident_b[:, :],
                           future[:, :].unsqueeze(1).broadcast_to((P, H, P)), start=False).then_inc(seg_ps[1][j], 1)
                return visit

            def y_of(bi):
                def visit(j, it):
                    wait(pe, dtx_done, j, it, bi + 1)
                    for k in range(CT):
                        mm(bank[4 * j + bi][:, k * L:(k + 1) * L], diag_d[:, k, :], xhT[j][:, k, bi * L:(bi + 1) * L],
                           stop=False)
                        if k == 0:
                            wait(pe, m_done, j, it, 3 * bi + 3)
                        for h in (2 * k, 2 * k + 1):
                            o = bank[4 * j + bi][(h % 2) * HD:(h % 2 + 1) * HD, k * L:(k + 1) * L]
                            mm(o, dtx[j][:, bi * NT, h * HD:(h + 1) * HD],
                               seg_m[j][:, k, (h % 2) * L:(h % 2 + 1) * L], start=False, stop=False)
                            q = mm(o[:, P:L], dtx[j][:, bi * NT + 1, h * HD:(h + 1) * HD],
                                   seg_m[j][:, 2, tile_cols(h)], start=False)
                    q.then_inc(y_ps[1][j], 1)
                return visit

            def project_out(bi):
                def visit(j, it):
                    wait(pe, yg_done, j, it, bi + 1)
                    wait(pe, basis_done, j, it)
                    for n in range(NT):
                        t = bi * NT + n
                        for k in range(CT):
                            q = mm(bank[4 * j + bi][:, tile_cols(n)], xhT[j][:, k, tile_cols(t)], wo_gated[j][:, bi, k, :],
                                   start=k == 0, stop=k == CT - 1)
                    q.then_inc(o_ps[1][j], 1)
                return visit

            def by_token(j, bi, n):
                return bank[4 * j + (2, 0)[bi] + n]

            def by_slot(j, bi, n):
                return bank[4 * j + (0, 2)[bi] + n]

            def logits(bi):
                def visit(j, it):
                    wait(pe, xn2T_done, j, it, bi + 1)
                    if bi:
                        wait(pe, comb_done, j, it, 2)
                    else:
                        wait(pe, seg_done, j, it)
                    for n in range(NT):
                        mm(by_token(j, bi, n)[:, :], xn2T[j][:, tile_cols(bi * NT + n)],
                           snT[:, :]).then_inc(lt_ps[1][j], 1)
                return visit

            def t_logits(bi):
                def visit(j, it):
                    if bi:
                        wait(pe, slotsT_done, j, it, bi)
                    else:
                        wait(pe, xn2T_done, j, it, 2)
                    wait(pe, lt_done, j, it, 2 * bi + 2)
                    for m in range(MT):
                        o = by_slot(j, bi, m // 2)
                        for n in range(NT):
                            at = (m % 2) * L + n * P
                            q = nc.tensor.matmul(o[:, at:at + P], lt_sb[j][:, n, tile_cols(m)], ident[:, :],
                                                 is_transpose=True, start=at == 0, stop=at == 512 - P,
                                                 skip_group_check=True)
                        if m % 2:
                            q.then_inc(ls_ps[1][j], 1)
                return visit

            def shifts(bi):
                def visit(j, it):
                    wait(pe, diag_r_done, j, it, bi + 1)
                    wait(pe, diag_c_done, j, it, bi + 1)
                    for n in range(NT):
                        nc.tensor.matmul(by_token(j, bi, n)[:, :], neg_shift[:, :], diag_c[j][:, :, :],
                                         start=False, stop=True, skip_group_check=True
                                         ).then_inc(shift_ps[1][j], 1)
                    for m2 in range(2):
                        nc.tensor.matmul(by_slot(j, bi, m2)[:, :], neg_shift[:, :],
                                         diag_r[j][:, :, :].rearrange("p n t -> p (n t)").unsqueeze(1).broadcast_to((P, 2, L)),
                                         start=False, stop=True, skip_group_check=True
                                         ).then_inc(shift_ps[1][j], 1)
                return visit

            def fill_slots(bi):
                def visit(j, it):
                    wait(pe, disp_done, j, it, 2 * bi + 2)
                    for m in range(MT):
                        o = by_token(j, bi, m // 2)[:, (m % 2) * (P + 1):(m % 2 + 1) * (P + 1)]
                        for n in range(NT):
                            q = mm(o, e_disp[j][:, n, tile_cols(m)], xn2tok[j][:, bi * NT + n, :],
                                   start=n == 0, stop=n == NT - 1)
                        if m % 2:
                            q.then_inc(slots_ps[1][j], 1)
                return visit

            def t_slots(bi):
                def visit(j, it):
                    wait(pe, slots_done, j, it, bi + 1)
                    wait(pe, comb_done, j, it, 2 * bi + 2)
                    for m in range(MT):
                        q = nc.tensor.transpose(bank[4 * j + 2][:, tile_cols(m)], slots[j][:, m, :], ident[:, :])
                    q.then_inc(slotsT_ps[1][j], 1)
                return visit

            visits = [(-11.85, t_xn), (-8.25, project1), (-5.29, project2), (4.92, project3), (7.52, scores),
                      (7.54, running_sums), (17.64, part_rows), (17.66, t_xh), (25.92, segment(0)),
                      (25.94, segment(1)), (29.71, segment(2)), (30.48, segment(3)), (33.47, y_of(0)),
                      (34.7, segment(4)), (36.12, segment(5)), (36.97, project_out(0)), (40.29, y_of(1)),
                      (42.61, project_out(1)), (47.75, t_xn2(0)), (50.67, logits(0)), (50.69, t_xn2(1)),
                      (51.88, t_logits(0)), (55.23, shifts(0)), (59.07, fill_slots(0)), (60.99, logits(1)),
                      (63.88, t_slots(0)), (67.8, t_logits(1)), (74.22, shifts(1)), (77.74, fill_slots(1)),
                      (80.63, t_slots(1))]
            pipeline(pe, visits)

            for j in range(2):
                wait(pe, slotsT_done, j, PASSES - 1)
            def hidden(it):
                for j in range(2):
                    wait(pe, w1_in, j, it)
                    for k in range(HC):
                        if j == 0:
                            wait_before(pe, gelu_done, 1, it)
                        else:
                            wait(pe, gelu_done, 0, it, k + 1)
                        mm(bank[k][:, :], w1_sb[j][:, tile_cols(k)],
                           slotsT[:, bass.ds(it * 2 + j, 1), :, :].rearrange("p e b s -> p (e b s)")
                           ).then_inc(hid_ps[1][j], 1)

            def outputs(it):
                for j in range(2):
                    wait(pe, w2_in, j, it)
                    wait(pe, gelu_done, j, it)
                    wait_before(pe, eoT_done, j, it)
                    for k in range(HC):
                        q = mm(bank[4 + j][:, :], w2_sb[j][:, k, :], act_h[j][k // 2][:, k % 2, :],
                               start=k == 0, stop=k == HC - 1)
                    q.then_inc(eoT_ps[1][j], 1)

            def t_outputs(it):
                for j in range(2):
                    wait(pe, eoT_done, j, it)
                pe.wait_ge(eo_done, it * 2 + 1)
                for b in range(B):
                    q = nc.tensor.transpose(bank[6 + b // 4][:, tile_cols(b % 4)],
                                            eoT[:, b, :, :].rearrange("p e s -> p (e s)"), ident[:, :])
                    if b % 4 == 3:
                        q.then_inc(eo_ps, 1)

            hidden(0)
            outputs(0)
            with pe.Fori(0, E // 2 - 1) as it:
                hidden(it + 1)
                t_outputs(it)
                outputs(it + 1)
            t_outputs(E // 2 - 1)
            pe.wait_ge(eo_done, E + 1)
            pe.wait_ge(s_eo_ones, 1)
            with pe.Fori(0, B // 2) as it:
                for j in range(2):
                    wait(pe, cb_done, j, it)
                    wait_before(pe, y_out, j, it)
                    for n in range(NT):
                        for m in range(MT):
                            q = mm(bank[2 * j + n][:, 0:P + 1], cbuf[j][:, m // 2, (m % 2) * L + n * P:(m % 2) * L + n * P + P],
                                   eo[:, bass.ds(it * 2 + j, 1), m, :].rearrange("p b d -> p (b d)"),
                                   start=m == 0, stop=m == MT - 1)
                        q.then_inc(comb_out_ps[1][j], 1)

        @block.scalar
        def _(act):
            A = nc.scalar.activation
            start_from_base(act, slotsT_done, comb_done, gelu_done)
            act.sem_inc(eo_done, 1)
            act.dma_start(wmod_sb[:, :], wmod).then_inc(s_wmod, 16)
            nc.scalar.preload_act_table(ACT.Exp)
            act.wait_ge(s_dve0, DVE_C)
            A(cs_t[:, :], cT[:, :], ACT.Tanh, scale=0.5).then_inc(s_act0, 1)
            act.dma_start(se_nat[:, :, :],
                          slot_embeds.rearrange("(n a) s d -> (a s) n d", a=P // S)).then_inc(s_se, 16)
            act.dma_start(w_nat[:, :, :],
                          in_proj_w[0:ROW_BLOCKS * P, :].rearrange("(n p) d -> p n d", p=P)).then_inc(s_w, 16)
            act.dma_start(dt_nat[:, :], in_proj_w[DT0:ROWS, :]).then_inc(s_w, 16)
            act.dma_start(wo_nat[:, :], out_proj_w).then_inc(s_w, 16)
            act.dma_start(convw[:, :, :], conv_w.rearrange("(c p) k -> p c k", p=P)).then_inc(s_small, 16)
            act.dma_start(dtb_row[:, :],
                          dt_bias.rearrange("(o h) -> o h", o=1).broadcast_to((P, H))).then_inc(s_small, 16)
            act.dma_start(expA_row[:, :],
                          A_log.rearrange("(o h) -> o h", o=1).broadcast_to((P, H))).then_inc(s_small, 16)
            for h in range(H):
                act.dma_start(d_col[(h % 2) * HD:(h % 2 + 1) * HD, h // 2:h // 2 + 1],
                              D[h:h + 1].rearrange("(o h) -> o h", o=1).broadcast_to((HD, 1))).then_inc(s_small, 16)
            act.wait_ge(s_se, 16)
            for m in range(MT):
                A(se_sq[:, :], se_nat[:, m, :], ACT.Square, scale=float(DM) ** -0.5, accum_out=se_ss[:, m:m + 1]).then_inc(s_act0, 1)
                act.wait_ge(s_act0, ACT_TANH + m + 1)
            act.wait_ge(s_small, N_SMALL)
            A(expA_t[:, :], expA_row[:, :], ACT.Exp).then_inc(s_act0, 1)
            act.wait_ge(s_pool, POOL_ALL)
            for j in range(2):
                A(rsm[j][:, :, :], blk[:, 1, :].unsqueeze(2).broadcast_to((P, H, W)), ACT.Copy).then_inc(s_act0, 1)
            act.wait_ge(s_ready, 1)

            def mods(j, it, bi):
                return bass.ds(it * 2 * BP + j * BP + bi, 1)

            def squares(j, unused, tiles):
                for t in tiles:
                    q = A(unused[:, t, 0:P], hh[j][:, t, :], ACT.Square, scale=float(DM) ** -0.5,
                          accum_out=ms[j][:, t:t + 1])
                return q

            def mean_squares1(j, it):
                wait(act, h_done, j, it)
                squares(j, xntok[j], range(TP)).then_inc(ms_done[1][j], 1)

            def mean_squares2(bi):
                def visit(j, it):
                    wait(act, h2_done, j, it, bi + 1)
                    squares(j, xn2tok[j], range(bi * NT, (bi + 1) * NT)).then_inc(ms2_done[1][j], 1)
                return visit

            def copy_xnT(j, it):
                wait(act, xnT_ps, j, it)
                A(xnT[j][:, :], bank[4 * j + 3][:, :], ACT.Copy).then_inc(xnT_done[1][j], 1)

            def copy_xn2T(bi):
                def visit(j, it):
                    wait(act, xn2T_ps, j, it, bi + 1)
                    A(xn2T[j][:, bi * L:(bi + 1) * L], bank[4 * j + bi][:, L:2 * L], ACT.Copy
                      ).then_inc(xn2T_done[1][j], 1)
                return visit

            def first_tap(j, it):
                for k in range(CT):
                    wait(act, proj_ps, j, it, k + 2)
                    A(xcT[j][:, k, :], bank[4 * j + k][:, :], ACT.Identity, bias=vecT[:, RCB + k:RCB + k + 1],
                      scale=convw[:, k, TAPS - 1:TAPS]).then_inc(xbc_done[1][j], 1)
                wait(act, proj_ps, j, it, 4)
                A(BT[j][:, :], bank[4 * j + 2][:, :], ACT.Copy).then_inc(xbc_done[1][j], 1)

            def exp_dt(j, it):
                wait(act, nabs_done, j, it)
                A(dv[j][:, EDT, :], dv[j][:, NABS, :], ACT.Exp).then_inc(edt_done[1][j], 1)

            def copy_c(j, it):
                wait(act, proj_ps, j, it, 5)
                A(CTr[j][:, :], bank[4 * j + 3][:, :], ACT.Copy).then_inc(xbc_done[1][j], 1)

            def tanh_xz(k):
                def visit(j, it):
                    wait(act, z_ps, j, it, k + 1)
                    A(zsT[j][:, k, :], bank[4 * j + 2 + k][:, :], ACT.Tanh, scale=0.5).then_inc(tanh_done[1][j], 1)
                    wait(act, conv_done, j, it, k + 1)
                    A(xhT[j][:, k, :], xcT[j][:, k, :], ACT.Tanh, scale=0.5).then_inc(tanh_done[1][j], 1)
                return visit

            def copy_scores(j, it):
                for bi in range(BP):
                    wait(act, g_ps, j, it, bi + 1)
                    A(gm[j][:, bi, :, :].rearrange("p n t -> p (n t)"), bank[4 * j + bi][:, 0:3 * P], ACT.Copy
                      ).then_inc(g_done[1][j], 1)

            def copy_parts(j, it):
                wait(act, parts_ps, j, it)
                A(ksm[j][:, :], bank[4 * j + 2][:, :].bitcast(bf16)[:, 0:W], ACT.Copy).then_inc(ksm_done[1][j], 1)

            def decay(f):
                def visit(j, it):
                    wait(act, seg_ps, j, it, f + 1)
                    if f >= 3:
                        wait(act, m_done, j, it, f - 2)
                    A(seg_e[j][:, f % 3, :], bank[4 * j + 2 + f % 2][:, :], ACT.Exp).then_inc(seg_done[1][j], 1)
                return visit

            def copy_logits(bi):
                def visit(j, it):
                    for n in range(NT):
                        wait(act, lt_ps, j, it, 2 * bi + n + 1)
                        A(lt_sb[j][:, n, :], bank[4 * j + (2, 0)[bi] + n][:, :], ACT.Copy).then_inc(lt_done[1][j], 1)
                return visit

            def exps(bi):
                def visit(j, it):
                    for n in range(NT):
                        wait(act, shift_ps, j, it, 4 * bi + n + 1)
                        A(e_disp[j][:, n, :], bank[4 * j + (2, 0)[bi] + n][:, :], ACT.Exp).then_inc(disp_done[1][j], 1)
                    for m2 in range(2):
                        wait(act, shift_ps, j, it, 4 * bi + NT + m2 + 1)
                        A(combT[:, mods(j, it, bi), 2 * m2:2 * m2 + 2, :].rearrange("p b m t -> p (b m t)"),
                          bank[4 * j + (0, 2)[bi] + m2][:, :], ACT.Exp).then_inc(comb_done[1][j], 1)
                return visit

            def copy_slotsT(bi):
                def visit(j, it):
                    wait(act, slotsT_ps, j, it, bi + 1)
                    A(slotsT[:, :, mods(j, it, bi), :].rearrange("p e b s -> p e (b s)"),
                      bank[4 * j + 2][:, :].rearrange("p (e s) -> p e s", e=E),
                      ACT.Identity, scale=vecT[:, RG:RG + 1]).then_inc(slotsT_done[1][j], 1)
                return visit

            visits = [(-22.63, mean_squares1), (-5.87, copy_xnT), (-2.21, exp_dt), (-2, first_tap),
                      (-1.06, copy_c), (-0.25, tanh_xz(0)), (7.29, tanh_xz(1)), (8.26, copy_scores),
                      (8.28, copy_parts), (32.39, decay(0)), (32.41, decay(1)), (34, decay(2)),
                      (37.07, decay(3)), (40.7, decay(4)), (40.72, decay(5)), (44.99, mean_squares2(0)),
                      (49.71, mean_squares2(1)), (51.03, copy_xn2T(0)), (51.05, copy_logits(0)),
                      (52.83, copy_xn2T(1)), (58.82, exps(0)), (68.98, copy_logits(1)),
                      (72.32, copy_slotsT(0)), (78.39, exps(1)), (88.36, copy_slotsT(1))]
            pipeline(act, visits)

            def copy_comb(j, it):
                A(cbuf[j][:, :, :].rearrange("p a b -> p (a b)"),
                  combT[:, bass.ds(it * 2 + j, 1), :, :].rearrange("p b m t -> p (b m t)"), ACT.Copy
                  ).then_inc(cb_done[1][j], 1)

            def gelus(it):
                for j in range(2):
                    for k in range(HC):
                        wait(act, hid_ps, j, it, k + 1)
                        wait_before(act, eoT_ps, j, it)
                        A(act_h[j][k // 2][:, k % 2, :], bank[k][:, :], ACT.Gelu,
                          bias=vecT[:, bass.ds(it * 2 * HC + (RB1 + j * HC + k), 1)]).then_inc(gelu_done[1][j], 1)

            def copy_eo(it):
                for g in range(2):
                    act.wait_ge(eo_ps, it * 2 + (g + 2))
                    A(eo[:, 4 * g:4 * g + 4, bass.ds(it, 1), 0:P].rearrange("p b m d -> p b (m d)"),
                      bank[6 + g][:, :].rearrange("p (b d) -> p b d", b=4), ACT.Copy).then_inc(eo_done, 1)

            gelus(0)
            for j in range(2):
                copy_comb(j, 0)
            with act.Fori(0, E // 2 - 1) as it:
                gelus(it + 1)
                copy_eo(it)
            copy_eo(E // 2 - 1)
            with act.Fori(0, B // 2 - 1) as it:
                for j in range(2):
                    wait(act, comb_out_ps, j, it)
                    copy_comb(j, it + 1)

        @block.vector
        def _(dve):
            V = nc.vector
            start_from_base(dve, slots_done, h2_done, eoT_done, y_out)
            n0 = [0]

            def step0(q):
                n0[0] += 1
                q.then_inc(s_dve0, 1)
                dve.wait_ge(s_dve0, n0[0])

            dve.wait_ge(s_pe0, PE_C)
            step0(V.tensor_copy(cT[:, :], bank[0][:, P:P + B]))
            assert n0[0] == DVE_C
            dve.wait_ge(s_act0, ACT_TANH)
            step0(V.scalar_tensor_tensor(cs[:, :], cs_t[:, :], 1.0, cT[:, :], ALU.add, ALU.mult))
            step0(V.tensor_scalar(cs[:, :], cs[:, :], 0.5, None, ALU.mult))
            assert n0[0] == DVE_CS
            done = [{own_norm1[0]: 0, own_rest[0]: 0} for _ in range(2)]

            def step(j, it, q, own=own_rest):
                name, sems = own
                done[j][name] = done[j][name] % per_pass[name] + 1
                q.then_inc(sems[j], 1)
                wait(dve, own, j, it, done[j][name])

            def x1_tile(j, it, t, n=1):
                return x1tok[:, bass.ds(it * 2 * TP + (j * TP + t), n), :]

            def layer_input(layer, j, it, t):
                if layer == 0:
                    return xin[j][:, t, :]
                return x1_tile(j, it, t).rearrange("p t d -> p (t d)")

            def statistics_of(j, it, layer, tiles, own, done_signal):
                hold(dve)
                for t in tiles:
                    q = V.bn_stats(bst[j][:, t, :], layer_input(layer, j, it, t))
                step(j, it, q, own)
                hold(dve)
                for t in tiles:
                    q = V.bn_aggr(mv[j][:, t, :], bst[j][:, t, :])
                q.then_inc(done_signal[1][j], 1)

            def first_statistics(j):
                wait(dve, x_in, j, 0)
                statistics_of(j, 0, 0, range(TP), own_norm1, var_done)

            def statistics1(j, it):
                if isinstance(it, int) and it == 0:
                    return
                wait(dve, x_in, j, it)
                statistics_of(j, it, 0, range(TP), own_norm1, var_done)

            def statistics2(bi):
                def visit(j, it):
                    statistics_of(j, it, 1, range(bi * NT, (bi + 1) * NT), own_rest, var2_done)
                    wait(dve, var2_done, j, it, bi + 1)
                    centre(j, it, 1, [bi], own_rest)
                return visit

            first_statistics(0)
            dve.wait_ge(s_pe0, PE_MOD)
            for g in range(2):
                q = V.tensor_copy(mod_rows[:, 3 * g:3 * g + 3, :],
                                  bank[5 + g][0:B, 0:3 * P].rearrange("b (m d) -> b m d", m=3))
            step0(q)
            for m in (1, 4):
                V.tensor_scalar(mod_rows[:, m, :], mod_rows[:, m, :], 1.0, None, ALU.add)
            step0(V.tensor_copy(gbT[:, :], bank[7][:, 0:B]))

            def gate_of(g, sg):
                step0(V.tensor_scalar(sg, g, 0.0, 2.0, ALU.is_ge, ALU.mult))
                V.tensor_scalar(sg, sg, 1.0, None, ALU.subtract)
                step0(V.scalar_tensor_tensor(g, g, -1.0, g, ALU.mult, ALU.max))
                step0(V.tensor_scalar(g, g, 0.25, None, ALU.max))
                step0(V.tensor_tensor(g, g, sg, ALU.mult))

            gate_of(mod_rows[:, 2, :], sgn_r[:, :])
            dve.sem_inc(s_ready, 1)
            first_statistics(1)
            gate_of(gbT[:, :], sgn_T[:, :])
            dve.wait_ge(s_pool, POOL_SE)
            for m in range(MT):
                q = V.tensor_scalar(se_nat[:, m, :], se_nat[:, m, :], se_r[:, m:m + 1], None, ALU.mult)
            step0(q)
            dve.sem_inc(s_ready, 1)
            dve.wait_ge(s_pe0, PE_W)
            step0(V.tensor_copy(vecT[:, :], bank[0][:, 0:VR]))
            V.tensor_scalar(winT[:, 0:512], bank[1][:, :], vecT[:, RNW:RNW + 1], None, ALU.mult)
            V.tensor_scalar(winT[:, 512:DT0], bank[2][:, 0:DT0 - 512], vecT[:, RNW:RNW + 1], None, ALU.mult)
            V.tensor_scalar(winT[:, DT0:ROWS], bank[3][:, 0:H], vecT[:, RNW:RNW + 1], None, ALU.mult)
            V.tensor_scalar(woT[:, :, :], bank[3][:, P:P + CT * P].rearrange("p (k d) -> p k d", k=CT),
                            0.5, None, ALU.mult)
            dve.wait_ge(s_small, N_SMALL)
            step0(V.tensor_scalar(d_half[:, :], d_col[:, :], 0.5, None, ALU.mult))
            for k in range(CT):
                V.tensor_scalar(diag_d[:, k, :], ident[:, :], d_half[:, k:k + 1], None, ALU.mult)
            step0(V.tensor_tensor(g_all[:, :], vecT[:, RG:RG + 1], vecT[:, RSG:RSG + 1], ALU.mult))
            dve.wait_ge(s_pe0, PE_SE)
            step0(V.tensor_scalar(snT[:, :], bank[4][:, :], g_all[:, :], None, ALU.mult))
            dve.sem_inc(s_ready, 1)

            def centre(j, it, layer, batches, own):
                for bi in batches:
                    for t in range(bi * NT, (bi + 1) * NT):
                        q = V.scalar_tensor_tensor(hh[j][:, t, :], layer_input(layer, j, it, t), mv[j][:, t, 0:1],
                                                   mods_bc[j][:, bi, 3 * layer + 1, :], ALU.subtract, ALU.mult)
                step(j, it, q, own)

            def modulation(j, layer, batches):
                for bi in batches:
                    for t in range(bi * NT, (bi + 1) * NT):
                        q = V.scalar_tensor_tensor(hh[j][:, t, :], hh[j][:, t, :], root[j][:, t:t + 1],
                                                   mods_bc[j][:, bi, 3 * layer, :], ALU.mult, ALU.add)
                return q

            def centre1(j, it):
                wait(dve, mods_in, j, it)
                wait(dve, var_done, j, it)
                centre(j, it, 0, range(BP), own_norm1)

            def modulate1(j, it):
                wait(dve, root_done, j, it, 1)
                modulation(j, 0, range(BP)).then_inc(h_done[1][j], 1)

            def modulate2(bi):
                def visit(j, it):
                    wait(dve, var_root_done, j, it, bi + 1)
                    modulation(j, 1, [bi]).then_inc(h2_done[1][j], 1)
                return visit

            def unit1(j, it):
                wait(dve, root_done, j, it, 2)
                for t in range(TP):
                    q = V.tensor_scalar(xntok[j][:, t, 0:P], hh[j][:, t, :], root[j][:, t:t + 1], None, ALU.mult)
                q.then_inc(xn_done[1][j], 1)

            def unit2(bi):
                def visit(j, it):
                    wait(dve, ms_root_done, j, it, bi + 1)
                    for t in range(bi * NT, (bi + 1) * NT):
                        q = V.tensor_scalar(xn2tok[j][:, t, 0:P], hh[j][:, t, :], root[j][:, t:t + 1], None, ALU.mult)
                    q.then_inc(xn2_done[1][j], 1)
                return visit

            def dt_in(j, it):
                wait(dve, proj_ps, j, it, 1)
                d = dv[j]
                step(j, it, V.tensor_tensor(d[:, VV, :].rearrange("p (t h) -> p t h", h=H),
                                            bank[4 * j + 3][:, 0:TP * H].rearrange("p (t h) -> p t h", h=H),
                                            dtb_row[:, :].unsqueeze(1).broadcast_to((P, TP, H)), ALU.add))
                V.scalar_tensor_tensor(d[:, NABS, :], d[:, VV, :], -1.0, d[:, VV, :], ALU.mult, ALU.min
                                       ).then_inc(nabs_done[1][j], 1)

            def softplus_steps(j, it):
                wait(dve, edt_done, j, it)
                d = dv[j]
                yield V.tensor_scalar(d[:, U, :], d[:, EDT, :], 2.0, None, ALU.add)
                yield V.reciprocal(d[:, U, :], d[:, U, :])
                yield V.tensor_tensor(d[:, U, :], d[:, U, :], d[:, EDT, :], ALU.mult)
                yield V.tensor_tensor(d[:, U2, :], d[:, U, :], d[:, U, :], ALU.mult)
                yield V.tensor_scalar(d[:, PP, :], d[:, U2, :], ATANH_TERMS[0], None, ALU.mult)
                for term in ATANH_TERMS[1:]:
                    yield V.scalar_tensor_tensor(d[:, PP, :], d[:, PP, :], term, d[:, U2, :], ALU.add, ALU.mult)
                yield V.scalar_tensor_tensor(d[:, PP, :], d[:, PP, :], 1.0, d[:, U, :], ALU.add, ALU.mult)
                yield V.tensor_scalar(d[:, VV, :], d[:, VV, :], 0.0, 0.5, ALU.max, ALU.mult)
                yield V.tensor_tensor(d[:, DTH, :], d[:, PP, :], d[:, VV, :], ALU.add)
                V.scalar_tensor_tensor(d[:, WD, :].rearrange("p (t h) -> p t h", h=H),
                                       d[:, DTH, :].rearrange("p (t h) -> p t h", h=H), 2.0,
                                       expA_t[:, :].unsqueeze(1).broadcast_to((P, TP, H)), ALU.mult, ALU.mult
                                       ).then_inc(w_done[1][j], 1)

            def conv_steps(j, it):
                for k in range(CT):
                    wait(dve, xbc_done, j, it, k + 1)
                    acc = xcT[j][:, k, :].rearrange("p (b t) -> p b t", b=BP)
                    src = bank[4 * j + k][:, :].rearrange("p (b t) -> p b t", b=BP)
                    for back in range(1, TAPS):
                        q = V.scalar_tensor_tensor(acc[:, :, back:L], src[:, :, 0:L - back],
                                                   convw[:, k, TAPS - 1 - back:TAPS - back],
                                                   acc[:, :, back:L], ALU.mult, ALU.add)
                        if back < TAPS - 1:
                            yield q
                    q.then_inc(conv_done[1][j], 1)
                    yield None

            def conv_and_softplus(j, it):
                name, sems = own_rest
                chains, last = [conv_steps(j, it), softplus_steps(j, it)], [0, 0]
                while any(chains):
                    for n in range(2):
                        if chains[n] is None:
                            continue
                        if last[n]:
                            wait(dve, own_rest, j, it, last[n])
                        last[n] = 0
                        try:
                            q = next(chains[n])
                        except StopIteration:
                            chains[n] = None
                            continue
                        if q is not None:
                            done[j][name] = done[j][name] % per_pass[name] + 1
                            last[n] = done[j][name]
                            q.then_inc(sems[j], 1)

            def silus(k):
                def visit(j, it):
                    wait(dve, tanh_done, j, it, 2 * k + 1)
                    V.scalar_tensor_tensor(zsT[j][:, k, :], zsT[j][:, k, :], 1.0, bank[4 * j + 2 + k][:, :],
                                           ALU.add, ALU.mult).then_inc(silu_done[1][j], 1)
                    wait(dve, tanh_done, j, it, 2 * k + 2)
                    V.scalar_tensor_tensor(xhT[j][:, k, :], xhT[j][:, k, :], 1.0, xcT[j][:, k, :],
                                           ALU.add, ALU.mult).then_inc(silu_done[1][j], 1)
                return visit

            def parts(j, it):
                wait(dve, cum_ps, j, it)
                cum = bank[4 * j + 2][:, 0:TP * H].rearrange("p (t h) -> p t h", h=H)
                r = dv[j][:, PP, :].rearrange("p (t h) -> p t h", h=H)

                def part(i):
                    return Q[j][:, :, PART_ROW + i * H:PART_ROW + (i + 1) * H]
                step(j, it, V.tensor_copy(part(0), cum))
                step(j, it, V.tensor_tensor(r, cum, part(0), ALU.subtract))
                step(j, it, V.tensor_copy(part(1), r))
                step(j, it, V.tensor_tensor(r, r, part(1), ALU.subtract))
                V.tensor_copy(part(2), r).then_inc(parts_done[1][j], 1)

            def dt_times_x(j, it):
                for bi in range(BP):
                    wait(dve, xht_ps, j, it, bi + 1)
                    V.tensor_tensor(
                        dtx[j][:, bi * NT:(bi + 1) * NT, :].rearrange("p t (h d) -> p (t h) d", h=H),
                        bank[4 * j + bi][:, :].rearrange("p (g d) -> p g d", d=HD),
                        dv[j][:, DTH, bi * NT * H:(bi + 1) * NT * H].unsqueeze(2).broadcast_to((P, NT * H, HD)),
                        ALU.mult).then_inc(dtx_done[1][j], 1)

            def weigh(f):
                def visit(j, it):
                    bi, g = divmod(f, 3)
                    wait(dve, seg_done, j, it, f + 1)
                    if f >= 3:
                        wait(dve, y_ps, j, it, 1)
                    if g < 2:
                        n, s = 2, gm[j][:, bi, 0:2, :].rearrange("p n t -> p (n t)")
                    else:
                        n, s = H, gm[j][:, bi, 2, :]
                    w = 512 // n
                    V.tensor_tensor(seg_m[j][:, g, :].rearrange("p (h t) -> p h t", h=n),
                                    seg_e[j][:, g, :].rearrange("p (h t) -> p h t", h=n),
                                    s.unsqueeze(1).broadcast_to((P, n, w)), ALU.mult).then_inc(m_done[1][j], 1)
                return visit

            def gate(bi):
                def visit(j, it):
                    wait(dve, y_ps, j, it, bi + 1)
                    v = (slice(None), slice(None), slice(bi * L, (bi + 1) * L))
                    V.tensor_tensor(xhT[j][v], bank[4 * j + bi][:, :].rearrange("p (k t) -> p k t", k=CT), zsT[j][v],
                                    ALU.mult).then_inc(yg_done[1][j], 1)
                return visit

            def x1(bi):
                def visit(j, it):
                    wait(dve, basis_done, j, it, 1)
                    hold(dve)
                    wait(dve, o_ps, j, it, bi + 1)
                    step(j, it, V.tensor_tensor(x1_tile(j, it, bi * NT, NT),
                                                bank[4 * j + bi][:, 0:L].rearrange("p (t d) -> p t d", t=NT),
                                                basis[j][:, of_batch(bi), :], ALU.add))
                return visit

            def token_max(bi):
                def visit(j, it):
                    wait(dve, lt_done, j, it, 2 * bi + 2)
                    step(j, it, V.reduce_max(rmax[j][:, :], lt_sb[j][:, :, :], AX.X))
                    V.tensor_tensor(diag_r[j][:, :, :], ident_shift[:, :].unsqueeze(1).broadcast_to((P, NT, P)),
                                    rmax[j][:, :].unsqueeze(2).broadcast_to((P, NT, P)), ALU.mult
                                    ).then_inc(diag_r_done[1][j], 1)
                return visit

            def slot_max(bi):
                def visit(j, it):
                    for m2 in range(2):
                        wait(dve, ls_ps, j, it, 2 * bi + m2 + 1)
                        q = V.reduce_max(cmax[j][:, 2 * m2:2 * m2 + 2],
                                         bank[4 * j + (0, 2)[bi] + m2][:, :].rearrange("p (m t) -> p m t", m=2), AX.X)
                    step(j, it, q)
                    V.tensor_tensor(diag_c[j][:, :, :], ident_shift[:, :].unsqueeze(1).broadcast_to((P, MT, P)),
                                    cmax[j][:, :].unsqueeze(2).broadcast_to((P, MT, P)), ALU.mult
                                    ).then_inc(diag_c_done[1][j], 1)
                return visit

            def norm_slots(bi):
                def visit(j, it):
                    ps = [bank[4 * j + (2, 0)[bi] + m2][:, 0:2 * (P + 1)].rearrange("p (m d) -> p m d", m=2) for m2 in range(2)]
                    for m2 in range(2):
                        wait(dve, slots_ps, j, it, 2 * bi + m2 + 1)
                        q = V.reciprocal(rcs[j][:, 2 * m2:2 * m2 + 2], ps[m2][:, :, P])
                    step(j, it, q)
                    for m2 in range(2):
                        q = V.tensor_tensor(slots[j][:, 2 * m2:2 * m2 + 2, :], ps[m2][:, :, 0:P],
                                            rcs[j][:, 2 * m2:2 * m2 + 2].unsqueeze(2).broadcast_to((P, 2, P)), ALU.mult)
                    q.then_inc(slots_done[1][j], 1)
                return visit

            visits = [(-37.62, statistics1), (-35.75, centre1), (-34.13, modulate1), (-6.46, unit1),
                      (-1.93, dt_in), (0.56, conv_and_softplus), (2.21, silus(0)), (21.7, parts),
                      (22.92, silus(1)), (29.03, dt_times_x), (29.94, weigh(0)), (30.3, weigh(1)),
                      (32.61, weigh(2)), (36.36, gate(0)), (36.65, weigh(3)), (38.62, weigh(4)),
                      (38.64, weigh(5)), (38.86, x1(0)), (38.94, statistics2(0)), (42.02, modulate2(0)),
                      (42.71, gate(1)), (43.77, x1(1)), (43.79, statistics2(1)), (47.33, modulate2(1)),
                      (47.35, unit2(0)), (49.67, unit2(1)), (52.11, token_max(0)), (52.13, slot_max(0)),
                      (60.62, norm_slots(0)), (76.21, token_max(1)), (76.23, slot_max(1)),
                      (86.44, norm_slots(1))]
            pipeline(dve, visits)

            with dve.Fori(0, E // 2) as it:
                for j in range(2):
                    wait(dve, eoT_ps, j, it)
                    dve.wait_ge(eo_ps, it * 2 + 1)
                    V.scalar_tensor_tensor(eoT[:, :, j, :], bank[4 + j][:, :].rearrange("p (b s) -> p b s", b=B),
                                           vecT[:, bass.ds(it * 2 + (RB2 + j), 1)],
                                           gbT[:, :].unsqueeze(2).broadcast_to((P, B, S)), ALU.add, ALU.mult
                                           ).then_inc(eoT_done[1][j], 1)
            with dve.Fori(0, B // 2) as it:
                for j in range(2):
                    wait_before(dve, y_sent, j, it)
                    for n in range(NT):
                        wait(dve, comb_out_ps, j, it, n + 1)
                        ps = bank[2 * j + n]
                        q = V.reciprocal(rden[j][:, n:n + 1], ps[:, P:P + 1])
                    q.then_inc(rden_done, 1)
                    dve.wait_ge(rden_done, it * 2 + (j + 1))
                    for n in range(NT):
                        q = V.scalar_tensor_tensor(yout[j][:, n, :], bank[2 * j + n][:, 0:P], rden[j][:, n:n + 1],
                                                   x1tok[:, bass.ds(it * 2 * NT + (j * NT + n), 1), :]
                                                   .rearrange("p t d -> p (t d)"), ALU.mult, ALU.add)
                    q.then_inc(y_out[1][j], 1)


_INS = ["L0_attn_x", "L0_attn_norm_w", "L0_attn_in_proj_w", "L0_attn_conv_w", "L0_attn_conv_b", "L0_attn_A_log",
        "L0_attn_D", "L0_attn_dt_bias", "L0_attn_out_proj_w", "L0_ffn_norm_gamma", "L0_ffn_slot_norm_gamma",
        "L0_ffn_slot_embeds", "L0_ffn_w1", "L0_ffn_b1", "L0_ffn_w2", "L0_ffn_b2", "L0_c", "L0_wmod"]


def kernel(**inputs):
    import numpy as _np
    import concourse.bacc as _bacc
    from concourse import mybir as _mybir
    from concourse.bass_utils import run_bass_kernel_spmd as _run

    nc = _bacc.Bacc("TRN2", target_bir_lowering=False, num_devices=1)
    arrays, args = {}, []
    for name in _INS:
        a = _np.ascontiguousarray(inputs[name])
        arrays[f"in_{name}_dram"] = a
        args.append(nc.dram_tensor(f"in_{name}_dram", a.shape, _mybir.dt.from_np(a.dtype), kind="ExternalInput").ap())
    shape = inputs["L0_attn_x"].shape
    args.append(nc.dram_tensor("out_0_dram", shape, _mybir.dt.float32, kind="ExternalOutput").ap())
    bass_adaln_mamba_softmoe_kernel(nc, *args)
    r = _run(nc, [arrays], core_ids=[0])
    return r.results[0]["out_0_dram"]
```
